# Optimizing a Trainium2 kernel written in Bass

```python
import numpy as np
import jax
import jax.numpy as jnp

def _softmax(x, axis=-1):
    return jax.nn.softmax(x, axis=axis)

def _gelu(x):
    return jax.nn.gelu(x, approximate=True)

def _silu(x):
    return jax.nn.silu(x)

def _sigmoid(x):
    return jax.nn.sigmoid(x)

def _layernorm(x, axis=-1, eps=1e-05):
    m = jnp.mean(x, axis=axis, keepdims=True)
    v = jnp.var(x, axis=axis, keepdims=True)
    return (x - m) / jnp.sqrt(v + eps)

def _scatter_add(tgt, idx, src, axis=0):
    return tgt.at[idx].add(src)

def _segment_sum(src, seg, n):
    return jax.ops.segment_sum(src, seg, n)
kernel_name = 'mk_xattn_ffn_d2_seqx_r4_f1dec4'

def setup_inputs(seed: int=0):
    np.random.seed(seed)
    _w = jnp.asarray

    def _rec_inputs():
        import jax
        import jax.numpy as jnp
        _rk = jax.random.key(seed)
        x = 7.22e-05 + 1 * jax.random.normal(jax.random.fold_in(_rk, 1), (4, 512, 512), jnp.float32)
        _lenS = 512 - jax.random.randint(jax.random.fold_in(_rk, 7), (4,), 0, max(1, 512 // 4) + 1, jnp.int32)
        _lenS2 = 512 - jax.random.randint(jax.random.fold_in(_rk, 8), (4,), 0, max(1, 512 // 4) + 1, jnp.int32)
        _ctx_1024P = jax.random.normal(jax.random.fold_in(_rk, 11), (4, 16, 256), jnp.float32)
        _ctx_1024c = jax.random.dirichlet(jax.random.fold_in(_rk, 511), 0.3 * jnp.ones((16,), jnp.float32), (4, 512))
        _ctx_1024t = jnp.einsum('bsk,bkd->bsd', _ctx_1024c, _ctx_1024P)
        _ctx_1024t = _ctx_1024t * jax.lax.rsqrt(jnp.mean(jnp.square(_ctx_1024t)) + 1e-12) * 0.953939
        ctx_1024 = 2.81802e-05 + 1.00001 * (_ctx_1024t + 0.3 * jax.random.normal(jax.random.fold_in(_rk, 611), (4, 512, 256), jnp.float32))
        return (x, ctx_1024)
    x, ctx_1024 = _rec_inputs()

    def _L0_xattn_setup():
        import jax, jax.numpy as jnp
        import numpy as np
        key = jax.random.key(seed)
        ks = jax.random.split(key, 6)
        B, L, N, C, D = (8, 128, 512, 256, 128)
        return {'teacher_logits': jax.random.normal(ks[0], (B, L, N), dtype=jnp.float32), 'teacher_features': jax.random.normal(ks[1], (B, N, C), dtype=jnp.float32), 'Wq': jax.random.normal(ks[2], (D, C), dtype=jnp.float32) * (1.0 / np.sqrt(C)), 'bq': jnp.zeros((D,), dtype=jnp.float32), 'Wk': jax.random.normal(ks[3], (D, C), dtype=jnp.float32) * (1.0 / np.sqrt(C)), 'bk': jnp.zeros((D,), dtype=jnp.float32)}
    _L0_xattn_all = _L0_xattn_setup()
    _L0_xattn_in = {k: v for k, v in _L0_xattn_all.items() if k in ('Wq', 'bq', 'Wk', 'bk')}
    del _L0_xattn_all

    def _L0_ffn_setup():
        import jax, jax.numpy as jnp
        import numpy as np
        HIDDEN = 512
        INTER = 2048
        COMPRESSION = 128.9

        def _n_ctrl(out_size, in_size):
            return max(16, int(out_size * in_size / COMPRESSION))

        def _catmull_rom_grid(n_ctrl, n_samples):
            t = np.linspace(0.0, n_ctrl - 1.0, n_samples, dtype=np.float64)
            i = np.clip(np.floor(t).astype(np.int64), 0, n_ctrl - 2)
            f = (t - i).astype(np.float32)
            idx = np.stack([np.clip(i + k, 0, n_ctrl - 1) for k in (-1, 0, 1, 2)], axis=0)
            return (jnp.asarray(idx.astype(np.int32)), jnp.asarray(f))

        def spline_reconstruct(control_points, out_size, in_size):
            n = out_size * in_size
            idx, f = _catmull_rom_grid(control_points.shape[0], n)
            p0, p1, p2, p3 = (control_points[idx[0]], control_points[idx[1]], control_points[idx[2]], control_points[idx[3]])
            f2 = f * f
            f3 = f2 * f
            w = 0.5 * (2.0 * p1 + (p2 - p0) * f + (2.0 * p0 - 5.0 * p1 + 4.0 * p2 - p3) * f2 + (3.0 * p1 - p0 - 3.0 * p2 + p3) * f3)
            return w.reshape(out_size, in_size)
        key = jax.random.key(seed)
        k0, k1, k2, k3 = jax.random.split(key, 4)
        hidden_states = jax.random.normal(k0, (4, 512, HIDDEN), dtype=jnp.float32)
        gate_cp = jax.random.normal(k1, (_n_ctrl(INTER, HIDDEN),), dtype=jnp.float32) * 0.02
        up_cp = jax.random.normal(k2, (_n_ctrl(INTER, HIDDEN),), dtype=jnp.float32) * 0.02
        down_cp = jax.random.normal(k3, (_n_ctrl(HIDDEN, INTER),), dtype=jnp.float32) * 0.02
        return {'hidden_states': hidden_states, 'gate_cp': gate_cp, 'up_cp': up_cp, 'down_cp': down_cp}
    _L0_ffn_all = _L0_ffn_setup()
    _L0_ffn_in = {k: v for k, v in _L0_ffn_all.items() if k in ('gate_cp', 'up_cp', 'down_cp')}
    del _L0_ffn_all

    def _L1_xattn_setup():
        import jax, jax.numpy as jnp
        import numpy as np
        B_, L_, D_MODEL = (4, 512, 256)
        D_STATE, D_CONV, EXPAND = (16, 4, 2)
        D_INNER = EXPAND * D_MODEL
        DT_RANK = (D_MODEL + 15) // 16

        def silu(x):
            return x * jax.nn.sigmoid(x)
        key = jax.random.key(seed)
        ks = jax.random.split(key, 10)
        f32 = jnp.float32
        hidden_states = jax.random.normal(ks[0], (B_, L_, D_MODEL), dtype=f32)
        z = jax.random.normal(ks[1], (B_, D_INNER, L_), dtype=f32)
        in_proj_w = jax.random.normal(ks[2], (D_INNER, D_MODEL), dtype=f32) * 0.02
        conv_w = jax.random.normal(ks[3], (D_INNER, 1, D_CONV), dtype=f32) * 0.1
        conv_b = jax.random.normal(ks[4], (D_INNER,), dtype=f32) * 0.02
        x_proj_w = jax.random.normal(ks[5], (DT_RANK + 2 * D_STATE, D_INNER), dtype=f32) * 0.02
        dt_proj_w = jax.random.uniform(ks[6], (D_INNER, DT_RANK), dtype=f32, minval=-DT_RANK ** (-0.5), maxval=DT_RANK ** (-0.5))
        dt = jnp.exp(jax.random.uniform(ks[7], (D_INNER,), dtype=f32, minval=np.log(0.001), maxval=np.log(0.1)))
        dt_proj_b = jnp.log(jnp.expm1(dt))
        A_log = jnp.log(jnp.broadcast_to(jnp.arange(1, D_STATE + 1, dtype=f32), (D_INNER, D_STATE)))
        D = jnp.ones((D_INNER,), f32)
        return {'hidden_states': hidden_states, 'z': z, 'in_proj_w': in_proj_w, 'conv_w': conv_w, 'conv_b': conv_b, 'x_proj_w': x_proj_w, 'dt_proj_w': dt_proj_w, 'dt_proj_b': dt_proj_b, 'A_log': A_log, 'D': D}
    _L1_xattn_all = _L1_xattn_setup()
    _L1_xattn_in = {k: v for k, v in _L1_xattn_all.items() if k in ('in_proj_w', 'conv_w', 'conv_b', 'x_proj_w', 'dt_proj_w', 'dt_proj_b', 'A_log', 'D')}
    del _L1_xattn_all

    def _L1_ffn_setup():
        import jax, jax.numpy as jnp
        import numpy as np
        TOP_K = 8
        NUM_EXPERTS = 32
        key = jax.random.key(seed)
        k1, k2, k3, k4, k5 = jax.random.split(key, 5)
        B, S, D, M, E = (4, 256, 512, 192, NUM_EXPERTS)
        return {'hidden_states': jax.random.normal(k1, (B, S, D), dtype=jnp.float32), 'gate_kernel': jax.random.normal(k2, (D, E), dtype=jnp.float32) * 0.02, 'gate_proj': jax.random.normal(k3, (E, D, M), dtype=jnp.float32) * 0.02, 'up_proj': jax.random.normal(k4, (E, D, M), dtype=jnp.float32) * 0.02, 'down_proj': jax.random.normal(k5, (E, M, D), dtype=jnp.float32) * 0.02}
    _L1_ffn_all = _L1_ffn_setup()
    _L1_ffn_in = {k: v for k, v in _L1_ffn_all.items() if k in ('gate_kernel', 'gate_proj', 'up_proj', 'down_proj')}
    del _L1_ffn_all
    return {'x': x, 'ctx_1024': ctx_1024, 'L0_xattn_Wq': _L0_xattn_in['Wq'], 'L0_xattn_bq': _L0_xattn_in['bq'], 'L0_xattn_Wk': _L0_xattn_in['Wk'], 'L0_xattn_bk': _L0_xattn_in['bk'], 'L0_ffn_gate_cp': _L0_ffn_in['gate_cp'], 'L0_ffn_up_cp': _L0_ffn_in['up_cp'], 'L0_ffn_down_cp': _L0_ffn_in['down_cp'], 'L1_xattn_in_proj_w': _L1_xattn_in['in_proj_w'], 'L1_xattn_conv_w': _L1_xattn_in['conv_w'], 'L1_xattn_conv_b': _L1_xattn_in['conv_b'], 'L1_xattn_x_proj_w': _L1_xattn_in['x_proj_w'], 'L1_xattn_dt_proj_w': _L1_xattn_in['dt_proj_w'], 'L1_xattn_dt_proj_b': _L1_xattn_in['dt_proj_b'], 'L1_xattn_A_log': _L1_xattn_in['A_log'], 'L1_xattn_D': _L1_xattn_in['D'], 'L1_ffn_gate_kernel': _L1_ffn_in['gate_kernel'], 'L1_ffn_gate_proj': _L1_ffn_in['gate_proj'], 'L1_ffn_up_proj': _L1_ffn_in['up_proj'], 'L1_ffn_down_proj': _L1_ffn_in['down_proj']}

def reference(x, ctx_1024, L0_xattn_Wq, L0_xattn_bq, L0_xattn_Wk, L0_xattn_bk, L0_ffn_gate_cp, L0_ffn_up_cp, L0_ffn_down_cp, L1_xattn_in_proj_w, L1_xattn_conv_w, L1_xattn_conv_b, L1_xattn_x_proj_w, L1_xattn_dt_proj_w, L1_xattn_dt_proj_b, L1_xattn_A_log, L1_xattn_D, L1_ffn_gate_kernel, L1_ffn_gate_proj, L1_ffn_up_proj, L1_ffn_down_proj):
    import jax
    import jax.numpy as jnp

    def _L0_xattn_ref(teacher_logits, teacher_features, Wq, bq, Wk, bk):
        import jax, jax.numpy as jnp
        import numpy as np
        query = jnp.einsum('bnc,dc->bnd', teacher_features, Wq) + bq
        key = jnp.einsum('bnc,dc->bnd', teacher_features, Wk) + bk
        energy = jnp.einsum('bnd,bmd->bnm', query, key)
        attention = jax.nn.softmax(energy, axis=-1)
        x_m = jnp.einsum('bln,bmn->blm', teacher_logits, attention)
        return x_m

    def _L0_ffn_ref(hidden_states, gate_cp, up_cp, down_cp):
        import jax, jax.numpy as jnp
        import numpy as np
        HIDDEN = 512
        INTER = 2048
        COMPRESSION = 128.9

        def _n_ctrl(out_size, in_size):
            return max(16, int(out_size * in_size / COMPRESSION))

        def _catmull_rom_grid(n_ctrl, n_samples):
            t = np.linspace(0.0, n_ctrl - 1.0, n_samples, dtype=np.float64)
            i = np.clip(np.floor(t).astype(np.int64), 0, n_ctrl - 2)
            f = (t - i).astype(np.float32)
            idx = np.stack([np.clip(i + k, 0, n_ctrl - 1) for k in (-1, 0, 1, 2)], axis=0)
            return (jnp.asarray(idx.astype(np.int32)), jnp.asarray(f))

        def spline_reconstruct(control_points, out_size, in_size):
            n = out_size * in_size
            idx, f = _catmull_rom_grid(control_points.shape[0], n)
            p0, p1, p2, p3 = (control_points[idx[0]], control_points[idx[1]], control_points[idx[2]], control_points[idx[3]])
            f2 = f * f
            f3 = f2 * f
            w = 0.5 * (2.0 * p1 + (p2 - p0) * f + (2.0 * p0 - 5.0 * p1 + 4.0 * p2 - p3) * f2 + (3.0 * p1 - p0 - 3.0 * p2 + p3) * f3)
            return w.reshape(out_size, in_size)
        gate_w = spline_reconstruct(gate_cp, INTER, HIDDEN)
        up_w = spline_reconstruct(up_cp, INTER, HIDDEN)
        down_w = spline_reconstruct(down_cp, HIDDEN, INTER)
        gate = jnp.einsum('bsh,ih->bsi', hidden_states, gate_w)
        up = jnp.einsum('bsh,ih->bsi', hidden_states, up_w)
        inter = jax.nn.silu(gate) * up
        return jnp.einsum('bsi,hi->bsh', inter, down_w)

    def _L1_xattn_ref(hidden_states, z, in_proj_w, conv_w, conv_b, x_proj_w, dt_proj_w, dt_proj_b, A_log, D):
        import jax, jax.numpy as jnp
        import numpy as np
        B_, L_, D_MODEL = (4, 512, 256)
        D_STATE, D_CONV, EXPAND = (16, 4, 2)
        D_INNER = EXPAND * D_MODEL
        DT_RANK = (D_MODEL + 15) // 16

        def silu(x):
            return x * jax.nn.sigmoid(x)
        Bsz, L, _ = hidden_states.shape
        d_inner, _, d_conv = conv_w.shape
        dt_rank = dt_proj_w.shape[1]
        d_state = A_log.shape[1]
        x = jnp.einsum('bld,ed->bel', hidden_states, in_proj_w)
        xc = jax.lax.conv_general_dilated(x, conv_w, window_strides=(1,), padding=[(d_conv - 1, 0)], feature_group_count=d_inner, dimension_numbers=('NCH', 'OIH', 'NCH'))
        x = silu(xc + conv_b[None, :, None])
        x_dbl = jnp.einsum('bdl,ed->bel', x, x_proj_w)
        dt_low, Bm, Cm = jnp.split(x_dbl, [dt_rank, dt_rank + d_state], axis=1)
        dt = jnp.einsum('brl,dr->bdl', dt_low, dt_proj_w)
        dt = jax.nn.softplus(dt + dt_proj_b[None, :, None])
        A = -jnp.exp(A_log)
        dt_t = jnp.moveaxis(dt, -1, 0)
        B_t = jnp.moveaxis(Bm, -1, 0)
        C_t = jnp.moveaxis(Cm, -1, 0)
        u_t = jnp.moveaxis(x, -1, 0)

        def step(state, inp):
            d, b, c, u = inp
            dA = jnp.exp(d[..., None] * A)
            state = state * dA + (d * u)[..., None] * b[:, None, :]
            y = jnp.einsum('bdn,bn->bd', state, c)
            return (state, y)
        state0 = jnp.zeros((Bsz, d_inner, d_state), x.dtype)
        _, ys = jax.lax.scan(step, state0, (dt_t, B_t, C_t, u_t))
        y = jnp.moveaxis(ys, 0, 2)
        y = y + D[None, :, None] * x
        y = y * silu(z)
        return jnp.swapaxes(y, 1, 2)

    def _L1_ffn_ref(hidden_states, gate_kernel, gate_proj, up_proj, down_proj):
        import jax, jax.numpy as jnp
        import numpy as np
        TOP_K = 8
        NUM_EXPERTS = 32
        B, S, D = hidden_states.shape
        T = B * S
        x2d = hidden_states.reshape(T, D)
        router_logits = x2d @ gate_kernel
        routing_weights = jax.nn.softmax(router_logits, axis=-1)
        routing_weights, selected_experts = jax.lax.top_k(routing_weights, TOP_K)
        routing_weights = routing_weights / jnp.sum(routing_weights, axis=-1, keepdims=True)
        flat_experts = selected_experts.reshape(-1)
        sort_idx = jnp.argsort(flat_experts)
        token_rows = sort_idx // TOP_K
        sorted_inputs = jnp.take(x2d, token_rows, axis=0)
        group_sizes = jnp.bincount(flat_experts, length=NUM_EXPERTS).astype(jnp.int32)
        w0 = jax.lax.ragged_dot(sorted_inputs, gate_proj, group_sizes, preferred_element_type=jnp.float32)
        w1 = jax.lax.ragged_dot(sorted_inputs, up_proj, group_sizes, preferred_element_type=jnp.float32)
        inter = jax.nn.silu(w0) * w1
        expert_out = jax.lax.ragged_dot(inter, down_proj, group_sizes, preferred_element_type=jnp.float32)
        unsorted = jnp.take(expert_out, jnp.argsort(sort_idx), axis=0)
        per_token = unsorted.reshape(T, TOP_K, D)
        output = jnp.einsum('BKE,BK->BE', per_token.astype(jnp.float32), routing_weights.astype(jnp.float32))
        return output.reshape(B, S, D)
    x = x + _L0_xattn_ref(_layernorm(x, axis=-1), ctx_1024, L0_xattn_Wq, L0_xattn_bq, L0_xattn_Wk, L0_xattn_bk)
    x = x + _L0_ffn_ref(_layernorm(x, axis=-1), L0_ffn_gate_cp, L0_ffn_up_cp, L0_ffn_down_cp)
    x = x + _L1_xattn_ref(ctx_1024, _layernorm(x, axis=-1), L1_xattn_in_proj_w, L1_xattn_conv_w, L1_xattn_conv_b, L1_xattn_x_proj_w, L1_xattn_dt_proj_w, L1_xattn_dt_proj_b, L1_xattn_A_log, L1_xattn_D)
    x = x + _L1_ffn_ref(_layernorm(x, axis=-1), L1_ffn_gate_kernel, L1_ffn_gate_proj, L1_ffn_up_proj, L1_ffn_down_proj)
    return x

_drawn_inputs = setup_inputs


def setup_inputs(seed=0):
    import zlib

    import numpy as np

    out = dict(_drawn_inputs(seed))
    spreads = {'L0_xattn_bq': (0.0, 0.1), 'L0_xattn_bk': (0.0, 0.8), 'L1_xattn_D': (1.0, 0.6)}
    factors = {'L1_xattn_in_proj_w': 3.755,
     'L1_xattn_conv_w': 3.836,
     'L1_xattn_conv_b': 8.0,
     'L1_xattn_x_proj_w': 8.0,
     'L1_xattn_dt_proj_w': 8.0,
     'L1_xattn_dt_proj_b': 8.0,
     'L1_xattn_A_log': 8.0,
     'L1_ffn_gate_kernel': 7.528,
     'L1_ffn_gate_proj': 6.738,
     'L1_ffn_up_proj': 6.586,
     'L1_ffn_down_proj': 6.587}
    for name, (base, spread) in spreads.items():
        noise = np.random.default_rng([zlib.crc32(name.encode()), seed]).standard_normal(out[name].shape)
        drawn = base * np.exp(spread * noise) if base else spread * noise
        out[name] = jnp.asarray(drawn.astype(out[name].dtype))
    for name, factor in factors.items():
        out[name] = (out[name] * factor).astype(out[name].dtype)
    return out
```

```python
from contextlib import ExitStack

import numpy as np

import concourse.bass as bass
from concourse import mybir

ds = bass.ds
F32 = mybir.dt.float32
F32R = mybir.dt.float32r
U8, I32 = mybir.dt.uint8, mybir.dt.int32
ALU = mybir.AluOpType
ACT = mybir.ActivationFunctionType
AX = mybir.AxisListType.X

P = 128
NB, L, D = 4, 512, 512
DC = 256
KC = D // P
LT = L // P
NT = NB * LT
DK = 128
DI, NS, R, TAPS = 512, 16, 16, 4
INTER = 2048
NE, M, TOPK = 32, 192, 8
EPS = 1e-5
NCTRL = max(16, int(INTER * D / 128.9))
GW = 2 * P
NG = INTER // GW
IPAD = INTER + L
PC = 3


def spline_constants():
    n = INTER * D
    t = np.linspace(0.0, NCTRL - 1.0, n, dtype=np.float64)
    i = np.clip(np.floor(t).astype(np.int64), 0, NCTRL - 2)
    t0, ia = t[::P], i[::P]
    ib = np.minimum(ia + 1, NCTRL - 2)
    r = (NCTRL - 1.0) / (n - 1)
    cubic = 0.5 * np.array([[0, -1, 2, -1], [2, 0, -5, 3], [0, 1, 4, -3], [0, 0, -1, 1]], np.float64)
    table = np.zeros((KC, 2, 4, 4, IPAD))
    taps = np.full((KC, 2, 4, IPAD), -1, np.int64)
    for ab, ix in enumerate((ia, ib)):
        f = (t0 - ix).reshape(INTER, KC).T
        for j in range(4):
            c0, c1, c2, c3 = cubic[j]
            shifted = [c0 + c1 * f + c2 * f**2 + c3 * f**3, c1 + 2 * c2 * f + 3 * c3 * f**2, c2 + 3 * c3 * f,
                       c3 + 0 * f]
            for p in range(4):
                table[:, ab, j, p, :INTER] = shifted[p]
            taps[:, ab, j, :INTER] = np.clip(ix + j - 1, 0, NCTRL - 1).reshape(INTER, KC).T
    powers = np.zeros((KC, 2, 4, 4, KC, 2, P))
    y = np.arange(P) * r
    for c in range(KC):
        for ab in range(2):
            for p in range(4):
                powers[c, ab, :, p, c, ab, :] = y**p
    second = (i.reshape(-1, P) != ia[:, None]).T.astype(np.uint8)
    by_gate = second.reshape(P, NG, GW, KC).transpose(1, 0, 3, 2).reshape(NG, P, KC * GW)
    by_down = second.reshape(P, D, NG, 2).transpose(2, 0, 3, 1).reshape(NG, P, 2 * D)
    masks = np.zeros((NG + 2, P, KC * GW + 2 * D), np.uint8)
    masks[:NG] = np.concatenate([by_gate, by_down], 2)
    return (table.reshape(P, IPAD).astype(np.float32), taps, powers.reshape(P, KC * 2 * P).astype(np.float32), masks)


def build(nc, a):
    ctx = ExitStack()

    def dram(name, shape):
        return nc.dram_tensor(name, shape, F32).ap()

    dt_d, dtu_d, du_d, y_d = (dram(n, (NB, KC, P, L)) for n in ("dt_d", "dtu_d", "du_d", "y_d"))
    bc_d = dram("bc_d", (NB, 2 * NS, L))
    rw_d = dram("rw_d", (NE, NB * L))

    with ctx:
        X = ctx.enter_context(nc.sbuf_tensor("X", [P, NT, D], F32))
        ident = ctx.enter_context(nc.sbuf_tensor("ident", [P, P], F32))
        negA = ctx.enter_context(nc.sbuf_tensor("negA", [P, KC, NS], F32))
        bank = [ctx.enter_context(nc.psum_tensor(f"bank{i}", [P, 512], F32)) for i in range(8)]
        block_a(nc, a, X, ident, negA, bank, dt_d, dtu_d, du_d, bc_d)
        with ExitStack() as s:
            hT = s.enter_context(nc.sbuf_tensor("hT", [P, KC, NB * L], F32))
            Rt = [s.enter_context(nc.sbuf_tensor(f"R{n}", [P, IPAD], F32)) for n in ("gate", "up", "down")]
            powers = s.enter_context(nc.sbuf_tensor("powers", [P, KC, 2, P], F32))
            block_b0(nc, a, X, ident, bank, hT, Rt, powers)
            block_b(nc, a, X, negA, bank, hT, Rt, powers, dt_d, dtu_d, du_d, bc_d, y_d)
        with ExitStack() as s:
            hhi = s.enter_context(nc.sbuf_tensor("hhi", [P, KC, NB * L], F32R))
            hlo = s.enter_context(nc.sbuf_tensor("hlo", [P, KC, NB * L], F32R))
            block_c(nc, a, X, ident, bank, hhi, hlo, y_d, rw_d)
            block_d(nc, a, X, bank, hhi, hlo, rw_d)


def mem(nc, s, block_name):
    def sb(name, shape, dt=F32):
        return s.enter_context(nc.sbuf_tensor(f"{block_name}_{name}", shape, dt))

    def sem(name):
        return s.enter_context(nc.semaphore(f"{block_name}_{name}"))
    return sb, sem


def block_a(nc, a, X, ident, negA, bank, dt_d, dtu_d, du_d, bc_d):
    with ExitStack() as s:
        sb, sem = mem(nc, s, "A")
        ctxT = sb("ctxT", [P, 2, L])
        wqT, wkT = sb("wqT", [P, 2, DK]), sb("wkT", [P, 2, DK])
        bq, bk = sb("bq", [P, 1]), sb("bk", [P, 1])
        inwT = sb("inwT", [P, 2, DI])
        convw, convb = sb("convw", [P, KC, TAPS]), sb("convb", [P, KC])
        xpT = sb("xpT", [P, KC, R + 2 * NS])
        dpT, dpb, Dp = sb("dpT", [R, DI]), sb("dpb", [P, KC]), sb("Dp", [P, KC])
        alog = sb("alog", [P, KC, NS])
        st, mv, rstd = sb("st", [P, 4, 6]), sb("mv", [P, 4, 2]), sb("rstd", [P, 4])
        xn, XT = sb("xn", [P, LT, D]), sb("XT", [P, KC, L])
        att, attT = sb("att", [P, LT, L]), sb("attT", [P, KC, L])
        nmax, rsum, rinv = sb("nmax", [P, 4]), sb("rsum", [P, 4]), sb("rinv", [P, 4])
        qT, kT = sb("qT", [P, L]), sb("kT", [P, L])
        conv, u = sb("conv", [P, KC, L]), sb("u", [P, KC, L])
        xdbl = sb("xdbl", [R + 2 * NS, L])
        pos, ex, one, ln = (sb(n, [P, KC, L]) for n in ("pos", "ex", "one", "ln"))
        dtv, dtu, du = (sb(n, [P, KC, L]) for n in ("dtv", "dtu", "du"))

        ld_x, ld_w, ld_ctx = sem("ld_x"), sem("ld_w"), sem("ld_ctx")
        qk_ps, qk_sb = sem("qk_ps"), sem("qk_sb")
        in_ps, conv_seed, conv_step, conv_done, u_done = (sem(n) for n in ("in_ps", "conv_seed", "conv_step", "conv_done", "u_done"))
        passed = sem("passed")
        ln_var, ln_root = sem("ln_var"), sem("ln_root")
        ln_step, xn_done, xT_ps, xT_sb = sem("ln_step"), sem("xn_done"), sem("xT_ps"), sem("xT_sb")
        e_ps, row_max, att_exp, att_inv, att_done = (sem(n) for n in ("e_ps", "row_max", "att_exp", "att_inv", "att_done"))
        aT_ps, aT_sb, o_ps, x1_done = sem("aT_ps"), sem("aT_sb"), sem("o_ps"), sem("x1_done")
        xd_ps, xd_sb, dt_ps, dt_abs, dt_pos = (sem(n) for n in ("xd_ps", "xd_sb", "dt_ps", "dt_abs", "dt_pos"))
        sp_exp, sp_one, sp_ln, sp_fix, sp_sum, dt_done = (sem(n) for n in ("sp_exp", "sp_one", "sp_ln", "sp_fix", "sp_sum", "dt_done"))
        dtu_done, du_done, stored, negA_exp, negA_done = (sem(n) for n in ("dtu_done", "du_done", "stored", "negA_exp", "negA_done"))
        block = s.enter_context(nc.Block())
        NW = 13

        @block.sync
        def _(sp):
            for dst, name in ((ident[:, :], "ident"), (wqT[:, :, :], "wqT"), (wkT[:, :, :], "wkT"), (bq[:, :], "bq"),
                              (bk[:, :], "bk"), (inwT[:, :, :], "inwT"), (convw[:, :, :], "convw"),
                              (convb[:, :], "convb"), (xpT[:, :, :], "xpT"), (dpT[:, :], "dpT"), (dpb[:, :], "dpb"),
                              (Dp[:, :], "Dp"), (alog[:, :, :], "alog")):
                sp.dma_start(dst, a[name]).then_inc(ld_w, 16)
            for b in range(NB):
                sp.dma_start(X[:, b * LT:(b + 1) * LT, :], a["x"][b].rearrange("(t p) n -> p t n", p=P)).then_inc(ld_x, 16)
            with sp.Fori(0, NB) as b:
                sp.wait_ge(in_ps, b * 4)
                sp.dma_start(ctxT[:, :, :], a["ctxT"][ds(b, 1)].rearrange("o p c l -> p (o c) l")).then_inc(ld_ctx, 16)
                for wait, dst, src in ((xd_sb, bc_d[ds(b, 1)].rearrange("o n l -> (o n) l"), xdbl[R:R + 2 * NS, :]),
                                       (dt_done, dt_d[ds(b, 1)].rearrange("o k p l -> p (o k) l"), dtv[:, :, :]),
                                       (du_done, du_d[ds(b, 1)].rearrange("o k p l -> p (o k) l"), du[:, :, :]),
                                       (dtu_done, dtu_d[ds(b, 1)].rearrange("o k p l -> p (o k) l"), dtu[:, :, :])):
                    sp.wait_ge(wait, b + 1)
                    sp.dma_start(dst, src).then_inc(stored, 16)
            sp.wait_ge(stored, NB * 64)

        @block.tensor
        def _(pe):
            pe.wait_ge(ld_w, 16 * NW)
            with pe.Fori(0, NB) as b:
                pe.wait_ge(ld_ctx, b * 16 + 16)
                for n, w in enumerate((wqT, wkT)):
                    for c in range(2):
                        mm = pe.matmul(bank[n][:, :], w[:, c, :], ctxT[:, c, :], start=c == 0, stop=c == 1)
                    mm.then_inc(qk_ps, 1)
                for e in range(KC):
                    for c in range(2):
                        mm = pe.matmul(bank[2 + e][:, :], inwT[:, c, e * P:(e + 1) * P], ctxT[:, c, :], start=c == 0, stop=c == 1)
                    mm.then_inc(in_ps, 1)
                pe.wait_ge(xn_done, b * 4 + 4)
                for k in range(KC):
                    if k == 2:
                        pe.wait_ge(qk_sb, b * 2 + 2)
                    for t in range(LT):
                        mm = pe.transpose(bank[(6 + k) % 8][:, t * P:(t + 1) * P], xn[:, t, k * P:(k + 1) * P], ident[:, :])
                    mm.then_inc(xT_ps, 1)
                for m in range(4):
                    pe.wait_ge(conv_done, b * 4 + m + 1)
                    pe.matmul(bank[2 + m][:, :], qT[:, m * P:(m + 1) * P], kT[:, :], start=True, stop=True).then_inc(e_ps, 1)
                pe.wait_ge(u_done, b * 4 + 4)
                pe.wait_ge(xT_sb, b * 4 + 4)
                for k in range(KC):
                    mm = pe.matmul(bank[6][0:R + 2 * NS, :], xpT[:, k, :], u[:, k, :], start=k == 0, stop=k == KC - 1)
                mm.then_inc(xd_ps, 1)
                pe.wait_ge(xd_sb, b + 1)
                for k in range(KC):
                    pe.matmul(bank[(7, 0, 1, 6)[k]][:, :], dpT[:, k * P:(k + 1) * P], xdbl[0:R, :], start=True, stop=True).then_inc(dt_ps, 1)
                pe.wait_ge(att_done, b * 4 + 4)
                for k in range(KC):
                    for m in range(4):
                        mm = pe.transpose(bank[2 + k][:, m * P:(m + 1) * P], att[:, m, k * P:(k + 1) * P], ident[:, :])
                    mm.then_inc(aT_ps, 1)
                pe.wait_ge(dt_abs, b * 4 + 4)
                pe.wait_ge(dt_pos, b * 4 + 4)
                pe.wait_ge(aT_sb, b * 4 + 4)
                for t in range(LT):
                    for k in range(KC):
                        mm = pe.matmul(bank[(7, 0, 1, 6)[t]][:, :], XT[:, k, t * P:(t + 1) * P], attT[:, k, :], start=k == 0, stop=k == KC - 1)
                    mm.then_inc(o_ps, 1)
                pe.wait_ge(x1_done, b * 4 + 4)

        @block.scalar
        def _(act):
            act.wait_ge(ld_w, 16 * NW)
            act.activation(alog[:, :, :], alog[:, :, :], ACT.Exp).then_inc(negA_exp, 1)
            with act.Fori(0, NB) as b:
                act.wait_ge(ln_var, b + 1)
                act.activation(rstd[:, :], rstd[:, :], ACT.Sqrt).then_inc(ln_root, 1)
                act.wait_ge(qk_ps, b * 2 + 1)
                act.activation(qT[:, :], bank[0][:, :], ACT.Identity, bias=bq[:, 0:1]).then_inc(qk_sb, 1)
                act.wait_ge(qk_ps, b * 2 + 2)
                act.activation(kT[:, :], bank[1][:, :], ACT.Identity, bias=bk[:, 0:1]).then_inc(qk_sb, 1)
                for e in range(KC):
                    act.wait_ge(in_ps, b * 4 + e + 1)
                    act.activation(conv[:, e, :], bank[2 + e][:, :], ACT.Copy, scale=convw[:, e, TAPS - 1:TAPS]).then_inc(conv_seed, 1)
                for k in range(2):
                    act.wait_ge(xT_ps, b * 4 + k + 1)
                    act.activation(XT[:, k, :], bank[6 + k][:, :], ACT.Copy).then_inc(xT_sb, 1)
                act.wait_ge(dtu_done, b)
                act.wait_ge(du_done, b)
                for e in range(KC):
                    act.wait_ge(conv_done, b * 4 + e + 1)
                    act.activation(u[:, e, :], conv[:, e, :], ACT.Silu, bias=convb[:, e:e + 1]).then_inc(u_done, 1)
                for k in range(2, 4):
                    act.wait_ge(xT_ps, b * 4 + k + 1)
                    act.activation(XT[:, k, :], bank[k - 2][:, :], ACT.Copy).then_inc(xT_sb, 1)
                act.wait_ge(xd_ps, b + 1)
                act.wait_ge(stored, b * 64)
                act.activation(xdbl[:, :], bank[6][0:R + 2 * NS, :], ACT.Copy).then_inc(xd_sb, 1)
                for m in range(4):
                    act.wait_ge(row_max, b * 4 + m + 1)
                    act.activation(att[:, m, :], bank[2 + m][:, :], ACT.Exp, bias=nmax[:, m:m + 1], accum_out=rsum[:, m:m + 1]).then_inc(att_exp, 1)
                for k in range(KC):
                    act.wait_ge(dt_ps, b * 4 + k + 1)
                    act.activation(ex[:, k, :], bank[(7, 0, 1, 6)[k]][:, :], ACT.Abs, bias=dpb[:, k:k + 1]).then_inc(dt_abs, 1)
                act.wait_ge(dt_abs, b * 4 + 4)
                act.activation(ex[:, :, :], ex[:, :, :], ACT.Exp, scale=-1.0).then_inc(sp_exp, 1)
                for k in range(2):
                    act.wait_ge(aT_ps, b * 4 + k + 1)
                    act.activation(attT[:, k, :], bank[2 + k][:, :], ACT.Copy).then_inc(aT_sb, 1)
                act.wait_ge(sp_one, b + 1)
                act.activation(ln[:, :, :], one[:, :, :], ACT.Ln).then_inc(sp_ln, 1)

        @block.vector
        def _(v):
            v.wait_ge(negA_exp, 1)
            v.tensor_scalar(negA[:, :, :], alog[:, :, :], -1.0, None, ALU.mult).then_inc(negA_done, 1)
            v.wait_ge(ld_x, 16 * NB)
            with v.Fori(0, NB) as b:
                for t in range(LT):
                    i = v.bn_stats(st[:, t, :], X[:, ds(b * LT + t, 1), :])
                i.then_inc(ln_step, 1)
                v.wait_ge(ln_step, b * 3 + 1)
                v.sem_inc(passed)
                for t in range(LT):
                    i = v.bn_aggr(mv[:, t, :], st[:, t, :])
                i.then_inc(ln_step, 1)
                v.wait_ge(ln_step, b * 3 + 2)
                v.tensor_scalar(rstd[:, :], mv[:, :, 1], EPS, None, ALU.add).then_inc(ln_var, 1)
                v.wait_ge(ln_root, b + 1)
                v.reciprocal(rstd[:, :], rstd[:, :]).then_inc(ln_step, 1)
                v.wait_ge(ln_step, b * 3 + 3)
                for t in range(LT):
                    v.tensor_scalar(xn[:, t, :], X[:, ds(b * LT + t, 1), :].rearrange("p o n -> p (o n)"), mv[:, t, 0:1], rstd[:, t:t + 1],
                                    ALU.subtract, ALU.mult).then_inc(xn_done, 1)
                for e in range(KC):
                    v.wait_ge(conv_seed, b * 4 + e + 1)
                    for j in range(1, TAPS):
                        i = v.scalar_tensor_tensor(out=conv[:, e, j:], in0=bank[2 + e][:, 0:L - j],
                                                   scalar=convw[:, e, TAPS - 1 - j:TAPS - j], in1=conv[:, e, j:],
                                                   op0=ALU.mult, op1=ALU.add)
                        if j < TAPS - 1:
                            i.then_inc(conv_step, 1)
                            v.wait_ge(conv_step, b * 8 + e * 2 + j)
                        else:
                            i.then_inc(conv_done, 1)
                for m in range(4):
                    v.wait_ge(e_ps, b * 4 + m + 1)
                    v.tensor_reduce(nmax[:, m:m + 1], bank[2 + m][:, :], AX, ALU.max, negate=True).then_inc(row_max, 1)
                v.wait_ge(stored, b * 64)
                v.wait_ge(u_done, b * 4 + 4)
                for k in range(KC):
                    i = v.tensor_scalar(du[:, k, :], u[:, k, :], Dp[:, k:k + 1], None, ALU.mult)
                i.then_inc(du_done, 1)
                v.wait_ge(att_exp, b * 4 + 4)
                v.reciprocal(rinv[:, :], rsum[:, :]).then_inc(att_inv, 1)
                v.wait_ge(att_inv, b + 1)
                for m in range(4):
                    v.tensor_scalar(att[:, m, :], att[:, m, :], rinv[:, m:m + 1], None, ALU.mult).then_inc(att_done, 1)
                for k in range(KC):
                    v.wait_ge(dt_abs, b * 4 + k + 1)
                    v.tensor_scalar(pos[:, k, :], bank[(7, 0, 1, 6)[k]][:, :], dpb[:, k:k + 1], 0.0, ALU.add, ALU.max).then_inc(dt_pos, 1)
                for k in range(2, 4):
                    v.wait_ge(aT_ps, b * 4 + k + 1)
                    v.tensor_copy(attT[:, k, :], bank[2 + k][:, :]).then_inc(aT_sb, 1)
                v.wait_ge(sp_one, b + 1)
                v.wait_ge(dt_pos, b * 4 + 4)
                v.scalar_tensor_tensor(out=ex[:, :, :], in0=one[:, :, :], scalar=-1.0, in1=ex[:, :, :], op0=ALU.add, op1=ALU.subtract).then_inc(sp_fix, 1)
                v.wait_ge(sp_fix, b + 1)
                v.tensor_tensor(pos[:, :, :], pos[:, :, :], ex[:, :, :], ALU.subtract).then_inc(sp_sum, 1)
                v.wait_ge(sp_sum, b + 1)
                v.wait_ge(sp_ln, b + 1)
                v.tensor_tensor(dtv[:, :, :], pos[:, :, :], ln[:, :, :], ALU.add).then_inc(dt_done, 1)
                for t in range(LT):
                    v.wait_ge(o_ps, b * 4 + t + 1)
                    v.tensor_tensor(X[:, ds(b * LT + t, 1), :].rearrange("p o n -> p (o n)"), bank[(7, 0, 1, 6)[t]][:, :],
                                    X[:, ds(b * LT + t, 1), :].rearrange("p o n -> p (o n)"), ALU.add).then_inc(x1_done, 1)

        @block.gpsimd
        def _(g):
            with g.Fori(0, NB) as b:
                g.wait_ge(sp_ln, b)
                g.wait_ge(sp_fix, b)
                g.wait_ge(sp_exp, b + 1)
                g.sem_inc(passed)
                g.tensor_scalar(one[:, :, :], ex[:, :, :], 1.0, None, ALU.add).then_inc(sp_one, 1)
                g.wait_ge(dt_done, b + 1)
                g.wait_ge(u_done, b * 4 + 4)
                g.wait_ge(stored, b * 64)
                g.tensor_tensor(dtu[:, :, :], dtv[:, :, :], u[:, :, :], ALU.mult).then_inc(dtu_done, 1)


def ln_statistics(v, X, st, mv, rstd, stats, root, n):
    for t in range(NT):
        i = v.bn_stats(st[:, t, :], X[:, t, :])
    i.then_inc(stats, 1)
    v.wait_ge(stats, 4 * n + 1)
    for t in range(NT):
        i = v.bn_aggr(mv[:, t, :], st[:, t, :])
    i.then_inc(stats, 1)
    v.wait_ge(stats, 4 * n + 2)
    v.tensor_scalar(rstd[:, :], mv[:, :, 1], EPS, None, ALU.add).then_inc(stats, 1)
    v.wait_ge(root, n + 1)
    v.reciprocal(rstd[:, :], rstd[:, :]).then_inc(stats, 1)
    v.wait_ge(stats, 4 * n + 4)


def ln_root(act, rstd, stats, root, n):
    act.wait_ge(stats, 4 * n + 3)
    act.activation(rstd[:, :], rstd[:, :], ACT.Sqrt).then_inc(root, 1)


def ln_tile(v, X, t, mv, rstd, out):
    mean, scale = (c.rearrange("p o -> p o") for c in (mv[:, ds(t, 1), 0], rstd[:, ds(t, 1)]))
    return v.tensor_scalar(out, X[:, ds(t, 1), :].rearrange("p o n -> p (o n)"), mean, scale, ALU.subtract, ALU.mult)


def block_b0(nc, a, X, ident, bank, hT, Rt, powers):
    with ExitStack() as s:
        sb, sem = mem(nc, s, "B0")
        table = sb("table", [P, IPAD])
        st, mv, rstd, xn = sb("st", [P, NT, 6]), sb("mv", [P, NT, 2]), sb("rstd", [P, NT]), sb("xn", [P, 2, D])
        stats, root = sem("stats"), sem("root")
        ld, ln_step, xn_done, tr, hT_done, r_done = (sem(n) for n in ("ld", "ln_step", "xn_done", "tr", "hT_done", "r_done"))
        block = s.enter_context(nc.Block())

        @block.sync
        def _(sp):
            sp.dma_start(table[:, :], a["table"]).then_inc(ld, 16)
            sp.dma_start(powers[:, :, :, :], a["powers"]).then_inc(ld, 16)
            for n, name in enumerate(("gate", "up", "down")):
                for q in range(4):
                    sp.dma_start(Rt[n][q:P:4, :], a["taps_" + name]).then_inc(ld, 16)

        @block.gpsimd
        def _(g):
            g.wait_ge(ld, 16 * 14)
            for n in range(3):
                g.tensor_tensor(Rt[n][:, :], Rt[n][:, :], table[:, :], ALU.mult).then_inc(r_done, 1)
            g.wait_ge(r_done, 3)

        @block.vector
        def _(v):
            ln_statistics(v, X, st, mv, rstd, stats, root, 0)
            with v.Fori(0, NT // 2) as pair:
                for j in range(2):
                    v.wait_ge(tr, pair * 2)
                    ln_tile(v, X, pair * 2 + j, mv, rstd, xn[:, j, :]).then_inc(xn_done, 1)

        @block.tensor
        def _(pe):
            with pe.Fori(0, NT // 2) as pair:
                for j in range(2):
                    pe.wait_ge(xn_done, pair * 2 + j + 1)
                    pe.wait_ge(hT_done, pair * 2)
                    for k in range(KC):
                        mm = pe.transpose(bank[j][:, k * P:(k + 1) * P], xn[:, j, k * P:(k + 1) * P], ident[:, :])
                    mm.then_inc(tr, 1)

        @block.scalar
        def _(act):
            ln_root(act, rstd, stats, root, 0)
            with act.Fori(0, NT // 2) as pair:
                for j in range(2):
                    act.wait_ge(tr, pair * 2 + j + 1)
                    act.activation(hT[:, :, ds((pair * 2 + j) * P, P)], bank[j][:, :].rearrange("p (k l) -> p k l", k=KC), ACT.Copy).then_inc(hT_done, 1)


def block_b(nc, a, X, negA, bank, hT, Rt, powers, dt_d, dtu_d, du_d, bc_d, y_d):
    with ExitStack() as s:
        sb, sem = mem(nc, s, "B")
        G, U = [bank[0], bank[2]], [bank[1], bank[3]]
        Yb, WA, WB = [bank[4], bank[5]], bank[6], bank[7]
        Wg, Wu = [sb(f"Wg{i}", [P, KC, GW]) for i in range(2)], [sb(f"Wu{i}", [P, KC, GW]) for i in range(2)]
        Wd = [sb(f"Wd{i}", [P, 2, D]) for i in range(2)]
        words = [sb(f"masks{i}", [P, GW + D // 2], I32) for i in range(2)]
        msk = [w[:, :].bitcast(U8) for w in words]
        sil = [sb(f"sil{i}", [P, L]) for i in range(2)]
        inter = [sb(f"inter{i}", [P, 2, L]) for i in range(2)]
        dtv, dtu, yac = sb("dtv", [P, KC, L]), sb("dtu", [P, KC, L]), sb("yac", [P, KC, L])
        Bb, Cb = [sb(f"Bb{i}", [P, 2, L]) for i in range(2)], [sb(f"Cb{i}", [P, 2, L]) for i in range(2)]
        NR, NQ = 3, 2
        dA, dBu, S = (sb(n, [P, NR, L]) for n in ("dA", "dBu", "S"))
        prod = sb("prod", [P, NQ, L])

        ld_dt, ld_yac = sem("ld_dt"), sem("ld_yac")
        ld_bc, ld_msk = [sem(f"ld_bc{i}") for i in range(2)], [sem(f"ld_msk{i}") for i in range(2)]
        g_ps, u_ps, sil_done, inter_done, y_ps, add_done = (sem(n) for n in ("g_ps", "u_ps", "sil_done", "inter_done", "y_ps", "add_done"))
        passed = sem("passed")
        w_ps, w_first, w_done = sem("w_ps"), sem("w_first"), sem("w_done")
        dA_done, dBu_done, s_done, prod_done, yac_done, stored = (sem(n) for n in ("dA_done", "dBu_done", "s_done", "prod_done", "yac_done", "stored"))
        block = s.enter_context(nc.Block())
        NU = 6
        IT = 8 * 8

        def w_unit(unit, buf):
            if unit < 4:
                w = (Wg, Wu)[unit // 2][buf]
                return w[:, 2 * (unit % 2):2 * (unit % 2) + 2, :].rearrange("p c i -> p (c i)")
            return Wd[buf][:, unit - 4, :]

        def unit_order():
            return {(4 * h + 1 + unit // 2, unit % 2): (1 - h, unit) for h in range(2) for unit in range(NU)}

        UNITS = unit_order()
        COUNT = {k: n for n, k in enumerate(sorted(UNITS))}

        @block.sync
        def _(sp):
            sp.dma_start(words[0][:, :], a["masks"][0]).then_inc(ld_msk[0], 16)
            with sp.Fori(0, NB) as b:
                sp.wait_ge(s_done, b * IT)
                sp.dma_start(dtv[:, :, :], dt_d[ds(b, 1)].rearrange("o k p l -> p (o k) l")).then_inc(ld_dt, 16)
                sp.dma_start(dtu[:, :, :], dtu_d[ds(b, 1)].rearrange("o k p l -> p (o k) l")).then_inc(ld_dt, 16)
                for j in range(8):
                    if j >= 2:
                        sp.wait_ge(prod_done, b * IT + 8 * (j - 1))
                    else:
                        sp.wait_ge(prod_done, b * IT)
                    for m, t in ((0, Bb), (NS, Cb)):
                        src = bc_d[ds(b, 1), m + 2 * j:m + 2 * j + 2, :].rearrange("o n l -> o (n l)").broadcast_to([P, 2 * L])
                        sp.dma_start(t[j % 2][:, :, :].rearrange("p n l -> p (n l)"), src).then_inc(ld_bc[j % 2], 16)
                    if j == 0:
                        sp.wait_ge(stored, b * 16)
                        sp.dma_start(yac[:, :, :], du_d[ds(b, 1)].rearrange("o k p l -> p (o k) l")).then_inc(ld_yac, 16)
                        sp.wait_ge(w_done, b * 2 * NU + NU)
                        sp.dma_start(words[1][:, :], a["masks"][ds(b * 2 + 1, 1)].rearrange("o p n -> (o p) n")).then_inc(ld_msk[1], 16)
                    if j == 4:
                        sp.dma_start(words[0][:, :], a["masks"][ds(b * 2 + 2, 1)].rearrange("o p n -> (o p) n")).then_inc(ld_msk[0], 16)
                sp.wait_ge(yac_done, b * IT + IT)
                sp.dma_start(y_d[ds(b, 1)].rearrange("o k p l -> p (o k) l"), yac[:, :, :]).then_inc(stored, 16)
            sp.wait_ge(stored, NB * 16)

        def pe_unit(pe, unit, buf, b, done):
            pe.wait_ge(w_done, done)
            col = b * L + buf * GW if buf else b * L
            for ab, ps in enumerate((WA, WB)):
                if unit < 4:
                    for c in range(2):
                        cc = 2 * (unit % 2) + c
                        mm = pe.matmul(ps[:, c * GW:(c + 1) * GW], powers[:, cc, ab, :], Rt[unit // 2][:, ds(col, GW)], start=True, stop=True)
                else:
                    mm = pe.matmul(ps[:, :], powers[:, 2 * buf + unit - 4, ab, :], Rt[2][:, ds(b, D, 4)], start=True, stop=True)
            mm.then_inc(w_ps, 1)

        def act_unit(act, unit, buf, n):
            act.wait_ge(w_ps, n + 1)
            act.activation(w_unit(unit, buf), WA[:, :], ACT.Copy).then_inc(w_first, 1)

        def dve_unit(v, unit, buf, n, masks):
            v.wait_ge(ld_msk[buf], masks)
            v.wait_ge(w_first, n + 1)
            v.sem_inc(passed)
            m = msk[buf][:, (unit % 2) * 2 * GW:(unit % 2 + 1) * 2 * GW] if unit < 4 else msk[buf][:, 4 * GW + (unit - 4) * D:4 * GW + (unit - 3) * D]
            v.copy_predicated(w_unit(unit, buf), m, WB[:, :]).then_inc(w_done, 1)

        @block.tensor
        def _(pe):
            for unit in range(NU):
                pe_unit(pe, unit, 0, 0, unit)
            with pe.Fori(0, NB) as b:
                def w_slot(j, pos):
                    if (j, pos) in UNITS:
                        buf, unit = UNITS[(j, pos)]
                        n = NU + COUNT[(j, pos)]
                        pe_unit(pe, unit, buf, b if buf else b + 1, b * 2 * NU + n)

                def gate_up(j, ch):
                    q = 2 * j + ch
                    w, tb = j // 4, j % 4
                    pe.wait_ge(inter_done, b * 16 + max(q - 1, 0))
                    for ps, W, done in ((G[ch], Wg[w], g_ps), (U[ch], Wu[w], u_ps)):
                        for k in range(KC):
                            mm = pe.matmul(ps[:, :], W[:, k, ch * P:(ch + 1) * P], hT[:, k, tb * L:(tb + 1) * L], start=k == 0, stop=k == KC - 1)
                        mm.then_inc(done, 1)

                def down(j):
                    w = j // 4
                    pe.wait_ge(inter_done, b * 16 + 2 * j + 2)
                    for t in range(LT):
                        n = 4 * j + t
                        pe.wait_ge(add_done, b * 32 + max(n - 1, 0))
                        for ch in range(2):
                            mm = pe.matmul(Yb[t % 2][:, :], inter[j % 2][:, ch, t * P:(t + 1) * P], Wd[w][:, ch, :], start=ch == 0, stop=ch == 1)
                        mm.then_inc(y_ps, 1)

                for j in range(8):
                    if j % 4 == 0:
                        pe.wait_ge(w_done, b * 2 * NU + NU * (1 + j // 4))
                    w_slot(j, 0)
                    gate_up(j, 0)
                    w_slot(j, 1)
                    if j:
                        down(j - 1)
                    gate_up(j, 1)
                down(7)

        @block.scalar
        def _(act):
            for unit in range(NU):
                act_unit(act, unit, 0, unit)
            with act.Fori(0, NB) as b:
                def silu(j, ch):
                    q = 2 * j + ch
                    act.wait_ge(g_ps, b * 16 + q + 1)
                    act.wait_ge(inter_done, b * 16 + max(q - 1, 0))
                    act.activation(sil[ch][:, :], G[ch][:, :], ACT.Silu).then_inc(sil_done, 1)

                def decay(j, i):
                    n = 8 * j + i
                    act.wait_ge(s_done, b * IT + max(n - NR + 1, 0))
                    act.activation(dA[:, n % NR, :], dtv[:, i % 4, :], ACT.Exp, scale=negA[:, i % 4, 2 * j + i // 4:2 * j + i // 4 + 1]).then_inc(dA_done, 1)

                act.wait_ge(ld_dt, b * 32 + 32)
                for j in range(8):
                    for pos in range(2):
                        if (j, pos) in UNITS:
                            buf, unit = UNITS[(j, pos)]
                            act_unit(act, unit, buf, b * 2 * NU + NU + COUNT[(j, pos)])
                        for i in range(4 * pos, 4 * pos + 4):
                            decay(j, i)
                        silu(j, pos)

        @block.vector
        def _(v):
            for unit in range(NU):
                dve_unit(v, unit, 0, unit, 16)
            with v.Fori(0, NB) as b:
                def mult(j, ch):
                    q = 2 * j + ch
                    v.wait_ge(sil_done, b * 16 + q + 1)
                    v.wait_ge(u_ps, b * 16 + q + 1)
                    if j >= 2:
                        v.wait_ge(y_ps, b * 32 + 4 * (j - 1))
                    else:
                        v.wait_ge(y_ps, b * 32)
                    v.tensor_tensor(inter[j % 2][:, ch, :], U[ch][:, :], sil[ch][:, :], ALU.mult).then_inc(inter_done, 1)

                def add(j, t):
                    v.wait_ge(y_ps, b * 32 + 4 * j + t + 1)
                    x = X[:, (j % 4) * LT + t, :]
                    v.tensor_tensor(x, Yb[t % 2][:, :], x, ALU.add).then_inc(add_done, 1)

                def drive(j, i):
                    n = 8 * j + i
                    if i == 0:
                        v.wait_ge(ld_bc[j % 2], b * 128 + 32 * (j // 2 + 1))
                    v.wait_ge(s_done, b * IT + max(n - NR + 1, 0))
                    v.tensor_tensor(dBu[:, n % NR, :], dtu[:, i % 4, :], Bb[j % 2][:, i // 4, :], ALU.mult).then_inc(dBu_done, 1)

                def scan(n):
                    v.wait_ge(dBu_done, b * IT + n + 1)
                    v.wait_ge(dA_done, b * IT + n + 1)
                    v.wait_ge(prod_done, b * IT + max(n - NR + 1, 0))
                    v.tensor_tensor_scan(S[:, n % NR, :], dA[:, n % NR, :], dBu[:, n % NR, :], 0.0, ALU.mult, ALU.add).then_inc(s_done, 1)

                v.wait_ge(ld_dt, b * 32 + 32)
                for j in range(8):
                    for i in range(8):
                        drive(j, i)
                        if 8 * j + i >= 1:
                            scan(8 * j + i - 1)
                        if i == 0 and j:
                            mult(j - 1, 1)
                        if i == 3:
                            mult(j, 0)
                        if i >= 4 and j:
                            add(j - 1, i - 4)
                        if i in (0, 4) and (j, i // 4) in UNITS:
                            buf, unit = UNITS[(j, i // 4)]
                            dve_unit(v, unit, buf, b * 2 * NU + NU + COUNT[(j, i // 4)], b * 16 + (16 if buf else 32))
                scan(IT - 1)
                mult(7, 1)
                for t in range(LT):
                    add(7, t)

        @block.gpsimd
        def _(g):
            with g.Fori(0, NB) as b:
                def weigh(n):
                    j, i = n // 8, n % 8
                    if i == 0:
                        g.wait_ge(ld_bc[j % 2], b * 128 + 32 * (j // 2 + 1))
                    g.wait_ge(s_done, b * IT + n + 1)
                    g.wait_ge(yac_done, b * IT + max(n - NQ + 1, 0))
                    g.tensor_tensor(prod[:, n % NQ, :], S[:, n % NR, :], Cb[j % 2][:, i // 4, :], ALU.mult).then_inc(prod_done, 1)

                def gather(n):
                    g.wait_ge(prod_done, b * IT + n + 1)
                    g.wait_ge(yac_done, b * IT + max(n - 3, 0))
                    g.tensor_tensor(yac[:, n % 4, :], yac[:, n % 4, :], prod[:, n % NQ, :], ALU.add).then_inc(yac_done, 1)

                for n in range(IT):
                    weigh(n)
                    if n == 1:
                        g.wait_ge(ld_yac, b * 16 + 16)
                    if n:
                        gather(n - 1)
                gather(IT - 1)


def block_c(nc, a, X, ident, bank, hhi, hlo, y_d, rw_d):
    with ExitStack() as s:
        sb, sem = mem(nc, s, "C")
        st, mv, rstd = sb("st", [P, NT, 6]), sb("mv", [P, NT, 2]), sb("rstd", [P, NT])
        stats, root = sem("stats"), sem("root")
        xn = sb("xn", [P, 2, D])
        y, z, yg = sb("y", [P, LT, L]), sb("z", [P, LT, D]), sb("yg", [P, LT, L])
        gk = sb("gk", [P, KC, NE])
        hf = sb("hf", [P, 2, KC, P])
        lg, pe_, pr, mk, rw = (sb(n, [P, NT, NE]) for n in ("logit", "expo", "prob", "rest", "weight"))
        mx, sm, inv, top, tsum, tinv = sb("mx", [P, NT]), sb("sm", [P, NT]), sb("inv", [P, NT]), sb("top", [P, NT, 8]), sb("tsum", [P, NT]), sb("tinv", [P, NT])
        rwT = sb("rwT", [NE, NB * L])
        ld_y, ld_g, ln_step, z_in, z_done, g_done = (sem(n) for n in ("ld_y", "ld_g", "ln_step", "z_in", "z_done", "g_done"))
        yT_ps, x2_done, x2_step, h_in, h_ps, h_sb, h_hi, h_lo = (sem(n) for n in ("yT_ps", "x2_done", "x2_step", "h_in", "h_ps", "h_sb", "h_hi", "h_lo"))
        lg_ps, lg_sb, r_step, r_exp, rT_ps, rT_sb, stored = (sem(n) for n in ("lg_ps", "lg_sb", "r_step", "r_exp", "rT_ps", "rT_sb", "stored"))
        block = s.enter_context(nc.Block())
        RS = 12

        @block.sync
        def _(sp):
            sp.dma_start(gk[:, :, :], a["gk"]).then_inc(ld_g, 16)
            with sp.Fori(0, NB) as b:
                sp.wait_ge(g_done, b)
                sp.dma_start(y[:, :, :], y_d[ds(b, 1)].rearrange("o k p l -> p (o k) l")).then_inc(ld_y, 16)
            sp.wait_ge(rT_sb, 4)
            sp.dma_start(rw_d, rwT[:, :]).then_inc(stored, 16)
            sp.wait_ge(stored, 16)

        @block.vector
        def _(v):
            ln_statistics(v, X, st, mv, rstd, stats, root, 0)
            with v.Fori(0, NB) as b:
                v.wait_ge(z_done, b)
                for t in range(LT):
                    i = ln_tile(v, X, b * LT + t, mv, rstd, z[:, t, :])
                i.then_inc(z_in, 1)
                v.wait_ge(z_done, b + 1)
                v.wait_ge(ld_y, b * 16 + 16)
                v.wait_ge(yT_ps, b * 4)
                v.tensor_tensor(yg[:, :, :], y[:, :, :], z[:, :, :], ALU.mult).then_inc(g_done, 1)
                for t in range(LT):
                    v.wait_ge(yT_ps, b * 4 + t + 1)
                    x = X[:, ds(b * LT + t, 1), :].rearrange("p o n -> p (o n)")
                    v.tensor_tensor(x, bank[t][:, :], x, ALU.add).then_inc(x2_done, 1)
            v.wait_ge(x2_done, NT)
            ln_statistics(v, X, st, mv, rstd, stats, root, 1)
            with v.Fori(0, NT // 2) as pair:
                for j in range(2):
                    v.wait_ge(h_ps, pair * 2)
                    ln_tile(v, X, pair * 2 + j, mv, rstd, xn[:, j, :]).then_inc(h_in, 1)
                for j in range(2):
                    v.wait_ge(h_hi, pair * 2 + j + 1)
                    v.tensor_tensor(hlo[:, :, ds((pair * 2 + j) * P, P)], hf[:, j, :, :], hhi[:, :, ds((pair * 2 + j) * P, P)], ALU.subtract).then_inc(h_lo, 1)
                    v.wait_ge(lg_ps, pair * 2 + j + 1)
                    v.tensor_copy(lg[:, ds(pair * 2 + j, 1), :].rearrange("p o e -> p (o e)"), bank[2 + j][:, 0:NE]).then_inc(lg_sb, 1)
            v.wait_ge(lg_sb, NT)
            n = [0]

            def step(i):
                n[0] += 1
                i.then_inc(r_step, 1)
                v.wait_ge(r_step, n[0])

            def cols(t):
                return t[:, :].rearrange("p (t o) -> p t o", o=1).broadcast_to([P, NT, NE])
            step(v.tensor_reduce(mx[:, :], lg[:, :, :], AX, ALU.max))
            step(v.tensor_tensor(lg[:, :, :], lg[:, :, :], cols(mx), ALU.subtract))
            v.wait_ge(r_exp, 1)
            step(v.tensor_reduce(sm[:, :], pe_[:, :, :], AX, ALU.add))
            step(v.reciprocal(inv[:, :], sm[:, :]))
            step(v.tensor_tensor(pr[:, :, :], pe_[:, :, :], cols(inv), ALU.mult))
            for t in range(NT):
                i = v.max(top[:, t, :], pr[:, t, :])
            step(i)
            for t in range(NT):
                i = v.match_replace(mk[:, t, :], top[:, t, :], pr[:, t, :], -1.0)
            step(i)
            step(v.tensor_scalar(mk[:, :, :], mk[:, :, :], 0.0, None, ALU.is_lt))
            step(v.tensor_tensor(rw[:, :, :], mk[:, :, :], pr[:, :, :], ALU.mult))
            step(v.tensor_reduce(tsum[:, :], rw[:, :, :], AX, ALU.add))
            step(v.reciprocal(tinv[:, :], tsum[:, :]))
            step(v.tensor_tensor(rw[:, :, :], rw[:, :, :], cols(tinv), ALU.mult))
            assert n[0] == RS
            for b in range(NB):
                v.wait_ge(rT_ps, b + 1)
                v.tensor_copy(rwT[:, b * L:(b + 1) * L], bank[4 + b][0:NE, :]).then_inc(rT_sb, 1)

        @block.scalar
        def _(act):
            ln_root(act, rstd, stats, root, 0)
            with act.Fori(0, NB) as b:
                act.wait_ge(z_in, b + 1)
                act.activation(z[:, :, :], z[:, :, :], ACT.Silu).then_inc(z_done, 1)
            ln_root(act, rstd, stats, root, 1)
            with act.Fori(0, NT // 2) as pair:
                for j in range(2):
                    act.wait_ge(h_ps, pair * 2 + j + 1)
                    act.wait_ge(h_lo, pair * 2)
                    act.wait_ge(lg_ps, pair * 2)
                    act.activation(hf[:, j, :, :], bank[j][:, :].rearrange("p (k l) -> p k l", k=KC), ACT.Copy).then_inc(h_sb, 1)
                    act.activation(hhi[:, :, ds((pair * 2 + j) * P, P)], bank[j][:, :].rearrange("p (k l) -> p k l", k=KC), ACT.Copy).then_inc(h_hi, 1)
            act.wait_ge(r_step, 2)
            act.activation(pe_[:, :, :], lg[:, :, :], ACT.Exp).then_inc(r_exp, 1)

        @block.tensor
        def _(pe):
            with pe.Fori(0, NB) as b:
                pe.wait_ge(g_done, b + 1)
                pe.wait_ge(x2_done, b * 4)
                for t in range(LT):
                    for k in range(KC):
                        mm = pe.transpose(bank[t][:, k * P:(k + 1) * P], yg[:, k, t * P:(t + 1) * P], ident[:, :])
                    mm.then_inc(yT_ps, 1)
            pe.wait_ge(x2_done, NT)
            pe.wait_ge(ld_g, 16)
            with pe.Fori(0, NT // 2) as pair:
                for j in range(2):
                    pe.wait_ge(h_in, pair * 2 + j + 1)
                    pe.wait_ge(h_hi, pair * 2)
                    for k in range(KC):
                        mm = pe.transpose(bank[j][:, k * P:(k + 1) * P], xn[:, j, k * P:(k + 1) * P], ident[:, :])
                    mm.then_inc(h_ps, 1)
                for j in range(2):
                    pe.wait_ge(h_sb, pair * 2 + j + 1)
                    pe.wait_ge(lg_sb, pair * 2)
                    for k in range(KC):
                        mm = pe.matmul(bank[2 + j][:, 0:NE], hf[:, j, k, :], gk[:, k, :], start=k == 0, stop=k == KC - 1)
                    mm.then_inc(lg_ps, 1)
            pe.wait_ge(r_step, RS)
            for b in range(NB):
                for t in range(LT):
                    mm = pe.transpose(bank[4 + b][0:NE, t * P:(t + 1) * P], rw[:, b * LT + t, :], ident[:, :])
                mm.then_inc(rT_ps, 1)


def block_d(nc, a, X, bank, hhi, hlo, rw_d):
    with ExitStack() as s:
        sb, sem = mem(nc, s, "D")
        PW = PC * P
        G, U, Yb = [bank[0], bank[2]], [bank[1], bank[3]], [bank[4], bank[5]]
        W = [[[sb(f"{n}{h}{i}", [P, 4 * PW], F32R) for h in ("hi", "lo")] for n in ("gate", "up", "down")] for i in range(2)]
        NRAW, HU = 3, 2 * PW
        raw = sb("raw", [P, NRAW, HU])
        sil = [sb(f"sil{i}", [P, L]) for i in range(2)]
        ihi, ilo = sb("ihi", [P, PC, L], F32R), sb("ilo", [P, PC, L], F32R)
        rwb = [sb(f"rwb{i}", [P, PC, L]) for i in range(2)]
        passed = sem("passed")
        ld_raw, ld_rw, w_hi, w_lo = [sem(f"ld_raw{i}") for i in range(NRAW)], [sem(f"ld_rw{i}") for i in range(2)], sem("w_hi"), sem("w_lo")
        g_ps, u_ps, sil_done, silw_done, v_done, i_hi, i_lo, y_ps, add_done, stored = (
            sem(n) for n in ("g_ps", "u_ps", "sil_done", "silw_done", "v_done", "i_hi", "i_lo", "y_ps", "add_done", "stored"))
        block = s.enter_context(nc.Block())
        NP = NE // 2
        UN = 6
        SL = 8

        def w_half(buf, unit, part):
            m, half = divmod(unit, 2)
            return W[buf][m][part][:, half * HU:(half + 1) * HU]

        def gu(buf, m, part, k, ch):
            return W[buf][m][part][:, k * PW + ch * P:k * PW + (ch + 1) * P]

        @block.sync
        def _(sp):
            def load_unit(pair, unit, n):
                m, half = divmod(unit, 2)
                src = a[("eg", "eu", "ed")[m]][ds(pair, 1)] if not isinstance(pair, int) else a[("eg", "eu", "ed")[m]][pair:pair + 1]
                sp.dma_start(raw[:, unit % NRAW, :], src[:, :, half * HU:(half + 1) * HU].rearrange("o p n -> p (o n)")).then_inc(ld_raw[unit % NRAW], 16)

            def load_rw(pair2, j):
                e0 = pair2 * 4 + 2 * (j // 4)
                dst = rwb[j % 2]
                tok = slice((j % 4) * L, (j % 4 + 1) * L)
                for p0, p1, ch, e in ((0, P, 0, 0), (0, P // 2, 1, 0), (P // 2, P, 1, 1), (0, P, 2, 1)):
                    sp.dma_start(dst[p0:p1, ch, :], rw_d[ds(e0 + e, 1), tok].broadcast_to([p1 - p0, L])).then_inc(ld_rw[j % 2], 16)

            for unit in range(UN):
                if unit >= NRAW:
                    sp.wait_ge(w_lo, unit - NRAW + 1)
                load_unit(0, unit, unit)
            with sp.Fori(0, NP // 2) as q:
                for j in range(SL):
                    sp.wait_ge(silw_done, q * 24 + 3 * max(j - 1, 0))
                    load_rw(q, j)
                    if j % 4 < 3:
                        for unit in (2 * (j % 4), 2 * (j % 4) + 1):
                            n = UN * (1 + j // 4) + unit
                            sp.wait_ge(w_lo, q * 2 * UN + n - NRAW + 1)
                            load_unit(q * 2 + 1 + j // 4, unit, n)
            sp.wait_ge(add_done, 16 * NP)
            sp.dma_start(a["out"].rearrange("b (t p) n -> p (b t) n", p=P), X[:, :, :]).then_inc(stored, 16)
            sp.wait_ge(stored, 16)

        def split_hi(g, buf, unit, n):
            g.wait_ge(ld_raw[unit % NRAW], (n // NRAW) * 16 + 16 if isinstance(n, int) else n)
            g.sem_inc(passed)
            g.tensor_copy(w_half(buf, unit, 0), raw[:, unit % NRAW, :]).then_inc(w_hi, 1)

        @block.gpsimd
        def _(g):
            for unit in range(UN):
                split_hi(g, 0, unit, unit)
            with g.Fori(0, NP // 2) as q:
                def weigh(j, ch):
                    c = 3 * j + ch
                    if ch == 0:
                        g.wait_ge(ld_rw[j % 2], q * 256 + 64 * (j // 2 + 1))
                    g.wait_ge(sil_done, q * 24 + c + 1)
                    g.tensor_tensor(sil[c % 2][:, :], sil[c % 2][:, :], rwb[j % 2][:, ch, :], ALU.mult).then_inc(silw_done, 1)
                for j in range(SL):
                    weigh(j, 0)
                    if j % 4 < 3:
                        for i, unit in enumerate((2 * (j % 4), 2 * (j % 4) + 1)):
                            if j == 0 or j == 4:
                                g.wait_ge(y_ps, q * 32 + 4 * j)
                            g.wait_ge(ld_raw[unit % NRAW], q * 64 + (UN * (1 + j // 4) + unit) // NRAW * 16 + 16)
                            g.sem_inc(passed)
                            g.tensor_copy(w_half(1 - j // 4, unit, 0), raw[:, unit % NRAW, :]).then_inc(w_hi, 1)
                            if i == 0:
                                weigh(j, 1)
                    else:
                        weigh(j, 1)
                    weigh(j, 2)

        @block.vector
        def _(v):
            def split_lo(buf, unit, n):
                v.wait_ge(w_hi, n + 1)
                v.tensor_tensor(w_half(buf, unit, 1), raw[:, unit % NRAW, :], w_half(buf, unit, 0), ALU.subtract).then_inc(w_lo, 1)

            for unit in range(UN):
                split_lo(0, unit, unit)
            with v.Fori(0, NP // 2) as q:
                def value(j, ch):
                    c = 3 * j + ch
                    v.wait_ge(u_ps, q * 24 + c + 1)
                    v.wait_ge(silw_done, q * 24 + c + 1)
                    v.tensor_tensor(sil[c % 2][:, :], U[c % 2][:, :], sil[c % 2][:, :], ALU.mult).then_inc(v_done, 1)

                def rest(j, ch):
                    c = 3 * j + ch
                    v.wait_ge(i_hi, q * 24 + c + 1)
                    v.tensor_tensor(ilo[:, ch, :], sil[c % 2][:, :], ihi[:, ch, :], ALU.subtract).then_inc(i_lo, 1)

                def add(j, t):
                    v.wait_ge(y_ps, q * 32 + 4 * j + t + 1)
                    x = X[:, (j % 4) * LT + t, :]
                    v.tensor_tensor(x, Yb[t % 2][:, :], x, ALU.add).then_inc(add_done, 1)

                for j in range(SL):
                    value(j, 0)
                    if j:
                        for t in range(LT):
                            add(j - 1, t)
                    rest(j, 0)
                    value(j, 1)
                    rest(j, 1)
                    if j % 4 < 3:
                        for unit in (2 * (j % 4), 2 * (j % 4) + 1):
                            split_lo(1 - j // 4, unit, q * 2 * UN + UN * (1 + j // 4) + unit)
                    value(j, 2)
                    rest(j, 2)
                for t in range(LT):
                    add(SL - 1, t)

        @block.scalar
        def _(act):
            with act.Fori(0, NP // 2) as q:
                for j in range(SL):
                    for ch in range(PC):
                        c = 3 * j + ch
                        act.wait_ge(g_ps, q * 24 + c + 1)
                        act.wait_ge(i_lo, q * 24 + max(c - 1, 0))
                        act.activation(sil[c % 2][:, :], G[c % 2][:, :], ACT.Silu).then_inc(sil_done, 1)
                        act.wait_ge(v_done, q * 24 + c + 1)
                        act.wait_ge(y_ps, q * 32 + 4 * j)
                        act.activation(ihi[:, ch, :], sil[c % 2][:, :], ACT.Copy).then_inc(i_hi, 1)

        @block.tensor
        def _(pe):
            with pe.Fori(0, NP // 2) as q:
                def gate_up(j, ch):
                    c = 3 * j + ch
                    buf, tok = j // 4, slice((j % 4) * L, (j % 4 + 1) * L)
                    pe.wait_ge(v_done, q * 24 + max(c - 1, 0))
                    for m, (ps, done) in enumerate(((G[c % 2], g_ps), (U[c % 2], u_ps))):
                        for k in range(KC):
                            hi = gu(buf, m, 0, k, ch)
                            pe.matmul(ps[:, :], hi, hhi[:, k, tok], start=k == 0, stop=False)
                            pe.matmul(ps[:, :], hi, hlo[:, k, tok], start=False, stop=False)
                            mm = pe.matmul(ps[:, :], gu(buf, m, 1, k, ch), hhi[:, k, tok], start=False, stop=k == KC - 1)
                        mm.then_inc(done, 1)

                def down(j):
                    buf = j // 4
                    pe.wait_ge(i_lo, q * 24 + 3 * j + 3)
                    for t in range(LT):
                        pe.wait_ge(add_done, q * 32 + max(4 * j + t - 1, 0))
                        for ch in range(PC):
                            dh, dl = (W[buf][2][h][:, ch * D:(ch + 1) * D] for h in range(2))
                            th = ihi[:, ch, t * P:(t + 1) * P]
                            pe.matmul(Yb[t % 2][:, :], th, dh, start=ch == 0, stop=False)
                            pe.matmul(Yb[t % 2][:, :], th, dl, start=False, stop=False)
                            mm = pe.matmul(Yb[t % 2][:, :], ilo[:, ch, t * P:(t + 1) * P], dh, start=False, stop=ch == PC - 1)
                        mm.then_inc(y_ps, 1)

                for j in range(SL):
                    if j % 4 == 0:
                        pe.wait_ge(w_lo, q * 2 * UN + UN * (1 + j // 4))
                    gate_up(j, 0)
                    if j:
                        down(j - 1)
                    gate_up(j, 1)
                    gate_up(j, 2)
                down(SL - 1)


def kernel(**inputs):
    import concourse.bacc as bacc
    from concourse.bass_utils import run_bass_kernel_spmd as run

    x = {k: np.ascontiguousarray(v) for k, v in inputs.items()}
    table, taps, powers, masks = spline_constants()

    def chunked(w):
        return w.reshape(-1, P, w.shape[-1]).transpose(1, 0, 2)

    def windows(cp):
        return np.where(taps >= 0, cp[np.maximum(taps, 0)], np.float32(0)).reshape(KC * 2 * 4, IPAD)

    def experts(w):
        return w.reshape(NE // 2, 2, KC, P, M).transpose(0, 3, 2, 1, 4).reshape(NE // 2, P, KC * 2 * M)

    def padded(w):
        return np.concatenate([w, np.zeros_like(w[:1])])

    ed = x["L1_ffn_down_proj"].reshape(NE // 2, PC, P, D).transpose(0, 2, 1, 3).reshape(NE // 2, P, PC * D)
    arrays = {
        "x": x["x"],
        "ctxT": x["ctx_1024"].transpose(0, 2, 1).reshape(NB, 2, P, L).transpose(0, 2, 1, 3),
        "wqT": chunked(x["L0_xattn_Wq"].T), "wkT": chunked(x["L0_xattn_Wk"].T),
        "bq": x["L0_xattn_bq"].reshape(P, 1), "bk": x["L0_xattn_bk"].reshape(P, 1),
        "inwT": chunked(x["L1_xattn_in_proj_w"].T),
        "convw": x["L1_xattn_conv_w"].reshape(KC, P, TAPS).transpose(1, 0, 2),
        "convb": x["L1_xattn_conv_b"].reshape(KC, P).T,
        "xpT": chunked(x["L1_xattn_x_proj_w"].T), "dpT": x["L1_xattn_dt_proj_w"].T,
        "dpb": x["L1_xattn_dt_proj_b"].reshape(KC, P).T, "Dp": x["L1_xattn_D"].reshape(KC, P).T,
        "alog": chunked(x["L1_xattn_A_log"]),
        "taps_gate": windows(x["L0_ffn_gate_cp"]), "taps_up": windows(x["L0_ffn_up_cp"]),
        "taps_down": windows(x["L0_ffn_down_cp"]),
        "gk": chunked(x["L1_ffn_gate_kernel"]),
        "eg": padded(experts(x["L1_ffn_gate_proj"])), "eu": padded(experts(x["L1_ffn_up_proj"])), "ed": padded(ed),
        "ident": np.eye(P, dtype=np.float32), "table": table, "powers": powers.reshape(P, KC, 2, P), "masks": masks.view(np.int32),
    }
    nc = bacc.Bacc("TRN2", target_bir_lowering=False, num_devices=1)
    a, sent = {}, {}
    for name, v in arrays.items():
        sent[f"in_{name}"] = np.ascontiguousarray(v)
        a[name] = nc.dram_tensor(f"in_{name}", v.shape, mybir.dt.from_np(v.dtype), kind="ExternalInput").ap()
    a["out"] = nc.dram_tensor("out_x", (NB, L, D), F32, kind="ExternalOutput").ap()
    build(nc, a)
    return run(nc, [sent], core_ids=[0]).results[0]["out_x"]
```

```python
from contextlib import ExitStack

import numpy as np

import concourse.bass as bass
from concourse import mybir

ds = bass.ds
F32 = mybir.dt.float32
F32R = mybir.dt.float32r
U8, I32, U32 = mybir.dt.uint8, mybir.dt.int32, mybir.dt.uint32
ALU = mybir.AluOpType
ACT = mybir.ActivationFunctionType
AX = mybir.AxisListType.X

P = 128
NB, L, D = 4, 512, 512
DC = 256
KC = D // P
LT = L // P
NT = NB * LT
DK = 128
DI, NS, R, TAPS = 512, 16, 16, 4
INTER = 2048
NE, M, TOPK = 32, 192, 8
EPS = 1e-5
NCTRL = max(16, int(INTER * D / 128.9))
GW = 2 * P
NG = INTER // GW
IPAD = INTER + L
ROW = D + NE + 1
REGION = NB * L + P
NTILE = -(-(NB * L * TOPK // P + NE - 1) // 4) * 4
NMETA = NTILE + 4
NW4, AHEAD = 4, 3
BASE, NEW, SRC, DST, CUR, COL, WLD, GO, RLD = range(9)


def spline_constants():
    n = INTER * D
    t = np.linspace(0.0, NCTRL - 1.0, n, dtype=np.float64)
    i = np.clip(np.floor(t).astype(np.int64), 0, NCTRL - 2)
    t0, ia = t[::P], i[::P]
    ib = np.minimum(ia + 1, NCTRL - 2)
    r = (NCTRL - 1.0) / (n - 1)
    cubic = 0.5 * np.array([[0, -1, 2, -1], [2, 0, -5, 3], [0, 1, 4, -3], [0, 0, -1, 1]], np.float64)
    table = np.zeros((KC, 2, 4, 4, IPAD))
    taps = np.full((KC, 2, 4, IPAD), -1, np.int64)
    for ab, ix in enumerate((ia, ib)):
        f = (t0 - ix).reshape(INTER, KC).T
        for j in range(4):
            c0, c1, c2, c3 = cubic[j]
            shifted = [c0 + c1 * f + c2 * f**2 + c3 * f**3, c1 + 2 * c2 * f + 3 * c3 * f**2, c2 + 3 * c3 * f,
                       c3 + 0 * f]
            for p in range(4):
                table[:, ab, j, p, :INTER] = shifted[p]
            taps[:, ab, j, :INTER] = np.clip(ix + j - 1, 0, NCTRL - 1).reshape(INTER, KC).T
    powers = np.zeros((KC, 2, 4, 4, KC, 2, P))
    y = np.arange(P) * r
    for c in range(KC):
        for ab in range(2):
            for p in range(4):
                powers[c, ab, :, p, c, ab, :] = y**p
    second = (i.reshape(-1, P) != ia[:, None]).T.astype(np.uint8)
    by_gate = second.reshape(P, NG, GW, KC).transpose(1, 0, 3, 2).reshape(NG, P, KC * GW)
    by_down = second.reshape(P, D, NG, 2).transpose(2, 0, 3, 1).reshape(NG, P, 2 * D)
    masks = np.zeros((NG + 2, P, KC * GW + 2 * D), np.uint8)
    masks[:NG] = np.concatenate([by_gate, by_down], 2)
    return (table.reshape(P, IPAD).astype(np.float32), taps, powers.reshape(P, KC * 2 * P).astype(np.float32), masks)


def build(nc, a):
    ctx = ExitStack()

    def dram(name, shape):
        return nc.dram_tensor(name, shape, F32).ap()

    dt_d, dtu_d, du_d, y_d = (dram(n, (NB, KC, P, L)) for n in ("dt_d", "dtu_d", "du_d", "y_d"))
    bc_d = dram("bc_d", (NB, 2 * NS, L))
    rows_d = dram("rows_d", (NE * REGION + P, ROW))

    with ctx:
        X = ctx.enter_context(nc.sbuf_tensor("X", [P, NT, D], F32))
        ident = ctx.enter_context(nc.sbuf_tensor("ident", [P, P], F32))
        negA = ctx.enter_context(nc.sbuf_tensor("negA", [P, KC, NS], F32))
        bank = [ctx.enter_context(nc.psum_tensor(f"bank{i}", [P, 512], F32)) for i in range(8)]
        block_a(nc, a, X, ident, negA, bank, dt_d, dtu_d, du_d, bc_d)
        with ExitStack() as s:
            hT = s.enter_context(nc.sbuf_tensor("hT", [P, KC, NB * L], F32))
            Rt = [s.enter_context(nc.sbuf_tensor(f"R{n}", [P, IPAD], F32)) for n in ("gate", "up", "down")]
            powers = s.enter_context(nc.sbuf_tensor("powers", [P, KC, 2, P], F32))
            block_b0(nc, a, X, ident, bank, hT, Rt, powers)
            block_b(nc, a, X, negA, bank, hT, Rt, powers, dt_d, dtu_d, du_d, bc_d, y_d)
        meta = ctx.enter_context(nc.sbuf_tensor("meta", [1, 9, NMETA], I32))
        block_c(nc, a, X, ident, bank, meta, y_d, rows_d)
        block_d(nc, a, ident, bank, meta, rows_d)


def mem(nc, s, block_name):
    def sb(name, shape, dt=F32):
        return s.enter_context(nc.sbuf_tensor(f"{block_name}_{name}", shape, dt))

    def sem(name):
        return s.enter_context(nc.semaphore(f"{block_name}_{name}"))
    return sb, sem


def block_a(nc, a, X, ident, negA, bank, dt_d, dtu_d, du_d, bc_d):
    with ExitStack() as s:
        sb, sem = mem(nc, s, "A")
        ctxT = sb("ctxT", [P, 2, L])
        wqT, wkT = sb("wqT", [P, 2, DK]), sb("wkT", [P, 2, DK])
        bq, bk = sb("bq", [P, 1]), sb("bk", [P, 1])
        inwT = sb("inwT", [P, 2, DI])
        convw, convb = sb("convw", [P, KC, TAPS]), sb("convb", [P, KC])
        xpT = sb("xpT", [P, KC, R + 2 * NS])
        dpT, dpb, Dp = sb("dpT", [R, DI]), sb("dpb", [P, KC]), sb("Dp", [P, KC])
        alog = sb("alog", [P, KC, NS])
        st, mv, rstd = sb("st", [P, 4, 6]), sb("mv", [P, 4, 2]), sb("rstd", [P, 4])
        xn, XT = sb("xn", [P, LT, D]), sb("XT", [P, KC, L])
        att, attT = sb("att", [P, LT, L]), sb("attT", [P, KC, L])
        nmax, rsum, rinv = sb("nmax", [P, 4]), sb("rsum", [P, 4]), sb("rinv", [P, 4])
        qT, kT = sb("qT", [P, L]), sb("kT", [P, L])
        conv, u = sb("conv", [P, KC, L]), sb("u", [P, KC, L])
        xdbl = sb("xdbl", [R + 2 * NS, L])
        pos, ex, one, ln = (sb(n, [P, KC, L]) for n in ("pos", "ex", "one", "ln"))
        dtv, dtu, du = (sb(n, [P, KC, L]) for n in ("dtv", "dtu", "du"))

        ld_x, ld_w, ld_ctx = sem("ld_x"), sem("ld_w"), sem("ld_ctx")
        qk_ps, qk_sb = sem("qk_ps"), sem("qk_sb")
        in_ps, conv_seed, conv_step, conv_done, u_done = (sem(n) for n in ("in_ps", "conv_seed", "conv_step", "conv_done", "u_done"))
        passed = sem("passed")
        ln_var, ln_root = sem("ln_var"), sem("ln_root")
        ln_step, xn_done, xT_ps, xT_sb = sem("ln_step"), sem("xn_done"), sem("xT_ps"), sem("xT_sb")
        e_ps, row_max, att_exp, att_inv, att_done = (sem(n) for n in ("e_ps", "row_max", "att_exp", "att_inv", "att_done"))
        aT_ps, aT_sb, o_ps, x1_done = sem("aT_ps"), sem("aT_sb"), sem("o_ps"), sem("x1_done")
        xd_ps, xd_sb, dt_ps, dt_abs, dt_pos = (sem(n) for n in ("xd_ps", "xd_sb", "dt_ps", "dt_abs", "dt_pos"))
        sp_exp, sp_one, sp_ln, sp_fix, sp_sum, dt_done = (sem(n) for n in ("sp_exp", "sp_one", "sp_ln", "sp_fix", "sp_sum", "dt_done"))
        dtu_done, du_done, stored, negA_exp, negA_done = (sem(n) for n in ("dtu_done", "du_done", "stored", "negA_exp", "negA_done"))
        block = s.enter_context(nc.Block())
        NW = 13

        @block.sync
        def _(sp):
            for dst, name in ((ident[:, :], "ident"), (wqT[:, :, :], "wqT"), (wkT[:, :, :], "wkT"), (bq[:, :], "bq"),
                              (bk[:, :], "bk"), (inwT[:, :, :], "inwT"), (convw[:, :, :], "convw"),
                              (convb[:, :], "convb"), (xpT[:, :, :], "xpT"), (dpT[:, :], "dpT"), (dpb[:, :], "dpb"),
                              (Dp[:, :], "Dp"), (alog[:, :, :], "alog")):
                sp.dma_start(dst, a[name]).then_inc(ld_w, 16)
            for b in range(NB):
                sp.dma_start(X[:, b * LT:(b + 1) * LT, :], a["x"][b].rearrange("(t p) n -> p t n", p=P)).then_inc(ld_x, 16)
            with sp.Fori(0, NB) as b:
                sp.wait_ge(in_ps, b * 4)
                sp.dma_start(ctxT[:, :, :], a["ctxT"][ds(b, 1)].rearrange("o p c l -> p (o c) l")).then_inc(ld_ctx, 16)
                for wait, dst, src in ((xd_sb, bc_d[ds(b, 1)].rearrange("o n l -> (o n) l"), xdbl[R:R + 2 * NS, :]),
                                       (dt_done, dt_d[ds(b, 1)].rearrange("o k p l -> p (o k) l"), dtv[:, :, :]),
                                       (du_done, du_d[ds(b, 1)].rearrange("o k p l -> p (o k) l"), du[:, :, :]),
                                       (dtu_done, dtu_d[ds(b, 1)].rearrange("o k p l -> p (o k) l"), dtu[:, :, :])):
                    sp.wait_ge(wait, b + 1)
                    sp.dma_start(dst, src).then_inc(stored, 16)
            sp.wait_ge(stored, NB * 64)

        @block.tensor
        def _(pe):
            pe.wait_ge(ld_w, 16 * NW)
            with pe.Fori(0, NB) as b:
                pe.wait_ge(ld_ctx, b * 16 + 16)
                for n, w in enumerate((wqT, wkT)):
                    for c in range(2):
                        mm = pe.matmul(bank[n][:, :], w[:, c, :], ctxT[:, c, :], start=c == 0, stop=c == 1)
                    mm.then_inc(qk_ps, 1)
                for e in range(KC):
                    for c in range(2):
                        mm = pe.matmul(bank[2 + e][:, :], inwT[:, c, e * P:(e + 1) * P], ctxT[:, c, :], start=c == 0, stop=c == 1)
                    mm.then_inc(in_ps, 1)
                pe.wait_ge(xn_done, b * 4 + 4)
                for k in range(KC):
                    if k == 2:
                        pe.wait_ge(qk_sb, b * 2 + 2)
                    for t in range(LT):
                        mm = pe.transpose(bank[(6 + k) % 8][:, t * P:(t + 1) * P], xn[:, t, k * P:(k + 1) * P], ident[:, :])
                    mm.then_inc(xT_ps, 1)
                for m in range(4):
                    pe.wait_ge(conv_done, b * 4 + m + 1)
                    pe.matmul(bank[2 + m][:, :], qT[:, m * P:(m + 1) * P], kT[:, :], start=True, stop=True).then_inc(e_ps, 1)
                pe.wait_ge(u_done, b * 4 + 4)
                pe.wait_ge(xT_sb, b * 4 + 4)
                for k in range(KC):
                    mm = pe.matmul(bank[6][0:R + 2 * NS, :], xpT[:, k, :], u[:, k, :], start=k == 0, stop=k == KC - 1)
                mm.then_inc(xd_ps, 1)
                pe.wait_ge(xd_sb, b + 1)
                for k in range(KC):
                    pe.matmul(bank[(7, 0, 1, 6)[k]][:, :], dpT[:, k * P:(k + 1) * P], xdbl[0:R, :], start=True, stop=True).then_inc(dt_ps, 1)
                pe.wait_ge(att_done, b * 4 + 4)
                for k in range(KC):
                    for m in range(4):
                        mm = pe.transpose(bank[2 + k][:, m * P:(m + 1) * P], att[:, m, k * P:(k + 1) * P], ident[:, :])
                    mm.then_inc(aT_ps, 1)
                pe.wait_ge(dt_abs, b * 4 + 4)
                pe.wait_ge(dt_pos, b * 4 + 4)
                pe.wait_ge(aT_sb, b * 4 + 4)
                for t in range(LT):
                    for k in range(KC):
                        mm = pe.matmul(bank[(7, 0, 1, 6)[t]][:, :], XT[:, k, t * P:(t + 1) * P], attT[:, k, :], start=k == 0, stop=k == KC - 1)
                    mm.then_inc(o_ps, 1)
                pe.wait_ge(x1_done, b * 4 + 4)

        @block.scalar
        def _(act):
            act.wait_ge(ld_w, 16 * NW)
            act.activation(alog[:, :, :], alog[:, :, :], ACT.Exp).then_inc(negA_exp, 1)
            with act.Fori(0, NB) as b:
                act.wait_ge(ln_var, b + 1)
                act.activation(rstd[:, :], rstd[:, :], ACT.Sqrt).then_inc(ln_root, 1)
                act.wait_ge(qk_ps, b * 2 + 1)
                act.activation(qT[:, :], bank[0][:, :], ACT.Identity, bias=bq[:, 0:1]).then_inc(qk_sb, 1)
                act.wait_ge(qk_ps, b * 2 + 2)
                act.activation(kT[:, :], bank[1][:, :], ACT.Identity, bias=bk[:, 0:1]).then_inc(qk_sb, 1)
                for e in range(KC):
                    act.wait_ge(in_ps, b * 4 + e + 1)
                    act.activation(conv[:, e, :], bank[2 + e][:, :], ACT.Copy, scale=convw[:, e, TAPS - 1:TAPS]).then_inc(conv_seed, 1)
                for k in range(2):
                    act.wait_ge(xT_ps, b * 4 + k + 1)
                    act.activation(XT[:, k, :], bank[6 + k][:, :], ACT.Copy).then_inc(xT_sb, 1)
                act.wait_ge(dtu_done, b)
                act.wait_ge(du_done, b)
                for e in range(KC):
                    act.wait_ge(conv_done, b * 4 + e + 1)
                    act.activation(u[:, e, :], conv[:, e, :], ACT.Silu, bias=convb[:, e:e + 1]).then_inc(u_done, 1)
                for k in range(2, 4):
                    act.wait_ge(xT_ps, b * 4 + k + 1)
                    act.activation(XT[:, k, :], bank[k - 2][:, :], ACT.Copy).then_inc(xT_sb, 1)
                act.wait_ge(xd_ps, b + 1)
                act.wait_ge(stored, b * 64)
                act.activation(xdbl[:, :], bank[6][0:R + 2 * NS, :], ACT.Copy).then_inc(xd_sb, 1)
                for m in range(4):
                    act.wait_ge(row_max, b * 4 + m + 1)
                    act.activation(att[:, m, :], bank[2 + m][:, :], ACT.Exp, bias=nmax[:, m:m + 1], accum_out=rsum[:, m:m + 1]).then_inc(att_exp, 1)
                for k in range(KC):
                    act.wait_ge(dt_ps, b * 4 + k + 1)
                    act.activation(ex[:, k, :], bank[(7, 0, 1, 6)[k]][:, :], ACT.Abs, bias=dpb[:, k:k + 1]).then_inc(dt_abs, 1)
                act.wait_ge(dt_abs, b * 4 + 4)
                act.activation(ex[:, :, :], ex[:, :, :], ACT.Exp, scale=-1.0).then_inc(sp_exp, 1)
                for k in range(2):
                    act.wait_ge(aT_ps, b * 4 + k + 1)
                    act.activation(attT[:, k, :], bank[2 + k][:, :], ACT.Copy).then_inc(aT_sb, 1)
                act.wait_ge(sp_one, b + 1)
                act.activation(ln[:, :, :], one[:, :, :], ACT.Ln).then_inc(sp_ln, 1)

        @block.vector
        def _(v):
            v.wait_ge(negA_exp, 1)
            v.tensor_scalar(negA[:, :, :], alog[:, :, :], -1.0, None, ALU.mult).then_inc(negA_done, 1)
            v.wait_ge(ld_x, 16 * NB)
            with v.Fori(0, NB) as b:
                for t in range(LT):
                    i = v.bn_stats(st[:, t, :], X[:, ds(b * LT + t, 1), :])
                i.then_inc(ln_step, 1)
                v.wait_ge(ln_step, b * 3 + 1)
                v.sem_inc(passed)
                for t in range(LT):
                    i = v.bn_aggr(mv[:, t, :], st[:, t, :])
                i.then_inc(ln_step, 1)
                v.wait_ge(ln_step, b * 3 + 2)
                v.tensor_scalar(rstd[:, :], mv[:, :, 1], EPS, None, ALU.add).then_inc(ln_var, 1)
                v.wait_ge(ln_root, b + 1)
                v.reciprocal(rstd[:, :], rstd[:, :]).then_inc(ln_step, 1)
                v.wait_ge(ln_step, b * 3 + 3)
                for t in range(LT):
                    v.tensor_scalar(xn[:, t, :], X[:, ds(b * LT + t, 1), :].rearrange("p o n -> p (o n)"), mv[:, t, 0:1], rstd[:, t:t + 1],
                                    ALU.subtract, ALU.mult).then_inc(xn_done, 1)
                for e in range(KC):
                    v.wait_ge(conv_seed, b * 4 + e + 1)
                    for j in range(1, TAPS):
                        i = v.scalar_tensor_tensor(out=conv[:, e, j:], in0=bank[2 + e][:, 0:L - j],
                                                   scalar=convw[:, e, TAPS - 1 - j:TAPS - j], in1=conv[:, e, j:],
                                                   op0=ALU.mult, op1=ALU.add)
                        if j < TAPS - 1:
                            i.then_inc(conv_step, 1)
                            v.wait_ge(conv_step, b * 8 + e * 2 + j)
                        else:
                            i.then_inc(conv_done, 1)
                for m in range(4):
                    v.wait_ge(e_ps, b * 4 + m + 1)
                    v.tensor_reduce(nmax[:, m:m + 1], bank[2 + m][:, :], AX, ALU.max, negate=True).then_inc(row_max, 1)
                v.wait_ge(stored, b * 64)
                v.wait_ge(u_done, b * 4 + 4)
                for k in range(KC):
                    i = v.tensor_scalar(du[:, k, :], u[:, k, :], Dp[:, k:k + 1], None, ALU.mult)
                i.then_inc(du_done, 1)
                v.wait_ge(att_exp, b * 4 + 4)
                v.reciprocal(rinv[:, :], rsum[:, :]).then_inc(att_inv, 1)
                v.wait_ge(att_inv, b + 1)
                for m in range(4):
                    v.tensor_scalar(att[:, m, :], att[:, m, :], rinv[:, m:m + 1], None, ALU.mult).then_inc(att_done, 1)
                for k in range(KC):
                    v.wait_ge(dt_abs, b * 4 + k + 1)
                    v.tensor_scalar(pos[:, k, :], bank[(7, 0, 1, 6)[k]][:, :], dpb[:, k:k + 1], 0.0, ALU.add, ALU.max).then_inc(dt_pos, 1)
                for k in range(2, 4):
                    v.wait_ge(aT_ps, b * 4 + k + 1)
                    v.tensor_copy(attT[:, k, :], bank[2 + k][:, :]).then_inc(aT_sb, 1)
                v.wait_ge(sp_one, b + 1)
                v.wait_ge(dt_pos, b * 4 + 4)
                v.scalar_tensor_tensor(out=ex[:, :, :], in0=one[:, :, :], scalar=-1.0, in1=ex[:, :, :], op0=ALU.add, op1=ALU.subtract).then_inc(sp_fix, 1)
                v.wait_ge(sp_fix, b + 1)
                v.tensor_tensor(pos[:, :, :], pos[:, :, :], ex[:, :, :], ALU.subtract).then_inc(sp_sum, 1)
                v.wait_ge(sp_sum, b + 1)
                v.wait_ge(sp_ln, b + 1)
                v.tensor_tensor(dtv[:, :, :], pos[:, :, :], ln[:, :, :], ALU.add).then_inc(dt_done, 1)
                for t in range(LT):
                    v.wait_ge(o_ps, b * 4 + t + 1)
                    v.tensor_tensor(X[:, ds(b * LT + t, 1), :].rearrange("p o n -> p (o n)"), bank[(7, 0, 1, 6)[t]][:, :],
                                    X[:, ds(b * LT + t, 1), :].rearrange("p o n -> p (o n)"), ALU.add).then_inc(x1_done, 1)

        @block.gpsimd
        def _(g):
            with g.Fori(0, NB) as b:
                g.wait_ge(sp_ln, b)
                g.wait_ge(sp_fix, b)
                g.wait_ge(sp_exp, b + 1)
                g.sem_inc(passed)
                g.tensor_scalar(one[:, :, :], ex[:, :, :], 1.0, None, ALU.add).then_inc(sp_one, 1)
                g.wait_ge(dt_done, b + 1)
                g.wait_ge(u_done, b * 4 + 4)
                g.wait_ge(stored, b * 64)
                g.tensor_tensor(dtu[:, :, :], dtv[:, :, :], u[:, :, :], ALU.mult).then_inc(dtu_done, 1)


def ln_statistics(v, X, st, mv, rstd, stats, root, n):
    for t in range(NT):
        i = v.bn_stats(st[:, t, :], X[:, t, :])
    i.then_inc(stats, 1)
    v.wait_ge(stats, 4 * n + 1)
    for t in range(NT):
        i = v.bn_aggr(mv[:, t, :], st[:, t, :])
    i.then_inc(stats, 1)
    v.wait_ge(stats, 4 * n + 2)
    v.tensor_scalar(rstd[:, :], mv[:, :, 1], EPS, None, ALU.add).then_inc(stats, 1)
    v.wait_ge(root, n + 1)
    v.reciprocal(rstd[:, :], rstd[:, :]).then_inc(stats, 1)
    v.wait_ge(stats, 4 * n + 4)


def ln_root(act, rstd, stats, root, n):
    act.wait_ge(stats, 4 * n + 3)
    act.activation(rstd[:, :], rstd[:, :], ACT.Sqrt).then_inc(root, 1)


def ln_tile(v, X, t, mv, rstd, out):
    mean, scale = (c.rearrange("p o -> p o") for c in (mv[:, ds(t, 1), 0], rstd[:, ds(t, 1)]))
    return v.tensor_scalar(out, X[:, ds(t, 1), :].rearrange("p o n -> p (o n)"), mean, scale, ALU.subtract, ALU.mult)


def block_b0(nc, a, X, ident, bank, hT, Rt, powers):
    with ExitStack() as s:
        sb, sem = mem(nc, s, "B0")
        table = sb("table", [P, IPAD])
        st, mv, rstd, xn = sb("st", [P, NT, 6]), sb("mv", [P, NT, 2]), sb("rstd", [P, NT]), sb("xn", [P, 2, D])
        stats, root = sem("stats"), sem("root")
        ld, ln_step, xn_done, tr, hT_done, r_done = (sem(n) for n in ("ld", "ln_step", "xn_done", "tr", "hT_done", "r_done"))
        block = s.enter_context(nc.Block())

        @block.sync
        def _(sp):
            sp.dma_start(table[:, :], a["table"]).then_inc(ld, 16)
            sp.dma_start(powers[:, :, :, :], a["powers"]).then_inc(ld, 16)
            for n, name in enumerate(("gate", "up", "down")):
                for q in range(4):
                    sp.dma_start(Rt[n][q:P:4, :], a["taps_" + name]).then_inc(ld, 16)

        @block.gpsimd
        def _(g):
            g.wait_ge(ld, 16 * 14)
            for n in range(3):
                g.tensor_tensor(Rt[n][:, :], Rt[n][:, :], table[:, :], ALU.mult).then_inc(r_done, 1)
            g.wait_ge(r_done, 3)

        @block.vector
        def _(v):
            ln_statistics(v, X, st, mv, rstd, stats, root, 0)
            with v.Fori(0, NT // 2) as pair:
                for j in range(2):
                    v.wait_ge(tr, pair * 2)
                    ln_tile(v, X, pair * 2 + j, mv, rstd, xn[:, j, :]).then_inc(xn_done, 1)

        @block.tensor
        def _(pe):
            with pe.Fori(0, NT // 2) as pair:
                for j in range(2):
                    pe.wait_ge(xn_done, pair * 2 + j + 1)
                    pe.wait_ge(hT_done, pair * 2)
                    for k in range(KC):
                        mm = pe.transpose(bank[j][:, k * P:(k + 1) * P], xn[:, j, k * P:(k + 1) * P], ident[:, :])
                    mm.then_inc(tr, 1)

        @block.scalar
        def _(act):
            ln_root(act, rstd, stats, root, 0)
            with act.Fori(0, NT // 2) as pair:
                for j in range(2):
                    act.wait_ge(tr, pair * 2 + j + 1)
                    act.activation(hT[:, :, ds((pair * 2 + j) * P, P)], bank[j][:, :].rearrange("p (k l) -> p k l", k=KC), ACT.Copy).then_inc(hT_done, 1)


def block_b(nc, a, X, negA, bank, hT, Rt, powers, dt_d, dtu_d, du_d, bc_d, y_d):
    with ExitStack() as s:
        sb, sem = mem(nc, s, "B")
        G, U = [bank[0], bank[2]], [bank[1], bank[3]]
        Yb, WA, WB = [bank[4], bank[5]], bank[6], bank[7]
        Wg, Wu = [sb(f"Wg{i}", [P, KC, GW]) for i in range(2)], [sb(f"Wu{i}", [P, KC, GW]) for i in range(2)]
        Wd = [sb(f"Wd{i}", [P, 2, D]) for i in range(2)]
        words = [sb(f"masks{i}", [P, GW + D // 2], I32) for i in range(2)]
        msk = [w[:, :].bitcast(U8) for w in words]
        sil = [sb(f"sil{i}", [P, L]) for i in range(2)]
        inter = [sb(f"inter{i}", [P, 2, L]) for i in range(2)]
        dtv, dtu, yac = sb("dtv", [P, KC, L]), sb("dtu", [P, KC, L]), sb("yac", [P, KC, L])
        Bb, Cb = [sb(f"Bb{i}", [P, 2, L]) for i in range(2)], [sb(f"Cb{i}", [P, 2, L]) for i in range(2)]
        NR, NQ = 3, 2
        dA, dBu, S = (sb(n, [P, NR, L]) for n in ("dA", "dBu", "S"))
        prod = sb("prod", [P, NQ, L])

        ld_dt, ld_yac = sem("ld_dt"), sem("ld_yac")
        ld_bc, ld_msk = [sem(f"ld_bc{i}") for i in range(2)], [sem(f"ld_msk{i}") for i in range(2)]
        g_ps, u_ps, sil_done, inter_done, y_ps, add_done = (sem(n) for n in ("g_ps", "u_ps", "sil_done", "inter_done", "y_ps", "add_done"))
        passed = sem("passed")
        w_ps, w_first, w_done = sem("w_ps"), sem("w_first"), sem("w_done")
        dA_done, dBu_done, s_done, prod_done, yac_done, stored = (sem(n) for n in ("dA_done", "dBu_done", "s_done", "prod_done", "yac_done", "stored"))
        block = s.enter_context(nc.Block())
        NU = 6
        IT = 8 * 8

        def w_unit(unit, buf):
            if unit < 4:
                w = (Wg, Wu)[unit // 2][buf]
                return w[:, 2 * (unit % 2):2 * (unit % 2) + 2, :].rearrange("p c i -> p (c i)")
            return Wd[buf][:, unit - 4, :]

        def unit_order():
            return {(4 * h + 1 + unit // 2, unit % 2): (1 - h, unit) for h in range(2) for unit in range(NU)}

        UNITS = unit_order()
        COUNT = {k: n for n, k in enumerate(sorted(UNITS))}

        @block.sync
        def _(sp):
            sp.dma_start(words[0][:, :], a["masks"][0]).then_inc(ld_msk[0], 16)
            with sp.Fori(0, NB) as b:
                sp.wait_ge(s_done, b * IT)
                sp.dma_start(dtv[:, :, :], dt_d[ds(b, 1)].rearrange("o k p l -> p (o k) l")).then_inc(ld_dt, 16)
                sp.dma_start(dtu[:, :, :], dtu_d[ds(b, 1)].rearrange("o k p l -> p (o k) l")).then_inc(ld_dt, 16)
                for j in range(8):
                    if j >= 2:
                        sp.wait_ge(prod_done, b * IT + 8 * (j - 1))
                    else:
                        sp.wait_ge(prod_done, b * IT)
                    for m, t in ((0, Bb), (NS, Cb)):
                        src = bc_d[ds(b, 1), m + 2 * j:m + 2 * j + 2, :].rearrange("o n l -> o (n l)").broadcast_to([P, 2 * L])
                        sp.dma_start(t[j % 2][:, :, :].rearrange("p n l -> p (n l)"), src).then_inc(ld_bc[j % 2], 16)
                    if j == 0:
                        sp.wait_ge(stored, b * 16)
                        sp.dma_start(yac[:, :, :], du_d[ds(b, 1)].rearrange("o k p l -> p (o k) l")).then_inc(ld_yac, 16)
                        sp.wait_ge(w_done, b * 2 * NU + NU)
                        sp.dma_start(words[1][:, :], a["masks"][ds(b * 2 + 1, 1)].rearrange("o p n -> (o p) n")).then_inc(ld_msk[1], 16)
                    if j == 4:
                        sp.dma_start(words[0][:, :], a["masks"][ds(b * 2 + 2, 1)].rearrange("o p n -> (o p) n")).then_inc(ld_msk[0], 16)
                sp.wait_ge(yac_done, b * IT + IT)
                sp.dma_start(y_d[ds(b, 1)].rearrange("o k p l -> p (o k) l"), yac[:, :, :]).then_inc(stored, 16)
            sp.wait_ge(stored, NB * 16)

        def pe_unit(pe, unit, buf, b, done):
            pe.wait_ge(w_done, done)
            col = b * L + buf * GW if buf else b * L
            for ab, ps in enumerate((WA, WB)):
                if unit < 4:
                    for c in range(2):
                        cc = 2 * (unit % 2) + c
                        mm = pe.matmul(ps[:, c * GW:(c + 1) * GW], powers[:, cc, ab, :], Rt[unit // 2][:, ds(col, GW)], start=True, stop=True)
                else:
                    mm = pe.matmul(ps[:, :], powers[:, 2 * buf + unit - 4, ab, :], Rt[2][:, ds(b, D, 4)], start=True, stop=True)
            mm.then_inc(w_ps, 1)

        def act_unit(act, unit, buf, n):
            act.wait_ge(w_ps, n + 1)
            act.activation(w_unit(unit, buf), WA[:, :], ACT.Copy).then_inc(w_first, 1)

        def dve_unit(v, unit, buf, n, masks):
            v.wait_ge(ld_msk[buf], masks)
            v.wait_ge(w_first, n + 1)
            v.sem_inc(passed)
            m = msk[buf][:, (unit % 2) * 2 * GW:(unit % 2 + 1) * 2 * GW] if unit < 4 else msk[buf][:, 4 * GW + (unit - 4) * D:4 * GW + (unit - 3) * D]
            v.copy_predicated(w_unit(unit, buf), m, WB[:, :]).then_inc(w_done, 1)

        @block.tensor
        def _(pe):
            for unit in range(NU):
                pe_unit(pe, unit, 0, 0, unit)
            with pe.Fori(0, NB) as b:
                def w_slot(j, pos):
                    if (j, pos) in UNITS:
                        buf, unit = UNITS[(j, pos)]
                        n = NU + COUNT[(j, pos)]
                        pe_unit(pe, unit, buf, b if buf else b + 1, b * 2 * NU + n)

                def gate_up(j, ch):
                    q = 2 * j + ch
                    w, tb = j // 4, j % 4
                    pe.wait_ge(inter_done, b * 16 + max(q - 1, 0))
                    for ps, W, done in ((G[ch], Wg[w], g_ps), (U[ch], Wu[w], u_ps)):
                        for k in range(KC):
                            mm = pe.matmul(ps[:, :], W[:, k, ch * P:(ch + 1) * P], hT[:, k, tb * L:(tb + 1) * L], start=k == 0, stop=k == KC - 1)
                        mm.then_inc(done, 1)

                def down(j):
                    w = j // 4
                    pe.wait_ge(inter_done, b * 16 + 2 * j + 2)
                    for t in range(LT):
                        n = 4 * j + t
                        pe.wait_ge(add_done, b * 32 + max(n - 1, 0))
                        for ch in range(2):
                            mm = pe.matmul(Yb[t % 2][:, :], inter[j % 2][:, ch, t * P:(t + 1) * P], Wd[w][:, ch, :], start=ch == 0, stop=ch == 1)
                        mm.then_inc(y_ps, 1)

                for j in range(8):
                    if j % 4 == 0:
                        pe.wait_ge(w_done, b * 2 * NU + NU * (1 + j // 4))
                    w_slot(j, 0)
                    gate_up(j, 0)
                    w_slot(j, 1)
                    if j:
                        down(j - 1)
                    gate_up(j, 1)
                down(7)

        @block.scalar
        def _(act):
            for unit in range(NU):
                act_unit(act, unit, 0, unit)
            with act.Fori(0, NB) as b:
                def silu(j, ch):
                    q = 2 * j + ch
                    act.wait_ge(g_ps, b * 16 + q + 1)
                    act.wait_ge(inter_done, b * 16 + max(q - 1, 0))
                    act.activation(sil[ch][:, :], G[ch][:, :], ACT.Silu).then_inc(sil_done, 1)

                def decay(j, i):
                    n = 8 * j + i
                    act.wait_ge(s_done, b * IT + max(n - NR + 1, 0))
                    act.activation(dA[:, n % NR, :], dtv[:, i % 4, :], ACT.Exp, scale=negA[:, i % 4, 2 * j + i // 4:2 * j + i // 4 + 1]).then_inc(dA_done, 1)

                act.wait_ge(ld_dt, b * 32 + 32)
                for j in range(8):
                    for pos in range(2):
                        if (j, pos) in UNITS:
                            buf, unit = UNITS[(j, pos)]
                            act_unit(act, unit, buf, b * 2 * NU + NU + COUNT[(j, pos)])
                        for i in range(4 * pos, 4 * pos + 4):
                            decay(j, i)
                        silu(j, pos)

        @block.vector
        def _(v):
            for unit in range(NU):
                dve_unit(v, unit, 0, unit, 16)
            with v.Fori(0, NB) as b:
                def mult(j, ch):
                    q = 2 * j + ch
                    v.wait_ge(sil_done, b * 16 + q + 1)
                    v.wait_ge(u_ps, b * 16 + q + 1)
                    if j >= 2:
                        v.wait_ge(y_ps, b * 32 + 4 * (j - 1))
                    else:
                        v.wait_ge(y_ps, b * 32)
                    v.tensor_tensor(inter[j % 2][:, ch, :], U[ch][:, :], sil[ch][:, :], ALU.mult).then_inc(inter_done, 1)

                def add(j, t):
                    v.wait_ge(y_ps, b * 32 + 4 * j + t + 1)
                    x = X[:, (j % 4) * LT + t, :]
                    v.tensor_tensor(x, Yb[t % 2][:, :], x, ALU.add).then_inc(add_done, 1)

                def drive(j, i):
                    n = 8 * j + i
                    if i == 0:
                        v.wait_ge(ld_bc[j % 2], b * 128 + 32 * (j // 2 + 1))
                    v.wait_ge(s_done, b * IT + max(n - NR + 1, 0))
                    v.tensor_tensor(dBu[:, n % NR, :], dtu[:, i % 4, :], Bb[j % 2][:, i // 4, :], ALU.mult).then_inc(dBu_done, 1)

                def scan(n):
                    v.wait_ge(dBu_done, b * IT + n + 1)
                    v.wait_ge(dA_done, b * IT + n + 1)
                    v.wait_ge(prod_done, b * IT + max(n - NR + 1, 0))
                    v.tensor_tensor_scan(S[:, n % NR, :], dA[:, n % NR, :], dBu[:, n % NR, :], 0.0, ALU.mult, ALU.add).then_inc(s_done, 1)

                v.wait_ge(ld_dt, b * 32 + 32)
                for j in range(8):
                    for i in range(8):
                        drive(j, i)
                        if 8 * j + i >= 1:
                            scan(8 * j + i - 1)
                        if i == 0 and j:
                            mult(j - 1, 1)
                        if i == 3:
                            mult(j, 0)
                        if i >= 4 and j:
                            add(j - 1, i - 4)
                        if i in (0, 4) and (j, i // 4) in UNITS:
                            buf, unit = UNITS[(j, i // 4)]
                            dve_unit(v, unit, buf, b * 2 * NU + NU + COUNT[(j, i // 4)], b * 16 + (16 if buf else 32))
                scan(IT - 1)
                mult(7, 1)
                for t in range(LT):
                    add(7, t)

        @block.gpsimd
        def _(g):
            with g.Fori(0, NB) as b:
                def weigh(n):
                    j, i = n // 8, n % 8
                    if i == 0:
                        g.wait_ge(ld_bc[j % 2], b * 128 + 32 * (j // 2 + 1))
                    g.wait_ge(s_done, b * IT + n + 1)
                    g.wait_ge(yac_done, b * IT + max(n - NQ + 1, 0))
                    g.tensor_tensor(prod[:, n % NQ, :], S[:, n % NR, :], Cb[j % 2][:, i // 4, :], ALU.mult).then_inc(prod_done, 1)

                def gather(n):
                    g.wait_ge(prod_done, b * IT + n + 1)
                    g.wait_ge(yac_done, b * IT + max(n - 3, 0))
                    g.tensor_tensor(yac[:, n % 4, :], yac[:, n % 4, :], prod[:, n % NQ, :], ALU.add).then_inc(yac_done, 1)

                for n in range(IT):
                    weigh(n)
                    if n == 1:
                        g.wait_ge(ld_yac, b * 16 + 16)
                    if n:
                        gather(n - 1)
                gather(IT - 1)


def block_c(nc, a, X, ident, bank, meta, y_d, rows_d):
    with ExitStack() as s:
        sb, sem = mem(nc, s, "C")
        st, mv, rstd = sb("st", [P, NT, 6]), sb("mv", [P, NT, 2]), sb("rstd", [P, NT])
        st2, mv2, rstd2 = sb("st2", [P, LT, 6]), sb("mv2", [P, LT, 2]), sb("rstd2", [P, LT])
        y = [sb(f"y{i}", [P, LT, L]) for i in range(2)]
        z, yg = sb("z", [P, LT, D]), sb("yg", [P, LT, L])
        gk, hT = sb("gk", [P, KC, NE]), sb("hT", [P, LT, D])
        row = [sb(f"row{i}", [P, LT, ROW]) for i in range(2)]
        tok = sb("tok", [P, NT], I32)
        before, ones = sb("before", [P, P]), sb("ones", [P, P])
        lg, ex, pr, rest, chosen, place = (sb(n, [P, LT, NE]) for n in ("logit", "expo", "prob", "rest", "chosen", "place"))
        mx, sm, inv, tsum, tinv = (sb(n, [P, LT]) for n in ("mx", "sm", "inv", "tsum", "tinv"))
        top, top_place = sb("top", [P, LT, TOPK]), sb("top_place", [P, LT, TOPK])
        where = [sb(f"where{i}", [P, LT, TOPK], I32) for i in range(2)]
        fill = sb("fill", [P, NE])
        pad = sb("pad", [P, ROW])
        incl, neg_base, tau, tau0 = sb("incl", [NE, NE]), sb("neg_base", [NE, 1]), sb("tau", [NE, NMETA]), sb("tau0", [1, NMETA])
        need_i, need_s, need, ends = sb("need_i", [NE, 1], I32), sb("need_s", [NE, 1], I32), sb("need", [NE, 1]), sb("ends", [NE, 1])
        past = sb("past", [NE, NMETA])
        ev, sc, dd, f0, f1 = (sb(n, [1, NMETA]) for n in ("ev", "sc", "dd", "f0", "f1"))
        i0, i1 = sb("i0", [1, NMETA], I32), sb("i1", [1, NMETA], I32)
        padrow = sb("padrow", [1, NE], I32)

        stats, root, ln_step, ln_var, ln_rooted = sem("stats"), sem("root"), sem("ln_step"), sem("ln_var"), sem("ln_rooted")
        ld_y, ld_c = [sem(f"ld_y{i}") for i in range(2)], sem("ld_c")
        z_in, z_done, g_done, yT_ps, x2_done, h_in, h_ps, h_sb, lg_ps = (sem(n) for n in ("z_in", "z_done", "g_done", "yT_ps", "x2_done", "h_in", "h_ps", "h_sb", "lg_ps"))
        passed = sem("passed")
        r_step, r_in, r_exp, chosen_done, rank_ps, where_done, scattered, fill_done = (
            sem(n) for n in ("r_step", "r_in", "r_exp", "chosen_done", "rank_ps", "where_done", "scattered", "fill_done"))
        fT_ps, need_done, ends_ps, past_done, meta_ps, m_step, padrow_done, stored = (
            sem(n) for n in ("fT_ps", "need_done", "ends_ps", "past_done", "meta_ps", "m_step", "padrow_done", "stored"))
        block = s.enter_context(nc.Block())
        RS = 15
        out = a["out"]
        consts = ((gk[:, :, :], "gk"), (tok[:, :], "tok"), (before[:, :], "before"), (ones[:, :], "ones"), (fill[:, :], "fill"),
                  (pad[:, 0:ROW - 1], "pad"), (pad[:, ROW - 1:ROW].bitcast(I32), "pad_tok"), (incl[:, :], "incl"),
                  (neg_base[:, :], "neg_base"), (tau[:, :], "tau"), (tau0[:, :], "tau0"))

        @block.sync
        def _(sp):
            for b in range(2):
                sp.dma_start(y[b][:, :, :], y_d[b].rearrange("k p l -> p k l")).then_inc(ld_y[b], 16)
            for dst, name in consts:
                sp.dma_start(dst, a[name]).then_inc(ld_c, 16)
            sp.wait_ge(ld_c, 16 * len(consts))
            sp.dma_start(rows_d[NE * REGION:NE * REGION + P, :], pad[:, :]).then_inc(stored, 16)
            sp.dma_start(out[NT * P:NT * P + P, :], pad[:, 0:D]).then_inc(stored, 16)
            for b in range(NB):
                if b + 2 < NB:
                    sp.wait_ge(g_done, b + 1)
                    sp.dma_start(y[b % 2][:, :, :], y_d[b + 2].rearrange("k p l -> p k l")).then_inc(ld_y[b % 2], 16)
                sp.wait_ge(x2_done, 4 * b + 4)
                sp.dma_start(out[b * L:(b + 1) * L, :].rearrange("(t p) n -> p t n", p=P), X[:, b * LT:(b + 1) * LT, :]).then_inc(stored, 16)
            sp.wait_ge(padrow_done, 1)
            for e in range(NE):
                first = sp.value_load(padrow[0:1, e:e + 1], min_val=e * REGION, max_val=(e + 1) * REGION - P)
                sp.dma_start(rows_d[ds(first, P), :], pad[:, :]).then_inc(stored, 16)
            sp.wait_ge(stored, 16 * (2 + NB + NE))

        @block.gpsimd
        def _(g):
            with g.Fori(0, NB // 2) as pair:
                for h in range(2):
                    g.wait_ge(where_done, pair * 2 + h + 1)
                    g.sem_inc(passed)
                    for t in range(LT):
                        for k in range(TOPK):
                            g.indirect_dma_start(rows_d[:, :], bass.IndirectOffsetOnAxis(ap=where[h][:, t, k:k + 1].bitcast(U32), axis=0),
                                                 row[h][:, t, :], None).then_inc(scattered, 16)
                    g.wait_ge(scattered, (pair * 2 + h + 1) * 16 * LT * TOPK)

        @block.vector
        def _(v):
            ln_statistics(v, X, st, mv, rstd, stats, root, 0)
            v.wait_ge(ld_c, 16 * len(consts))

            def one(t):
                return t[:, :].rearrange("p (t o) -> p t o", o=1).broadcast_to([P, LT, NE])

            def batch(base, h):
                def step(i, n):
                    i.then_inc(r_step, 1)
                    v.wait_ge(r_step, base * RS + n)
                    if n in (4, 5, 13):
                        v.sem_inc(passed)
                for t in range(LT):
                    i = ln_tile(v, X, base * LT + t, mv, rstd, z[:, t, :])
                i.then_inc(z_in, 1)
                v.wait_ge(z_done, base + 1)
                v.wait_ge(ld_y[h], pair * 16 + 16)
                v.tensor_tensor(yg[:, :, :], y[h][:, :, :], z[:, :, :], ALU.mult).then_inc(g_done, 1)
                for t in range(LT):
                    v.wait_ge(yT_ps, base * 4 + t + 1)
                    x = X[:, ds(base * LT + t, 1), :].rearrange("p o n -> p (o n)")
                    v.tensor_tensor(x, bank[t][:, :], x, ALU.add).then_inc(x2_done, 1)
                v.wait_ge(x2_done, base * 4 + 4)
                v.sem_inc(passed)
                for t in range(LT):
                    i = v.bn_stats(st2[:, t, :], X[:, ds(base * LT + t, 1), :])
                i.then_inc(ln_step, 1)
                v.wait_ge(ln_step, base * 3 + 1)
                v.sem_inc(passed)
                for t in range(LT):
                    i = v.bn_aggr(mv2[:, t, :], st2[:, t, :])
                i.then_inc(ln_step, 1)
                v.wait_ge(ln_step, base * 3 + 2)
                v.tensor_scalar(rstd2[:, :], mv2[:, :, 1], EPS, None, ALU.add).then_inc(ln_var, 1)
                v.wait_ge(ln_rooted, base + 1)
                v.reciprocal(rstd2[:, :], rstd2[:, :]).then_inc(ln_step, 1)
                v.wait_ge(ln_step, base * 3 + 3)
                v.wait_ge(scattered, pair * ((1 + h) * 16 * LT * TOPK))
                for t in range(LT):
                    v.tensor_scalar(row[h][:, t, 0:D], X[:, ds(base * LT + t, 1), :].rearrange("p o n -> p (o n)"), mv2[:, t, 0:1],
                                    rstd2[:, t:t + 1], ALU.subtract, ALU.mult).then_inc(h_in, 1)
                v.tensor_copy(row[h][:, :, ROW - 1:ROW].bitcast(I32), tok[:, ds(base * LT, LT)].rearrange("p (t o) -> p t o", o=1))
                v.wait_ge(lg_ps, base + 1)
                logits = bank[0][:, 0:LT * NE].rearrange("p (t e) -> p t e", t=LT)
                step(v.tensor_reduce(mx[:, :], logits, AX, ALU.max), 1)
                v.tensor_tensor(lg[:, :, :], logits, one(mx), ALU.subtract).then_inc(r_in, 1)
                v.wait_ge(r_exp, base + 1)
                step(v.tensor_reduce(sm[:, :], ex[:, :, :], AX, ALU.add), 2)
                step(v.reciprocal(inv[:, :], sm[:, :]), 3)
                step(v.tensor_tensor(pr[:, :, :], ex[:, :, :], one(inv), ALU.mult), 4)
                for t in range(LT):
                    i = v.max(top[:, t, :], pr[:, t, :])
                step(i, 5)
                for t in range(LT):
                    i = v.match_replace(rest[:, t, :], top[:, t, :], pr[:, t, :], -1.0)
                step(i, 6)
                step(v.tensor_scalar(chosen[:, :, :], rest[:, :, :], 0.0, None, ALU.is_lt), 7)
                v.sem_inc(chosen_done)
                step(v.tensor_tensor(rest[:, :, :], chosen[:, :, :], pr[:, :, :], ALU.mult), 8)
                step(v.tensor_reduce(tsum[:, :], rest[:, :, :], AX, ALU.add), 9)
                step(v.reciprocal(tinv[:, :], tsum[:, :]), 10)
                step(v.tensor_tensor(row[h][:, :, D:D + NE], rest[:, :, :], one(tinv), ALU.mult), 11)
                v.wait_ge(rank_ps, base + 1)
                ranks = bank[1][:, 0:LT * NE].rearrange("p (t e) -> p t e", t=LT)
                step(v.tensor_tensor(place[:, :, :], ranks, fill[:, :].rearrange("p (o e) -> p o e", o=1).broadcast_to([P, LT, NE]), ALU.add), 12)
                step(v.tensor_tensor(place[:, :, :], place[:, :, :], chosen[:, :, :], ALU.mult), 13)
                for t in range(LT):
                    i = v.max(top_place[:, t, :], place[:, t, :])
                step(i, 14)
                v.tensor_scalar(where[h][:, :, :], top_place[:, :, :], -1.0, None, ALU.add).then_inc(where_done, 1)
                step(v.tensor_tensor(fill[:, :], bank[2][:, 0:NE], fill[:, :], ALU.add), 15)
                v.sem_inc(fill_done)

            with v.Fori(0, NB // 2) as pair:
                for h in range(2):
                    batch(pair * 2 + h, h)
            v.tensor_scalar(padrow[:, :], fill[0:1, :], -1.0, None, ALU.add).then_inc(padrow_done, 1)
            v.wait_ge(fT_ps, 1)
            n = [0]

            def step(i):
                n[0] += 1
                i.then_inc(m_step, 1)
                v.wait_ge(m_step, n[0])
            step(v.tensor_scalar(need_i[:, :], bank[3][0:NE, 0:1], neg_base[:, 0:1], P - 1.0, ALU.add, ALU.add))
            step(v.tensor_scalar(need_s[:, :], need_i[:, :], 7, None, ALU.logical_shift_right))
            v.tensor_scalar(need[:, :], need_s[:, :], 1.0, None, ALU.max).then_inc(need_done, 1)
            v.wait_ge(ends_ps, 1)
            step(v.tensor_copy(ends[:, :], bank[4][0:NE, 0:1]))
            v.tensor_scalar(past[:, :], tau[:, :], ends[:, 0:1], None, ALU.is_ge).then_inc(past_done, 1)
            v.wait_ge(meta_ps, 1)
            step(v.tensor_copy(ev[:, :], bank[5][0:1, 0:NMETA]))
            step(v.tensor_copy(sc[:, :], bank[6][0:1, 0:NMETA]))
            step(v.tensor_tensor(dd[:, :], tau0[:, :], sc[:, :], ALU.subtract))
            step(v.tensor_scalar(f0[:, :], dd[:, :], float(P), None, ALU.mult))
            step(v.scalar_tensor_tensor(out=f1[:, :], in0=ev[:, :], scalar=float(REGION), in1=f0[:, :], op0=ALU.mult, op1=ALU.add))
            step(v.tensor_scalar(meta[:, BASE, :], f1[:, :], float(NE * REGION), None, ALU.min))
            step(v.tensor_scalar(f0[:, :], ev[:, :], float(NE - 1 - AHEAD), None, ALU.is_le))
            step(v.scalar_tensor_tensor(out=meta[:, NEW, :], in0=dd[:, :], scalar=0.0, in1=f0[:, :], op0=ALU.is_equal, op1=ALU.mult))
            step(v.tensor_scalar(meta[:, SRC, :], ev[:, :], float(AHEAD), float(NE - 1), ALU.add, ALU.min))
            step(v.tensor_scalar(i0[:, :], ev[:, :], float(AHEAD), None, ALU.add))
            step(v.tensor_scalar(meta[:, DST, :], i0[:, :], NW4 - 1, None, ALU.bitwise_and))
            step(v.tensor_copy(i1[:, :], ev[:, :]))
            step(v.tensor_scalar(meta[:, CUR, :], i1[:, :], NW4 - 1, None, ALU.bitwise_and))
            step(v.tensor_scalar(meta[:, COL, :], ev[:, :], float(NE - 1), None, ALU.min))
            step(v.tensor_scalar(f0[:, :], ev[:, :], float(NE - 1), 1.0, ALU.min, ALU.add))
            step(v.tensor_scalar(meta[:, WLD, :], f0[:, :], 32.0, None, ALU.mult))
            step(v.tensor_scalar(i0[:, :], sc[:, :], 3.0, None, ALU.add))
            step(v.tensor_scalar(i1[:, :], i0[:, :], 2, 4, ALU.logical_shift_right, ALU.logical_shift_left))
            step(v.tensor_scalar(meta[:, RLD, :], i1[:, :], 16.0, None, ALU.add))
            step(v.tensor_scalar(meta[:, GO, :], ev[:, :], float(NE), None, ALU.is_lt))

        @block.scalar
        def _(act):
            ln_root(act, rstd, stats, root, 0)
            with act.Fori(0, NB) as b:
                act.wait_ge(z_in, b + 1)
                act.activation(z[:, :, :], z[:, :, :], ACT.Silu).then_inc(z_done, 1)
                act.wait_ge(ln_var, b + 1)
                act.activation(rstd2[:, :], rstd2[:, :], ACT.Sqrt).then_inc(ln_rooted, 1)
                for t in range(LT):
                    act.wait_ge(h_ps, b * 4 + t + 1)
                    act.activation(hT[:, t, :], bank[4 + t][:, :], ACT.Copy).then_inc(h_sb, 1)
                act.wait_ge(r_in, b + 1)
                act.activation(ex[:, :, :], lg[:, :, :], ACT.Exp).then_inc(r_exp, 1)

        @block.tensor
        def _(pe):
            pe.wait_ge(ld_c, 16 * len(consts))
            with pe.Fori(0, NB // 2) as pair:
                for h in range(2):
                    b = pair * 2 + h
                    pe.wait_ge(g_done, b + 1)
                    for t in range(LT):
                        for k in range(KC):
                            mm = pe.transpose(bank[t][:, k * P:(k + 1) * P], yg[:, k, t * P:(t + 1) * P], ident[:, :])
                        mm.then_inc(yT_ps, 1)
                    for t in range(LT):
                        pe.wait_ge(h_in, b * 4 + t + 1)
                        for k in range(KC):
                            mm = pe.transpose(bank[4 + t][:, k * P:(k + 1) * P], row[h][:, t, k * P:(k + 1) * P], ident[:, :])
                        mm.then_inc(h_ps, 1)
                    for t in range(LT):
                        pe.wait_ge(h_sb, b * 4 + t + 1)
                        for k in range(KC):
                            mm = pe.matmul(bank[0][:, t * NE:(t + 1) * NE], hT[:, t, k * P:(k + 1) * P], gk[:, k, :], start=k == 0, stop=k == KC - 1)
                    mm.then_inc(lg_ps, 1)
                    pe.wait_ge(chosen_done, b + 1)
                    for t in range(LT):
                        for q in range(t):
                            pe.matmul(bank[1][:, t * NE:(t + 1) * NE], ones[:, :], chosen[:, q, :], start=q == 0, stop=False)
                        pe.matmul(bank[1][:, t * NE:(t + 1) * NE], before[:, :], chosen[:, t, :], start=t == 0, stop=True)
                    for t in range(LT):
                        mm = pe.matmul(bank[2][:, 0:NE], ones[:, :], chosen[:, t, :], start=t == 0, stop=t == LT - 1)
                    mm.then_inc(rank_ps, 1)
                    pe.wait_ge(fill_done, b + 1)
            pe.transpose(bank[3][0:NE, 0:P], fill[:, :], ident[:, :]).then_inc(fT_ps, 1)
            pe.wait_ge(need_done, 1)
            pe.matmul(bank[4][0:NE, 0:1], incl[:, :], need[:, :], start=True, stop=True).then_inc(ends_ps, 1)
            pe.wait_ge(past_done, 1)
            pe.matmul(bank[5][0:1, 0:NMETA], ones[0:NE, 0:1], past[:, :], start=True, stop=True)
            pe.matmul(bank[6][0:1, 0:NMETA], need[:, :], past[:, :], start=True, stop=True).then_inc(meta_ps, 1)


def block_d(nc, a, ident, bank, meta, rows_d):
    with ExitStack() as s:
        sb, sem = mem(nc, s, "D")
        GUW, MH = 2 * M, M // 2
        wgu, wd = sb("wgu", [P, NW4, KC * GUW]), sb("wd", [MH, NW4, 2 * D])
        rows = [sb(f"rows{i}", [P, ROW]) for i in range(4)]
        xT = [sb(f"xT{i}", [P, KC * P]) for i in range(2)]
        sil, inner = [sb(f"sil{i}", [P, M]) for i in range(2)], [sb(f"inner{i}", [P, M]) for i in range(2)]
        iT = [sb(f"iT{i}", [MH, 2 * P]) for i in range(2)]
        ysb = [sb(f"y{i}", [P, D]) for i in range(4)]
        pT, piT, pgu, py = bank[0], bank[1], [bank[2], bank[3]], [bank[4], bank[5]]
        ld_rows, ld_w, ld_w0 = [sem(f"ld_rows{i}") for i in range(4)], sem("ld_w"), sem("ld_first_w")
        passed = sem("passed")
        xT_ps, xT_sb, gu_ps, sil_done, inner_done, iT_ps, iT_sb, y_ps, y_sb, added = (
            sem(n) for n in ("xT_ps", "xT_sb", "gu_ps", "sil_done", "inner_done", "iT_ps", "iT_sb", "y_ps", "y_sb", "added"))
        block = s.enter_context(nc.Block())

        def field(eng, f, tile, hi):
            return eng.value_load(meta[0:1, f, ds(tile, 1)], min_val=0, max_val=hi)

        @block.sync
        def _(sp):
            def load_rows(tile, i):
                first = field(sp, BASE, tile, NE * REGION)
                sp.dma_start(rows[i][:, :], rows_d[ds(first, P), :]).then_inc(ld_rows[i], 16)

            for e in range(AHEAD):
                sp.dma_start(wgu[:, e, :], a["wgu"][e]).then_inc(ld_w0, 16)
                sp.dma_start(wd[:, e, :], a["wd"][e]).then_inc(ld_w0, 16)
            for i in range(4):
                load_rows(i, i)
            sp.wait_ge(ld_w0, 32 * AHEAD)
            sp.sem_inc(ld_w, 32 * AHEAD)
            with sp.Fori(0, NTILE // 4) as q:
                with sp.If(field(sp, GO, q * 4, 1) > 0):
                    for i in range(4):
                        with sp.If(field(sp, NEW, q * 4 + i, 1) > 0):
                            src, dst = field(sp, SRC, q * 4 + i, NE - 1), field(sp, DST, q * 4 + i, NW4 - 1)
                            sp.wait_ge(ld_w, src * 32)
                            for W, name in ((wgu, "wgu"), (wd, "wd")):
                                sp.dma_start(W[:, ds(dst, 1), :].rearrange("p o n -> p (o n)"),
                                             a[name][ds(src, 1)].rearrange("o p n -> p (o n)")).then_inc(ld_w, 16)
                        first = field(sp, BASE, q * 4 + i + 4, NE * REGION)
                        sp.wait_ge(added, 16 * (q * 4 + i) + 16)
                        sp.dma_start(rows[i][:, :], rows_d[ds(first, P), :]).then_inc(ld_rows[i], 16)
            all_rows = field(sp, RLD, NMETA - 1, 16 * (NTILE // 4 + 1))
            sp.wait_ge(ld_w, 32 * NE)
            for i in range(4):
                sp.wait_ge(ld_rows[i], all_rows)

        @block.tensor
        def _(pe):
            def turn_rows(n, i):
                pe.wait_ge(ld_rows[i], (n - i) // 4 * 16 + 16 if isinstance(n, int) else n)
                for k in range(KC):
                    mm = pe.transpose(pT[:, k * P:(k + 1) * P], rows[i][:, k * P:(k + 1) * P], ident[:, :])
                mm.then_inc(xT_ps, 1)

            def gate_up(buf, i):
                for k in range(KC):
                    mm = pe.matmul(pgu[i % 2][:, 0:GUW], xT[i % 2][:, k * P:(k + 1) * P],
                                   wgu[:, ds(buf, 1), k * GUW:(k + 1) * GUW].rearrange("p o n -> p (o n)"), start=k == 0, stop=k == KC - 1)
                mm.then_inc(gu_ps, 1)

            turn_rows(0, 0)
            buf = field(pe, CUR, 0, NW4 - 1)
            pe.wait_ge(ld_w0, 32 * AHEAD)
            pe.wait_ge(xT_sb, 1)
            gate_up(buf, 0)
            turn_rows(1, 1)
            with pe.Fori(0, NTILE // 4) as q:
                with pe.If(field(pe, GO, q * 4, 1) > 0):
                    for i in range(4):
                        t = q * 4 + i
                        buf, next_buf = field(pe, CUR, t, NW4 - 1), field(pe, CUR, t + 1, NW4 - 1)
                        next_load = field(pe, WLD, t + 1, 32 * NE)
                        pe.wait_ge(inner_done, t + 1)
                        for c in range(2):
                            mm = pe.transpose(piT[0:MH, c * P:(c + 1) * P], inner[i % 2][:, c * MH:(c + 1) * MH], ident[:, :])
                        mm.then_inc(iT_ps, 1)
                        pe.wait_ge(xT_sb, t + 2)
                        pe.wait_ge(ld_w, next_load)
                        gate_up(next_buf, i + 1)
                        j = (i + 2) % 4
                        pe.wait_ge(ld_rows[j], (q * 16 + 16) if i + 2 < 4 else (q * 16 + 32))
                        for k in range(KC):
                            mm = pe.transpose(pT[:, k * P:(k + 1) * P], rows[j][:, k * P:(k + 1) * P], ident[:, :])
                        mm.then_inc(xT_ps, 1)
                        pe.wait_ge(iT_sb, t + 1)
                        for c in range(2):
                            mm = pe.matmul(py[i % 2][:, :], iT[i % 2][:, c * P:(c + 1) * P],
                                           wd[:, ds(buf, 1), c * D:(c + 1) * D].rearrange("p o n -> p (o n)"), start=c == 0, stop=c == 1)
                        mm.then_inc(y_ps, 1)

        @block.scalar
        def _(act):
            def turn(n, i):
                act.wait_ge(xT_ps, n + 1)
                act.activation(xT[i % 2][:, :], pT[:, :], ACT.Copy).then_inc(xT_sb, 1)

            def silu(n, i):
                act.wait_ge(gu_ps, n + 1)
                act.activation(sil[i % 2][:, :], pgu[i % 2][:, 0:M], ACT.Silu).then_inc(sil_done, 1)

            turn(0, 0)
            silu(0, 0)
            turn(1, 1)
            with act.Fori(0, NTILE // 4) as q:
                with act.If(field(act, GO, q * 4, 1) > 0):
                    for i in range(4):
                        silu(q * 4 + i + 1, i + 1)
                        turn(q * 4 + i + 2, i + 2)

        @block.vector
        def _(v):
            def weigh(tile, i):
                col = field(v, COL, tile, NE - 1)
                v.wait_ge(sil_done, tile + 1)
                v.scalar_tensor_tensor(out=inner[i % 2][:, :], in0=sil[i % 2][:, :], scalar=rows[i % 4][:, ds(col + D, 1)],
                                       in1=pgu[i % 2][:, M:2 * M], op0=ALU.mult, op1=ALU.mult).then_inc(inner_done, 1)

            weigh(0, 0)
            with v.Fori(0, NTILE // 4) as q:
                with v.If(field(v, GO, q * 4, 1) > 0):
                    for i in range(4):
                        t = q * 4 + i
                        v.wait_ge(iT_ps, t + 1)
                        v.tensor_copy(iT[i % 2][:, :], piT[0:MH, 0:2 * P]).then_inc(iT_sb, 1)
                        weigh(t + 1, i + 1)
                        v.wait_ge(y_ps, t + 1)
                        v.tensor_copy(ysb[i][:, :], py[i % 2][:, :]).then_inc(y_sb, 1)

        @block.gpsimd
        def _(g):
            with g.Fori(0, NTILE // 4) as q:
                with g.If(field(g, GO, q * 4, 1) > 0):
                    for i in range(4):
                        g.wait_ge(y_sb, q * 4 + i + 1)
                        g.sem_inc(passed)
                        g.indirect_dma_start(a["out"], bass.IndirectOffsetOnAxis(ap=rows[i][:, ROW - 1:ROW].bitcast(U32), axis=0),
                                             ysb[i][:, :], None, compute_op=ALU.add).then_inc(added, 16)
                        g.wait_ge(added, 16 * (q * 4 + i) + 16)


def kernel(**inputs):
    import concourse.bacc as bacc
    from concourse.bass_utils import run_bass_kernel_spmd as run

    x = {k: np.ascontiguousarray(v) for k, v in inputs.items()}
    table, taps, powers, masks = spline_constants()

    def chunked(w):
        return w.reshape(-1, P, w.shape[-1]).transpose(1, 0, 2)

    def windows(cp):
        return np.where(taps >= 0, cp[np.maximum(taps, 0)], np.float32(0)).reshape(KC * 2 * 4, IPAD)

    gu = np.concatenate([x["L1_ffn_gate_proj"], x["L1_ffn_up_proj"]], 2)
    gu = gu.reshape(NE, KC, P, 2 * M).transpose(0, 2, 1, 3).reshape(NE, P, KC * 2 * M)
    down = x["L1_ffn_down_proj"].reshape(NE, 2, M // 2, D).transpose(0, 2, 1, 3).reshape(NE, M // 2, 2 * D)
    tiles = np.arange(NMETA, dtype=np.float32)
    region = np.arange(NE, dtype=np.float32) * REGION + 1
    arrays = {
        "x": x["x"],
        "ctxT": x["ctx_1024"].transpose(0, 2, 1).reshape(NB, 2, P, L).transpose(0, 2, 1, 3),
        "wqT": chunked(x["L0_xattn_Wq"].T), "wkT": chunked(x["L0_xattn_Wk"].T),
        "bq": x["L0_xattn_bq"].reshape(P, 1), "bk": x["L0_xattn_bk"].reshape(P, 1),
        "inwT": chunked(x["L1_xattn_in_proj_w"].T),
        "convw": x["L1_xattn_conv_w"].reshape(KC, P, TAPS).transpose(1, 0, 2),
        "convb": x["L1_xattn_conv_b"].reshape(KC, P).T,
        "xpT": chunked(x["L1_xattn_x_proj_w"].T), "dpT": x["L1_xattn_dt_proj_w"].T,
        "dpb": x["L1_xattn_dt_proj_b"].reshape(KC, P).T, "Dp": x["L1_xattn_D"].reshape(KC, P).T,
        "alog": chunked(x["L1_xattn_A_log"]),
        "taps_gate": windows(x["L0_ffn_gate_cp"]), "taps_up": windows(x["L0_ffn_up_cp"]),
        "taps_down": windows(x["L0_ffn_down_cp"]),
        "gk": chunked(x["L1_ffn_gate_kernel"]),
        "wgu": gu, "wd": down,
        "tok": np.arange(NB * L, dtype=np.int32).reshape(NT, P).T,
        "before": np.triu(np.ones((P, P), np.float32), 1), "ones": np.ones((P, P), np.float32),
        "fill": np.tile(region, (P, 1)), "neg_base": -region[:, None], "incl": np.triu(np.ones((NE, NE), np.float32)),
        "pad": np.zeros((P, ROW - 1), np.float32), "pad_tok": NB * L + np.arange(P, dtype=np.int32)[:, None],
        "tau": np.tile(tiles, (NE, 1)), "tau0": tiles[None],
        "ident": np.eye(P, dtype=np.float32), "table": table, "powers": powers.reshape(P, KC, 2, P), "masks": masks.view(np.int32),
    }
    nc = bacc.Bacc("TRN2", target_bir_lowering=False, num_devices=1)
    a, sent = {}, {}
    for name, v in arrays.items():
        sent[f"in_{name}"] = np.ascontiguousarray(v)
        a[name] = nc.dram_tensor(f"in_{name}", v.shape, mybir.dt.from_np(v.dtype), kind="ExternalInput").ap()
    a["out"] = nc.dram_tensor("out_x", (NB * L + P, D), F32, kind="ExternalOutput").ap()
    build(nc, a)
    return run(nc, [sent], core_ids=[0]).results[0]["out_x"][:NB * L].reshape(NB, L, D)
```

```python
from contextlib import ExitStack

import numpy as np

import concourse.bass as bass
from concourse import mybir

ds = bass.ds
F32 = mybir.dt.float32
F32R = mybir.dt.float32r
U8, I32, U32 = mybir.dt.uint8, mybir.dt.int32, mybir.dt.uint32
ALU = mybir.AluOpType
ACT = mybir.ActivationFunctionType
AX = mybir.AxisListType.X

P = 128
NB, L, D = 4, 512, 512
DC = 256
KC = D // P
LT = L // P
NT = NB * LT
DK = 128
DI, NS, R, TAPS = 512, 16, 16, 4
INTER = 2048
NE, M, TOPK = 32, 192, 8
EPS = 1e-5
NCTRL = max(16, int(INTER * D / 128.9))
GW = 2 * P
NG = INTER // GW
IPAD = INTER + L
ROW = D + NE + 1
REGION = NB * L + P
UNROLL = 8
NTILE = -(-(NB * L * TOPK // P + NE - 1) // UNROLL) * UNROLL
NMETA = NTILE + UNROLL
NSLOT, NRAW = 4, 2
SPLIT_AHEAD, LOAD_AHEAD = 2, 3
FIELDS = 11
BASE, EXPERT, SLOT, FIRST, LOADS, SPLITS, LOAD_RAW, SPLIT_RAW, SPLIT_SLOT, GO, RLOADS = range(FIELDS)


def spline_constants():
    n = INTER * D
    t = np.linspace(0.0, NCTRL - 1.0, n, dtype=np.float64)
    i = np.clip(np.floor(t).astype(np.int64), 0, NCTRL - 2)
    t0, ia = t[::P], i[::P]
    ib = np.minimum(ia + 1, NCTRL - 2)
    r = (NCTRL - 1.0) / (n - 1)
    cubic = 0.5 * np.array([[0, -1, 2, -1], [2, 0, -5, 3], [0, 1, 4, -3], [0, 0, -1, 1]], np.float64)
    table = np.zeros((KC, 2, 4, 4, IPAD))
    taps = np.full((KC, 2, 4, IPAD), -1, np.int64)
    for ab, ix in enumerate((ia, ib)):
        f = (t0 - ix).reshape(INTER, KC).T
        for j in range(4):
            c0, c1, c2, c3 = cubic[j]
            shifted = [c0 + c1 * f + c2 * f**2 + c3 * f**3, c1 + 2 * c2 * f + 3 * c3 * f**2, c2 + 3 * c3 * f,
                       c3 + 0 * f]
            for p in range(4):
                table[:, ab, j, p, :INTER] = shifted[p]
            taps[:, ab, j, :INTER] = np.clip(ix + j - 1, 0, NCTRL - 1).reshape(INTER, KC).T
    powers = np.zeros((KC, 2, 4, 4, KC, 2, P))
    y = np.arange(P) * r
    for c in range(KC):
        for ab in range(2):
            for p in range(4):
                powers[c, ab, :, p, c, ab, :] = y**p
    second = (i.reshape(-1, P) != ia[:, None]).T.astype(np.uint8)
    by_gate = second.reshape(P, NG, GW, KC).transpose(1, 0, 3, 2).reshape(NG, P, KC * GW)
    by_down = second.reshape(P, D, NG, 2).transpose(2, 0, 3, 1).reshape(NG, P, 2 * D)
    masks = np.zeros((NG + 2, P, KC * GW + 2 * D), np.uint8)
    masks[:NG] = np.concatenate([by_gate, by_down], 2)
    return (table.reshape(P, IPAD).astype(np.float32), taps, powers.reshape(P, KC * 2 * P).astype(np.float32), masks)


def build(nc, a):
    ctx = ExitStack()

    def dram(name, shape):
        return nc.dram_tensor(name, shape, F32).ap()

    dt_d, dtu_d, du_d, y_d = (dram(n, (NB, KC, P, L)) for n in ("dt_d", "dtu_d", "du_d", "y_d"))
    bc_d = dram("bc_d", (NB, 2 * NS, L))
    rows_d = dram("rows_d", (NE * REGION + P, ROW))

    with ctx:
        X = ctx.enter_context(nc.sbuf_tensor("X", [P, NT, D], F32))
        ident = ctx.enter_context(nc.sbuf_tensor("ident", [P, P], F32))
        negA = ctx.enter_context(nc.sbuf_tensor("negA", [P, KC, NS], F32))
        bank = [ctx.enter_context(nc.psum_tensor(f"bank{i}", [P, 512], F32)) for i in range(8)]
        block_a(nc, a, X, ident, negA, bank, dt_d, dtu_d, du_d, bc_d)
        with ExitStack() as s:
            hT = s.enter_context(nc.sbuf_tensor("hT", [P, KC, NB * L], F32))
            Rt = [s.enter_context(nc.sbuf_tensor(f"R{n}", [P, IPAD], F32)) for n in ("gate", "up", "down")]
            powers = s.enter_context(nc.sbuf_tensor("powers", [P, KC, 2, P], F32))
            block_b0(nc, a, X, ident, bank, hT, Rt, powers)
            block_b(nc, a, X, negA, bank, hT, Rt, powers, dt_d, dtu_d, du_d, bc_d, y_d)
        meta = ctx.enter_context(nc.sbuf_tensor("meta", [1, FIELDS, NMETA], I32))
        block_c(nc, a, X, ident, bank, meta, y_d, rows_d)
        block_d(nc, a, ident, bank, meta, rows_d)


def mem(nc, s, block_name):
    def sb(name, shape, dt=F32):
        return s.enter_context(nc.sbuf_tensor(f"{block_name}_{name}", shape, dt))

    def sem(name):
        return s.enter_context(nc.semaphore(f"{block_name}_{name}"))
    return sb, sem


def block_a(nc, a, X, ident, negA, bank, dt_d, dtu_d, du_d, bc_d):
    with ExitStack() as s:
        sb, sem = mem(nc, s, "A")
        ctxT = sb("ctxT", [P, 2, L])
        wqT, wkT = sb("wqT", [P, 2, DK]), sb("wkT", [P, 2, DK])
        bq, bk = sb("bq", [P, 1]), sb("bk", [P, 1])
        inwT = sb("inwT", [P, 2, DI])
        convw, convb = sb("convw", [P, KC, TAPS]), sb("convb", [P, KC])
        xpT = sb("xpT", [P, KC, R + 2 * NS])
        dpT, dpb, Dp = sb("dpT", [R, DI]), sb("dpb", [P, KC]), sb("Dp", [P, KC])
        alog = sb("alog", [P, KC, NS])
        st, mv, rstd = sb("st", [P, 4, 6]), sb("mv", [P, 4, 2]), sb("rstd", [P, 4])
        xn, XT = sb("xn", [P, LT, D]), sb("XT", [P, KC, L])
        att, attT = sb("att", [P, LT, L]), sb("attT", [P, KC, L])
        nmax, rsum, rinv = sb("nmax", [P, 4]), sb("rsum", [P, 4]), sb("rinv", [P, 4])
        qT, kT = sb("qT", [P, L]), sb("kT", [P, L])
        conv, u = sb("conv", [P, KC, L]), sb("u", [P, KC, L])
        xdbl = sb("xdbl", [R + 2 * NS, L])
        pos, ex, one, ln = (sb(n, [P, KC, L]) for n in ("pos", "ex", "one", "ln"))
        dtv, dtu, du = (sb(n, [P, KC, L]) for n in ("dtv", "dtu", "du"))

        ld_x, ld_w, ld_ctx = sem("ld_x"), sem("ld_w"), sem("ld_ctx")
        qk_ps, qk_sb = sem("qk_ps"), sem("qk_sb")
        in_ps, conv_seed, conv_step, conv_done, u_done = (sem(n) for n in ("in_ps", "conv_seed", "conv_step", "conv_done", "u_done"))
        passed = sem("passed")
        ln_var, ln_root = sem("ln_var"), sem("ln_root")
        ln_step, xn_done, xT_ps, xT_sb = sem("ln_step"), sem("xn_done"), sem("xT_ps"), sem("xT_sb")
        e_ps, row_max, att_exp, att_inv, att_done = (sem(n) for n in ("e_ps", "row_max", "att_exp", "att_inv", "att_done"))
        aT_ps, aT_sb, o_ps, x1_done = sem("aT_ps"), sem("aT_sb"), sem("o_ps"), sem("x1_done")
        xd_ps, xd_sb, dt_ps, dt_abs, dt_pos = (sem(n) for n in ("xd_ps", "xd_sb", "dt_ps", "dt_abs", "dt_pos"))
        sp_exp, sp_one, sp_ln, sp_fix, sp_sum, dt_done = (sem(n) for n in ("sp_exp", "sp_one", "sp_ln", "sp_fix", "sp_sum", "dt_done"))
        dtu_done, du_done, stored, negA_exp, negA_done = (sem(n) for n in ("dtu_done", "du_done", "stored", "negA_exp", "negA_done"))
        block = s.enter_context(nc.Block())
        NW = 13

        @block.sync
        def _(sp):
            for dst, name in ((ident[:, :], "ident"), (wqT[:, :, :], "wqT"), (wkT[:, :, :], "wkT"), (bq[:, :], "bq"),
                              (bk[:, :], "bk"), (inwT[:, :, :], "inwT"), (convw[:, :, :], "convw"),
                              (convb[:, :], "convb"), (xpT[:, :, :], "xpT"), (dpT[:, :], "dpT"), (dpb[:, :], "dpb"),
                              (Dp[:, :], "Dp"), (alog[:, :, :], "alog")):
                sp.dma_start(dst, a[name]).then_inc(ld_w, 16)
            for b in range(NB):
                sp.dma_start(X[:, b * LT:(b + 1) * LT, :], a["x"][b].rearrange("(t p) n -> p t n", p=P)).then_inc(ld_x, 16)
            with sp.Fori(0, NB) as b:
                sp.wait_ge(in_ps, b * 4)
                sp.dma_start(ctxT[:, :, :], a["ctxT"][ds(b, 1)].rearrange("o p c l -> p (o c) l")).then_inc(ld_ctx, 16)
                for wait, dst, src in ((xd_sb, bc_d[ds(b, 1)].rearrange("o n l -> (o n) l"), xdbl[R:R + 2 * NS, :]),
                                       (dt_done, dt_d[ds(b, 1)].rearrange("o k p l -> p (o k) l"), dtv[:, :, :]),
                                       (du_done, du_d[ds(b, 1)].rearrange("o k p l -> p (o k) l"), du[:, :, :]),
                                       (dtu_done, dtu_d[ds(b, 1)].rearrange("o k p l -> p (o k) l"), dtu[:, :, :])):
                    sp.wait_ge(wait, b + 1)
                    sp.dma_start(dst, src).then_inc(stored, 16)
            sp.wait_ge(stored, NB * 64)

        @block.tensor
        def _(pe):
            pe.wait_ge(ld_w, 16 * NW)
            with pe.Fori(0, NB) as b:
                pe.wait_ge(ld_ctx, b * 16 + 16)
                for n, w in enumerate((wqT, wkT)):
                    for c in range(2):
                        mm = pe.matmul(bank[n][:, :], w[:, c, :], ctxT[:, c, :], start=c == 0, stop=c == 1)
                    mm.then_inc(qk_ps, 1)
                for e in range(KC):
                    for c in range(2):
                        mm = pe.matmul(bank[2 + e][:, :], inwT[:, c, e * P:(e + 1) * P], ctxT[:, c, :], start=c == 0, stop=c == 1)
                    mm.then_inc(in_ps, 1)
                pe.wait_ge(xn_done, b * 4 + 4)
                for k in range(KC):
                    if k == 2:
                        pe.wait_ge(qk_sb, b * 2 + 2)
                    for t in range(LT):
                        mm = pe.transpose(bank[(6 + k) % 8][:, t * P:(t + 1) * P], xn[:, t, k * P:(k + 1) * P], ident[:, :])
                    mm.then_inc(xT_ps, 1)
                for m in range(4):
                    pe.wait_ge(conv_done, b * 4 + m + 1)
                    pe.matmul(bank[2 + m][:, :], qT[:, m * P:(m + 1) * P], kT[:, :], start=True, stop=True).then_inc(e_ps, 1)
                pe.wait_ge(u_done, b * 4 + 4)
                pe.wait_ge(xT_sb, b * 4 + 4)
                for k in range(KC):
                    mm = pe.matmul(bank[6][0:R + 2 * NS, :], xpT[:, k, :], u[:, k, :], start=k == 0, stop=k == KC - 1)
                mm.then_inc(xd_ps, 1)
                pe.wait_ge(xd_sb, b + 1)
                for k in range(KC):
                    pe.matmul(bank[(7, 0, 1, 6)[k]][:, :], dpT[:, k * P:(k + 1) * P], xdbl[0:R, :], start=True, stop=True).then_inc(dt_ps, 1)
                pe.wait_ge(att_done, b * 4 + 4)
                for k in range(KC):
                    for m in range(4):
                        mm = pe.transpose(bank[2 + k][:, m * P:(m + 1) * P], att[:, m, k * P:(k + 1) * P], ident[:, :])
                    mm.then_inc(aT_ps, 1)
                pe.wait_ge(dt_abs, b * 4 + 4)
                pe.wait_ge(dt_pos, b * 4 + 4)
                pe.wait_ge(aT_sb, b * 4 + 4)
                for t in range(LT):
                    for k in range(KC):
                        mm = pe.matmul(bank[(7, 0, 1, 6)[t]][:, :], XT[:, k, t * P:(t + 1) * P], attT[:, k, :], start=k == 0, stop=k == KC - 1)
                    mm.then_inc(o_ps, 1)
                pe.wait_ge(x1_done, b * 4 + 4)

        @block.scalar
        def _(act):
            act.wait_ge(ld_w, 16 * NW)
            act.activation(alog[:, :, :], alog[:, :, :], ACT.Exp).then_inc(negA_exp, 1)
            with act.Fori(0, NB) as b:
                act.wait_ge(ln_var, b + 1)
                act.activation(rstd[:, :], rstd[:, :], ACT.Sqrt).then_inc(ln_root, 1)
                act.wait_ge(qk_ps, b * 2 + 1)
                act.activation(qT[:, :], bank[0][:, :], ACT.Identity, bias=bq[:, 0:1]).then_inc(qk_sb, 1)
                act.wait_ge(qk_ps, b * 2 + 2)
                act.activation(kT[:, :], bank[1][:, :], ACT.Identity, bias=bk[:, 0:1]).then_inc(qk_sb, 1)
                for e in range(KC):
                    act.wait_ge(in_ps, b * 4 + e + 1)
                    act.activation(conv[:, e, :], bank[2 + e][:, :], ACT.Copy, scale=convw[:, e, TAPS - 1:TAPS]).then_inc(conv_seed, 1)
                for k in range(2):
                    act.wait_ge(xT_ps, b * 4 + k + 1)
                    act.activation(XT[:, k, :], bank[6 + k][:, :], ACT.Copy).then_inc(xT_sb, 1)
                act.wait_ge(dtu_done, b)
                act.wait_ge(du_done, b)
                for e in range(KC):
                    act.wait_ge(conv_done, b * 4 + e + 1)
                    act.activation(u[:, e, :], conv[:, e, :], ACT.Silu, bias=convb[:, e:e + 1]).then_inc(u_done, 1)
                for k in range(2, 4):
                    act.wait_ge(xT_ps, b * 4 + k + 1)
                    act.activation(XT[:, k, :], bank[k - 2][:, :], ACT.Copy).then_inc(xT_sb, 1)
                act.wait_ge(xd_ps, b + 1)
                act.wait_ge(stored, b * 64)
                act.activation(xdbl[:, :], bank[6][0:R + 2 * NS, :], ACT.Copy).then_inc(xd_sb, 1)
                for m in range(4):
                    act.wait_ge(row_max, b * 4 + m + 1)
                    act.activation(att[:, m, :], bank[2 + m][:, :], ACT.Exp, bias=nmax[:, m:m + 1], accum_out=rsum[:, m:m + 1]).then_inc(att_exp, 1)
                for k in range(KC):
                    act.wait_ge(dt_ps, b * 4 + k + 1)
                    act.activation(ex[:, k, :], bank[(7, 0, 1, 6)[k]][:, :], ACT.Abs, bias=dpb[:, k:k + 1]).then_inc(dt_abs, 1)
                act.wait_ge(dt_abs, b * 4 + 4)
                act.activation(ex[:, :, :], ex[:, :, :], ACT.Exp, scale=-1.0).then_inc(sp_exp, 1)
                for k in range(2):
                    act.wait_ge(aT_ps, b * 4 + k + 1)
                    act.activation(attT[:, k, :], bank[2 + k][:, :], ACT.Copy).then_inc(aT_sb, 1)
                act.wait_ge(sp_one, b + 1)
                act.activation(ln[:, :, :], one[:, :, :], ACT.Ln).then_inc(sp_ln, 1)

        @block.vector
        def _(v):
            v.wait_ge(negA_exp, 1)
            v.tensor_scalar(negA[:, :, :], alog[:, :, :], -1.0, None, ALU.mult).then_inc(negA_done, 1)
            v.wait_ge(ld_x, 16 * NB)
            with v.Fori(0, NB) as b:
                for t in range(LT):
                    i = v.bn_stats(st[:, t, :], X[:, ds(b * LT + t, 1), :])
                i.then_inc(ln_step, 1)
                v.wait_ge(ln_step, b * 3 + 1)
                v.sem_inc(passed)
                for t in range(LT):
                    i = v.bn_aggr(mv[:, t, :], st[:, t, :])
                i.then_inc(ln_step, 1)
                v.wait_ge(ln_step, b * 3 + 2)
                v.tensor_scalar(rstd[:, :], mv[:, :, 1], EPS, None, ALU.add).then_inc(ln_var, 1)
                v.wait_ge(ln_root, b + 1)
                v.reciprocal(rstd[:, :], rstd[:, :]).then_inc(ln_step, 1)
                v.wait_ge(ln_step, b * 3 + 3)
                for t in range(LT):
                    v.tensor_scalar(xn[:, t, :], X[:, ds(b * LT + t, 1), :].rearrange("p o n -> p (o n)"), mv[:, t, 0:1], rstd[:, t:t + 1],
                                    ALU.subtract, ALU.mult).then_inc(xn_done, 1)
                for e in range(KC):
                    v.wait_ge(conv_seed, b * 4 + e + 1)
                    for j in range(1, TAPS):
                        i = v.scalar_tensor_tensor(out=conv[:, e, j:], in0=bank[2 + e][:, 0:L - j],
                                                   scalar=convw[:, e, TAPS - 1 - j:TAPS - j], in1=conv[:, e, j:],
                                                   op0=ALU.mult, op1=ALU.add)
                        if j < TAPS - 1:
                            i.then_inc(conv_step, 1)
                            v.wait_ge(conv_step, b * 8 + e * 2 + j)
                        else:
                            i.then_inc(conv_done, 1)
                for m in range(4):
                    v.wait_ge(e_ps, b * 4 + m + 1)
                    v.tensor_reduce(nmax[:, m:m + 1], bank[2 + m][:, :], AX, ALU.max, negate=True).then_inc(row_max, 1)
                v.wait_ge(stored, b * 64)
                v.wait_ge(u_done, b * 4 + 4)
                for k in range(KC):
                    i = v.tensor_scalar(du[:, k, :], u[:, k, :], Dp[:, k:k + 1], None, ALU.mult)
                i.then_inc(du_done, 1)
                v.wait_ge(att_exp, b * 4 + 4)
                v.reciprocal(rinv[:, :], rsum[:, :]).then_inc(att_inv, 1)
                v.wait_ge(att_inv, b + 1)
                for m in range(4):
                    v.tensor_scalar(att[:, m, :], att[:, m, :], rinv[:, m:m + 1], None, ALU.mult).then_inc(att_done, 1)
                for k in range(KC):
                    v.wait_ge(dt_abs, b * 4 + k + 1)
                    v.tensor_scalar(pos[:, k, :], bank[(7, 0, 1, 6)[k]][:, :], dpb[:, k:k + 1], 0.0, ALU.add, ALU.max).then_inc(dt_pos, 1)
                for k in range(2, 4):
                    v.wait_ge(aT_ps, b * 4 + k + 1)
                    v.tensor_copy(attT[:, k, :], bank[2 + k][:, :]).then_inc(aT_sb, 1)
                v.wait_ge(sp_one, b + 1)
                v.wait_ge(dt_pos, b * 4 + 4)
                v.scalar_tensor_tensor(out=ex[:, :, :], in0=one[:, :, :], scalar=-1.0, in1=ex[:, :, :], op0=ALU.add, op1=ALU.subtract).then_inc(sp_fix, 1)
                v.wait_ge(sp_fix, b + 1)
                v.tensor_tensor(pos[:, :, :], pos[:, :, :], ex[:, :, :], ALU.subtract).then_inc(sp_sum, 1)
                v.wait_ge(sp_sum, b + 1)
                v.wait_ge(sp_ln, b + 1)
                v.tensor_tensor(dtv[:, :, :], pos[:, :, :], ln[:, :, :], ALU.add).then_inc(dt_done, 1)
                for t in range(LT):
                    v.wait_ge(o_ps, b * 4 + t + 1)
                    v.tensor_tensor(X[:, ds(b * LT + t, 1), :].rearrange("p o n -> p (o n)"), bank[(7, 0, 1, 6)[t]][:, :],
                                    X[:, ds(b * LT + t, 1), :].rearrange("p o n -> p (o n)"), ALU.add).then_inc(x1_done, 1)

        @block.gpsimd
        def _(g):
            with g.Fori(0, NB) as b:
                g.wait_ge(sp_ln, b)
                g.wait_ge(sp_fix, b)
                g.wait_ge(sp_exp, b + 1)
                g.sem_inc(passed)
                g.tensor_scalar(one[:, :, :], ex[:, :, :], 1.0, None, ALU.add).then_inc(sp_one, 1)
                g.wait_ge(dt_done, b + 1)
                g.wait_ge(u_done, b * 4 + 4)
                g.wait_ge(stored, b * 64)
                g.tensor_tensor(dtu[:, :, :], dtv[:, :, :], u[:, :, :], ALU.mult).then_inc(dtu_done, 1)


def ln_statistics(v, X, st, mv, rstd, stats, root, n):
    for t in range(NT):
        i = v.bn_stats(st[:, t, :], X[:, t, :])
    i.then_inc(stats, 1)
    v.wait_ge(stats, 4 * n + 1)
    for t in range(NT):
        i = v.bn_aggr(mv[:, t, :], st[:, t, :])
    i.then_inc(stats, 1)
    v.wait_ge(stats, 4 * n + 2)
    v.tensor_scalar(rstd[:, :], mv[:, :, 1], EPS, None, ALU.add).then_inc(stats, 1)
    v.wait_ge(root, n + 1)
    v.reciprocal(rstd[:, :], rstd[:, :]).then_inc(stats, 1)
    v.wait_ge(stats, 4 * n + 4)


def ln_root(act, rstd, stats, root, n):
    act.wait_ge(stats, 4 * n + 3)
    act.activation(rstd[:, :], rstd[:, :], ACT.Sqrt).then_inc(root, 1)


def ln_tile(v, X, t, mv, rstd, out):
    mean, scale = (c.rearrange("p o -> p o") for c in (mv[:, ds(t, 1), 0], rstd[:, ds(t, 1)]))
    return v.tensor_scalar(out, X[:, ds(t, 1), :].rearrange("p o n -> p (o n)"), mean, scale, ALU.subtract, ALU.mult)


def block_b0(nc, a, X, ident, bank, hT, Rt, powers):
    with ExitStack() as s:
        sb, sem = mem(nc, s, "B0")
        table = sb("table", [P, IPAD])
        st, mv, rstd, xn = sb("st", [P, NT, 6]), sb("mv", [P, NT, 2]), sb("rstd", [P, NT]), sb("xn", [P, 2, D])
        stats, root = sem("stats"), sem("root")
        ld, ln_step, xn_done, tr, hT_done, r_done = (sem(n) for n in ("ld", "ln_step", "xn_done", "tr", "hT_done", "r_done"))
        block = s.enter_context(nc.Block())

        @block.sync
        def _(sp):
            sp.dma_start(table[:, :], a["table"]).then_inc(ld, 16)
            sp.dma_start(powers[:, :, :, :], a["powers"]).then_inc(ld, 16)
            for n, name in enumerate(("gate", "up", "down")):
                for q in range(4):
                    sp.dma_start(Rt[n][q:P:4, :], a["taps_" + name]).then_inc(ld, 16)

        @block.gpsimd
        def _(g):
            g.wait_ge(ld, 16 * 14)
            for n in range(3):
                g.tensor_tensor(Rt[n][:, :], Rt[n][:, :], table[:, :], ALU.mult).then_inc(r_done, 1)
            g.wait_ge(r_done, 3)

        @block.vector
        def _(v):
            ln_statistics(v, X, st, mv, rstd, stats, root, 0)
            with v.Fori(0, NT // 2) as pair:
                for j in range(2):
                    v.wait_ge(tr, pair * 2)
                    ln_tile(v, X, pair * 2 + j, mv, rstd, xn[:, j, :]).then_inc(xn_done, 1)

        @block.tensor
        def _(pe):
            with pe.Fori(0, NT // 2) as pair:
                for j in range(2):
                    pe.wait_ge(xn_done, pair * 2 + j + 1)
                    pe.wait_ge(hT_done, pair * 2)
                    for k in range(KC):
                        mm = pe.transpose(bank[j][:, k * P:(k + 1) * P], xn[:, j, k * P:(k + 1) * P], ident[:, :])
                    mm.then_inc(tr, 1)

        @block.scalar
        def _(act):
            ln_root(act, rstd, stats, root, 0)
            with act.Fori(0, NT // 2) as pair:
                for j in range(2):
                    act.wait_ge(tr, pair * 2 + j + 1)
                    act.activation(hT[:, :, ds((pair * 2 + j) * P, P)], bank[j][:, :].rearrange("p (k l) -> p k l", k=KC), ACT.Copy).then_inc(hT_done, 1)


def block_b(nc, a, X, negA, bank, hT, Rt, powers, dt_d, dtu_d, du_d, bc_d, y_d):
    with ExitStack() as s:
        sb, sem = mem(nc, s, "B")
        G, U = [bank[0], bank[2]], [bank[1], bank[3]]
        Yb, WA, WB = [bank[4], bank[5]], bank[6], bank[7]
        Wg, Wu = [sb(f"Wg{i}", [P, KC, GW]) for i in range(2)], [sb(f"Wu{i}", [P, KC, GW]) for i in range(2)]
        Wd = [sb(f"Wd{i}", [P, 2, D]) for i in range(2)]
        words = [sb(f"masks{i}", [P, GW + D // 2], I32) for i in range(2)]
        msk = [w[:, :].bitcast(U8) for w in words]
        sil = [sb(f"sil{i}", [P, L]) for i in range(2)]
        inter = [sb(f"inter{i}", [P, 2, L]) for i in range(2)]
        dtv, dtu, yac = sb("dtv", [P, KC, L]), sb("dtu", [P, KC, L]), sb("yac", [P, KC, L])
        Bb, Cb = [sb(f"Bb{i}", [P, 2, L]) for i in range(2)], [sb(f"Cb{i}", [P, 2, L]) for i in range(2)]
        NR, NQ = 3, 2
        dA, dBu, S = (sb(n, [P, NR, L]) for n in ("dA", "dBu", "S"))
        prod = sb("prod", [P, NQ, L])

        ld_dt, ld_yac = sem("ld_dt"), sem("ld_yac")
        ld_bc, ld_msk = [sem(f"ld_bc{i}") for i in range(2)], [sem(f"ld_msk{i}") for i in range(2)]
        g_ps, u_ps, sil_done, inter_done, y_ps, add_done = (sem(n) for n in ("g_ps", "u_ps", "sil_done", "inter_done", "y_ps", "add_done"))
        passed = sem("passed")
        w_ps, w_first, w_done = sem("w_ps"), sem("w_first"), sem("w_done")
        dA_done, dBu_done, s_done, prod_done, yac_done, stored = (sem(n) for n in ("dA_done", "dBu_done", "s_done", "prod_done", "yac_done", "stored"))
        block = s.enter_context(nc.Block())
        NU = 6
        IT = 8 * 8

        def w_unit(unit, buf):
            if unit < 4:
                w = (Wg, Wu)[unit // 2][buf]
                return w[:, 2 * (unit % 2):2 * (unit % 2) + 2, :].rearrange("p c i -> p (c i)")
            return Wd[buf][:, unit - 4, :]

        def unit_order():
            return {(4 * h + 1 + unit // 2, unit % 2): (1 - h, unit) for h in range(2) for unit in range(NU)}

        UNITS = unit_order()
        COUNT = {k: n for n, k in enumerate(sorted(UNITS))}

        @block.sync
        def _(sp):
            sp.dma_start(words[0][:, :], a["masks"][0]).then_inc(ld_msk[0], 16)
            with sp.Fori(0, NB) as b:
                sp.wait_ge(s_done, b * IT)
                sp.dma_start(dtv[:, :, :], dt_d[ds(b, 1)].rearrange("o k p l -> p (o k) l")).then_inc(ld_dt, 16)
                sp.dma_start(dtu[:, :, :], dtu_d[ds(b, 1)].rearrange("o k p l -> p (o k) l")).then_inc(ld_dt, 16)
                for j in range(8):
                    if j >= 2:
                        sp.wait_ge(prod_done, b * IT + 8 * (j - 1))
                    else:
                        sp.wait_ge(prod_done, b * IT)
                    for m, t in ((0, Bb), (NS, Cb)):
                        src = bc_d[ds(b, 1), m + 2 * j:m + 2 * j + 2, :].rearrange("o n l -> o (n l)").broadcast_to([P, 2 * L])
                        sp.dma_start(t[j % 2][:, :, :].rearrange("p n l -> p (n l)"), src).then_inc(ld_bc[j % 2], 16)
                    if j == 0:
                        sp.wait_ge(stored, b * 16)
                        sp.dma_start(yac[:, :, :], du_d[ds(b, 1)].rearrange("o k p l -> p (o k) l")).then_inc(ld_yac, 16)
                        sp.wait_ge(w_done, b * 2 * NU + NU)
                        sp.dma_start(words[1][:, :], a["masks"][ds(b * 2 + 1, 1)].rearrange("o p n -> (o p) n")).then_inc(ld_msk[1], 16)
                    if j == 4:
                        sp.dma_start(words[0][:, :], a["masks"][ds(b * 2 + 2, 1)].rearrange("o p n -> (o p) n")).then_inc(ld_msk[0], 16)
                sp.wait_ge(yac_done, b * IT + IT)
                sp.dma_start(y_d[ds(b, 1)].rearrange("o k p l -> p (o k) l"), yac[:, :, :]).then_inc(stored, 16)
            sp.wait_ge(stored, NB * 16)

        def pe_unit(pe, unit, buf, b, done):
            pe.wait_ge(w_done, done)
            col = b * L + buf * GW if buf else b * L
            for ab, ps in enumerate((WA, WB)):
                if unit < 4:
                    for c in range(2):
                        cc = 2 * (unit % 2) + c
                        mm = pe.matmul(ps[:, c * GW:(c + 1) * GW], powers[:, cc, ab, :], Rt[unit // 2][:, ds(col, GW)], start=True, stop=True)
                else:
                    mm = pe.matmul(ps[:, :], powers[:, 2 * buf + unit - 4, ab, :], Rt[2][:, ds(b, D, 4)], start=True, stop=True)
            mm.then_inc(w_ps, 1)

        def act_unit(act, unit, buf, n):
            act.wait_ge(w_ps, n + 1)
            act.activation(w_unit(unit, buf), WA[:, :], ACT.Copy).then_inc(w_first, 1)

        def dve_unit(v, unit, buf, n, masks):
            v.wait_ge(ld_msk[buf], masks)
            v.wait_ge(w_first, n + 1)
            v.sem_inc(passed)
            m = msk[buf][:, (unit % 2) * 2 * GW:(unit % 2 + 1) * 2 * GW] if unit < 4 else msk[buf][:, 4 * GW + (unit - 4) * D:4 * GW + (unit - 3) * D]
            v.copy_predicated(w_unit(unit, buf), m, WB[:, :]).then_inc(w_done, 1)

        @block.tensor
        def _(pe):
            for unit in range(NU):
                pe_unit(pe, unit, 0, 0, unit)
            with pe.Fori(0, NB) as b:
                def w_slot(j, pos):
                    if (j, pos) in UNITS:
                        buf, unit = UNITS[(j, pos)]
                        n = NU + COUNT[(j, pos)]
                        pe_unit(pe, unit, buf, b if buf else b + 1, b * 2 * NU + n)

                def gate_up(j, ch):
                    q = 2 * j + ch
                    w, tb = j // 4, j % 4
                    pe.wait_ge(inter_done, b * 16 + max(q - 1, 0))
                    for ps, W, done in ((G[ch], Wg[w], g_ps), (U[ch], Wu[w], u_ps)):
                        for k in range(KC):
                            mm = pe.matmul(ps[:, :], W[:, k, ch * P:(ch + 1) * P], hT[:, k, tb * L:(tb + 1) * L], start=k == 0, stop=k == KC - 1)
                        mm.then_inc(done, 1)

                def down(j):
                    w = j // 4
                    pe.wait_ge(inter_done, b * 16 + 2 * j + 2)
                    for t in range(LT):
                        n = 4 * j + t
                        pe.wait_ge(add_done, b * 32 + max(n - 1, 0))
                        for ch in range(2):
                            mm = pe.matmul(Yb[t % 2][:, :], inter[j % 2][:, ch, t * P:(t + 1) * P], Wd[w][:, ch, :], start=ch == 0, stop=ch == 1)
                        mm.then_inc(y_ps, 1)

                for j in range(8):
                    if j % 4 == 0:
                        pe.wait_ge(w_done, b * 2 * NU + NU * (1 + j // 4))
                    w_slot(j, 0)
                    gate_up(j, 0)
                    w_slot(j, 1)
                    if j:
                        down(j - 1)
                    gate_up(j, 1)
                down(7)

        @block.scalar
        def _(act):
            for unit in range(NU):
                act_unit(act, unit, 0, unit)
            with act.Fori(0, NB) as b:
                def silu(j, ch):
                    q = 2 * j + ch
                    act.wait_ge(g_ps, b * 16 + q + 1)
                    act.wait_ge(inter_done, b * 16 + max(q - 1, 0))
                    act.activation(sil[ch][:, :], G[ch][:, :], ACT.Silu).then_inc(sil_done, 1)

                def decay(j, i):
                    n = 8 * j + i
                    act.wait_ge(s_done, b * IT + max(n - NR + 1, 0))
                    act.activation(dA[:, n % NR, :], dtv[:, i % 4, :], ACT.Exp, scale=negA[:, i % 4, 2 * j + i // 4:2 * j + i // 4 + 1]).then_inc(dA_done, 1)

                act.wait_ge(ld_dt, b * 32 + 32)
                for j in range(8):
                    for pos in range(2):
                        if (j, pos) in UNITS:
                            buf, unit = UNITS[(j, pos)]
                            act_unit(act, unit, buf, b * 2 * NU + NU + COUNT[(j, pos)])
                        for i in range(4 * pos, 4 * pos + 4):
                            decay(j, i)
                        silu(j, pos)

        @block.vector
        def _(v):
            for unit in range(NU):
                dve_unit(v, unit, 0, unit, 16)
            with v.Fori(0, NB) as b:
                def mult(j, ch):
                    q = 2 * j + ch
                    v.wait_ge(sil_done, b * 16 + q + 1)
                    v.wait_ge(u_ps, b * 16 + q + 1)
                    if j >= 2:
                        v.wait_ge(y_ps, b * 32 + 4 * (j - 1))
                    else:
                        v.wait_ge(y_ps, b * 32)
                    v.tensor_tensor(inter[j % 2][:, ch, :], U[ch][:, :], sil[ch][:, :], ALU.mult).then_inc(inter_done, 1)

                def add(j, t):
                    v.wait_ge(y_ps, b * 32 + 4 * j + t + 1)
                    x = X[:, (j % 4) * LT + t, :]
                    v.tensor_tensor(x, Yb[t % 2][:, :], x, ALU.add).then_inc(add_done, 1)

                def drive(j, i):
                    n = 8 * j + i
                    if i == 0:
                        v.wait_ge(ld_bc[j % 2], b * 128 + 32 * (j // 2 + 1))
                    v.wait_ge(s_done, b * IT + max(n - NR + 1, 0))
                    v.tensor_tensor(dBu[:, n % NR, :], dtu[:, i % 4, :], Bb[j % 2][:, i // 4, :], ALU.mult).then_inc(dBu_done, 1)

                def scan(n):
                    v.wait_ge(dBu_done, b * IT + n + 1)
                    v.wait_ge(dA_done, b * IT + n + 1)
                    v.wait_ge(prod_done, b * IT + max(n - NR + 1, 0))
                    v.tensor_tensor_scan(S[:, n % NR, :], dA[:, n % NR, :], dBu[:, n % NR, :], 0.0, ALU.mult, ALU.add).then_inc(s_done, 1)

                v.wait_ge(ld_dt, b * 32 + 32)
                for j in range(8):
                    for i in range(8):
                        drive(j, i)
                        if 8 * j + i >= 1:
                            scan(8 * j + i - 1)
                        if i == 0 and j:
                            mult(j - 1, 1)
                        if i == 3:
                            mult(j, 0)
                        if i >= 4 and j:
                            add(j - 1, i - 4)
                        if i in (0, 4) and (j, i // 4) in UNITS:
                            buf, unit = UNITS[(j, i // 4)]
                            dve_unit(v, unit, buf, b * 2 * NU + NU + COUNT[(j, i // 4)], b * 16 + (16 if buf else 32))
                scan(IT - 1)
                mult(7, 1)
                for t in range(LT):
                    add(7, t)

        @block.gpsimd
        def _(g):
            with g.Fori(0, NB) as b:
                def weigh(n):
                    j, i = n // 8, n % 8
                    if i == 0:
                        g.wait_ge(ld_bc[j % 2], b * 128 + 32 * (j // 2 + 1))
                    g.wait_ge(s_done, b * IT + n + 1)
                    g.wait_ge(yac_done, b * IT + max(n - NQ + 1, 0))
                    g.tensor_tensor(prod[:, n % NQ, :], S[:, n % NR, :], Cb[j % 2][:, i // 4, :], ALU.mult).then_inc(prod_done, 1)

                def gather(n):
                    g.wait_ge(prod_done, b * IT + n + 1)
                    g.wait_ge(yac_done, b * IT + max(n - 3, 0))
                    g.tensor_tensor(yac[:, n % 4, :], yac[:, n % 4, :], prod[:, n % NQ, :], ALU.add).then_inc(yac_done, 1)

                for n in range(IT):
                    weigh(n)
                    if n == 1:
                        g.wait_ge(ld_yac, b * 16 + 16)
                    if n:
                        gather(n - 1)
                gather(IT - 1)


def block_c(nc, a, X, ident, bank, meta, y_d, rows_d):
    with ExitStack() as s:
        sb, sem = mem(nc, s, "C")
        st, mv, rstd = sb("st", [P, NT, 6]), sb("mv", [P, NT, 2]), sb("rstd", [P, NT])
        st2, mv2, rstd2 = sb("st2", [P, LT, 6]), sb("mv2", [P, LT, 2]), sb("rstd2", [P, LT])
        y = [sb(f"y{i}", [P, LT, L]) for i in range(2)]
        z, yg = sb("z", [P, LT, D]), sb("yg", [P, LT, L])
        gk, hT = sb("gk", [P, KC, NE]), sb("hT", [P, LT, D])
        row = [sb(f"row{i}", [P, LT, ROW]) for i in range(2)]
        tok = sb("tok", [P, NT], I32)
        before, ones = sb("before", [P, P]), sb("ones", [P, P])
        lg, ex, pr, rest, chosen, place = (sb(n, [P, LT, NE]) for n in ("logit", "expo", "prob", "rest", "chosen", "place"))
        mx, sm, inv, tsum, tinv = (sb(n, [P, LT]) for n in ("mx", "sm", "inv", "tsum", "tinv"))
        top, top_place = sb("top", [P, LT, TOPK]), sb("top_place", [P, LT, TOPK])
        where = [sb(f"where{i}", [P, LT, TOPK], I32) for i in range(2)]
        fill = sb("fill", [P, NE])
        pad = sb("pad", [P, ROW])
        incl, neg_base, tau, tau0 = sb("incl", [NE, NE]), sb("neg_base", [NE, 1]), sb("tau", [NE, NMETA]), sb("tau0", [1, NMETA])
        need_i, need_s, need, ends = sb("need_i", [NE, 1], I32), sb("need_s", [NE, 1], I32), sb("need", [NE, 1]), sb("ends", [NE, 1])
        past = sb("past", [NE, NMETA])
        ev, sc, dd, f0, f1 = (sb(n, [1, NMETA]) for n in ("ev", "sc", "dd", "f0", "f1"))
        i0, i1 = sb("i0", [1, NMETA], I32), sb("i1", [1, NMETA], I32)
        padrow = sb("padrow", [1, NE], I32)

        stats, root, ln_step, ln_var, ln_rooted = sem("stats"), sem("root"), sem("ln_step"), sem("ln_var"), sem("ln_rooted")
        ld_y, ld_c = [sem(f"ld_y{i}") for i in range(2)], sem("ld_c")
        z_in, z_done, g_done, yT_ps, x2_done, h_in, h_ps, h_sb, lg_ps = (sem(n) for n in ("z_in", "z_done", "g_done", "yT_ps", "x2_done", "h_in", "h_ps", "h_sb", "lg_ps"))
        passed = sem("passed")
        r_step, r_in, r_exp, chosen_done, rank_ps, where_done, scattered, fill_done = (
            sem(n) for n in ("r_step", "r_in", "r_exp", "chosen_done", "rank_ps", "where_done", "scattered", "fill_done"))
        fT_ps, need_done, ends_ps, past_done, meta_ps, m_step, padrow_done, stored = (
            sem(n) for n in ("fT_ps", "need_done", "ends_ps", "past_done", "meta_ps", "m_step", "padrow_done", "stored"))
        block = s.enter_context(nc.Block())
        RS = 15
        out = a["out"]
        consts = ((gk[:, :, :], "gk"), (tok[:, :], "tok"), (before[:, :], "before"), (ones[:, :], "ones"), (fill[:, :], "fill"),
                  (pad[:, 0:ROW - 1], "pad"), (pad[:, ROW - 1:ROW].bitcast(I32), "pad_tok"), (incl[:, :], "incl"),
                  (neg_base[:, :], "neg_base"), (tau[:, :], "tau"), (tau0[:, :], "tau0"))

        @block.sync
        def _(sp):
            for b in range(2):
                sp.dma_start(y[b][:, :, :], y_d[b].rearrange("k p l -> p k l")).then_inc(ld_y[b], 16)
            for dst, name in consts:
                sp.dma_start(dst, a[name]).then_inc(ld_c, 16)
            sp.wait_ge(ld_c, 16 * len(consts))
            sp.dma_start(rows_d[NE * REGION:NE * REGION + P, :], pad[:, :]).then_inc(stored, 16)
            sp.dma_start(out[NT * P:NT * P + P, :], pad[:, 0:D]).then_inc(stored, 16)
            for b in range(NB):
                if b + 2 < NB:
                    sp.wait_ge(g_done, b + 1)
                    sp.dma_start(y[b % 2][:, :, :], y_d[b + 2].rearrange("k p l -> p k l")).then_inc(ld_y[b % 2], 16)
                sp.wait_ge(x2_done, 4 * b + 4)
                sp.dma_start(out[b * L:(b + 1) * L, :].rearrange("(t p) n -> p t n", p=P), X[:, b * LT:(b + 1) * LT, :]).then_inc(stored, 16)
            sp.wait_ge(padrow_done, 1)
            for e in range(NE):
                first = sp.value_load(padrow[0:1, e:e + 1], min_val=e * REGION, max_val=(e + 1) * REGION - P)
                sp.dma_start(rows_d[ds(first, P), :], pad[:, :]).then_inc(stored, 16)
            sp.wait_ge(stored, 16 * (2 + NB + NE))

        @block.gpsimd
        def _(g):
            with g.Fori(0, NB // 2) as pair:
                for h in range(2):
                    g.wait_ge(where_done, pair * 2 + h + 1)
                    g.sem_inc(passed)
                    for t in range(LT):
                        for k in range(TOPK):
                            g.indirect_dma_start(rows_d[:, :], bass.IndirectOffsetOnAxis(ap=where[h][:, t, k:k + 1].bitcast(U32), axis=0),
                                                 row[h][:, t, :], None).then_inc(scattered, 16)
                    g.wait_ge(scattered, (pair * 2 + h + 1) * 16 * LT * TOPK)

        @block.vector
        def _(v):
            ln_statistics(v, X, st, mv, rstd, stats, root, 0)
            v.wait_ge(ld_c, 16 * len(consts))

            def one(t):
                return t[:, :].rearrange("p (t o) -> p t o", o=1).broadcast_to([P, LT, NE])

            def batch(base, h):
                def step(i, n):
                    i.then_inc(r_step, 1)
                    v.wait_ge(r_step, base * RS + n)
                    if n in (4, 5, 13):
                        v.sem_inc(passed)
                for t in range(LT):
                    i = ln_tile(v, X, base * LT + t, mv, rstd, z[:, t, :])
                i.then_inc(z_in, 1)
                v.wait_ge(z_done, base + 1)
                v.wait_ge(ld_y[h], pair * 16 + 16)
                v.tensor_tensor(yg[:, :, :], y[h][:, :, :], z[:, :, :], ALU.mult).then_inc(g_done, 1)
                for t in range(LT):
                    v.wait_ge(yT_ps, base * 4 + t + 1)
                    x = X[:, ds(base * LT + t, 1), :].rearrange("p o n -> p (o n)")
                    v.tensor_tensor(x, bank[t][:, :], x, ALU.add).then_inc(x2_done, 1)
                v.wait_ge(x2_done, base * 4 + 4)
                v.sem_inc(passed)
                for t in range(LT):
                    i = v.bn_stats(st2[:, t, :], X[:, ds(base * LT + t, 1), :])
                i.then_inc(ln_step, 1)
                v.wait_ge(ln_step, base * 3 + 1)
                v.sem_inc(passed)
                for t in range(LT):
                    i = v.bn_aggr(mv2[:, t, :], st2[:, t, :])
                i.then_inc(ln_step, 1)
                v.wait_ge(ln_step, base * 3 + 2)
                v.tensor_scalar(rstd2[:, :], mv2[:, :, 1], EPS, None, ALU.add).then_inc(ln_var, 1)
                v.wait_ge(ln_rooted, base + 1)
                v.reciprocal(rstd2[:, :], rstd2[:, :]).then_inc(ln_step, 1)
                v.wait_ge(ln_step, base * 3 + 3)
                v.wait_ge(scattered, pair * ((1 + h) * 16 * LT * TOPK))
                for t in range(LT):
                    v.tensor_scalar(row[h][:, t, 0:D], X[:, ds(base * LT + t, 1), :].rearrange("p o n -> p (o n)"), mv2[:, t, 0:1],
                                    rstd2[:, t:t + 1], ALU.subtract, ALU.mult).then_inc(h_in, 1)
                v.tensor_copy(row[h][:, :, ROW - 1:ROW].bitcast(I32), tok[:, ds(base * LT, LT)].rearrange("p (t o) -> p t o", o=1))
                v.wait_ge(lg_ps, base + 1)
                logits = bank[0][:, 0:LT * NE].rearrange("p (t e) -> p t e", t=LT)
                step(v.tensor_reduce(mx[:, :], logits, AX, ALU.max), 1)
                v.tensor_tensor(lg[:, :, :], logits, one(mx), ALU.subtract).then_inc(r_in, 1)
                v.wait_ge(r_exp, base + 1)
                step(v.tensor_reduce(sm[:, :], ex[:, :, :], AX, ALU.add), 2)
                step(v.reciprocal(inv[:, :], sm[:, :]), 3)
                step(v.tensor_tensor(pr[:, :, :], ex[:, :, :], one(inv), ALU.mult), 4)
                for t in range(LT):
                    i = v.max(top[:, t, :], pr[:, t, :])
                step(i, 5)
                for t in range(LT):
                    i = v.match_replace(rest[:, t, :], top[:, t, :], pr[:, t, :], -1.0)
                step(i, 6)
                step(v.tensor_scalar(chosen[:, :, :], rest[:, :, :], 0.0, None, ALU.is_lt), 7)
                v.sem_inc(chosen_done)
                step(v.tensor_tensor(rest[:, :, :], chosen[:, :, :], pr[:, :, :], ALU.mult), 8)
                step(v.tensor_reduce(tsum[:, :], rest[:, :, :], AX, ALU.add), 9)
                step(v.reciprocal(tinv[:, :], tsum[:, :]), 10)
                step(v.tensor_tensor(row[h][:, :, D:D + NE], rest[:, :, :], one(tinv), ALU.mult), 11)
                v.wait_ge(rank_ps, base + 1)
                ranks = bank[1][:, 0:LT * NE].rearrange("p (t e) -> p t e", t=LT)
                step(v.tensor_tensor(place[:, :, :], ranks, fill[:, :].rearrange("p (o e) -> p o e", o=1).broadcast_to([P, LT, NE]), ALU.add), 12)
                step(v.tensor_tensor(place[:, :, :], place[:, :, :], chosen[:, :, :], ALU.mult), 13)
                for t in range(LT):
                    i = v.max(top_place[:, t, :], place[:, t, :])
                step(i, 14)
                v.tensor_scalar(where[h][:, :, :], top_place[:, :, :], -1.0, None, ALU.add).then_inc(where_done, 1)
                step(v.tensor_tensor(fill[:, :], bank[2][:, 0:NE], fill[:, :], ALU.add), 15)
                v.sem_inc(fill_done)

            with v.Fori(0, NB // 2) as pair:
                for h in range(2):
                    batch(pair * 2 + h, h)
            v.tensor_scalar(padrow[:, :], fill[0:1, :], -1.0, None, ALU.add).then_inc(padrow_done, 1)
            v.wait_ge(fT_ps, 1)
            n = [0]

            def step(i):
                n[0] += 1
                i.then_inc(m_step, 1)
                v.wait_ge(m_step, n[0])
            step(v.tensor_scalar(need_i[:, :], bank[3][0:NE, 0:1], neg_base[:, 0:1], P - 1.0, ALU.add, ALU.add))
            step(v.tensor_scalar(need_s[:, :], need_i[:, :], 7, None, ALU.logical_shift_right))
            v.tensor_scalar(need[:, :], need_s[:, :], 1.0, None, ALU.max).then_inc(need_done, 1)
            v.wait_ge(ends_ps, 1)
            step(v.tensor_copy(ends[:, :], bank[4][0:NE, 0:1]))
            v.tensor_scalar(past[:, :], tau[:, :], ends[:, 0:1], None, ALU.is_ge).then_inc(past_done, 1)
            v.wait_ge(meta_ps, 1)
            step(v.tensor_copy(ev[:, :], bank[5][0:1, 0:NMETA]))
            step(v.tensor_copy(sc[:, :], bank[6][0:1, 0:NMETA]))
            step(v.tensor_tensor(dd[:, :], tau0[:, :], sc[:, :], ALU.subtract))
            step(v.tensor_scalar(f0[:, :], dd[:, :], float(P), None, ALU.mult))
            step(v.scalar_tensor_tensor(out=f1[:, :], in0=ev[:, :], scalar=float(REGION), in1=f0[:, :], op0=ALU.mult, op1=ALU.add))
            step(v.tensor_scalar(meta[:, BASE, :], f1[:, :], float(NE * REGION), None, ALU.min))
            step(v.tensor_scalar(meta[:, EXPERT, :], ev[:, :], float(NE - 1), None, ALU.min))
            step(v.tensor_scalar(meta[:, GO, :], ev[:, :], float(NE), None, ALU.is_lt))
            step(v.tensor_scalar(f0[:, :], dd[:, :], 0.0, None, ALU.is_equal))
            step(v.scalar_tensor_tensor(out=meta[:, FIRST, :], in0=ev[:, :], scalar=float(NE), in1=f0[:, :], op0=ALU.is_ge, op1=ALU.max))
            for f, ahead in ((LOADS, LOAD_AHEAD), (SPLITS, SPLIT_AHEAD)):
                step(v.scalar_tensor_tensor(out=meta[:, f, :], in0=ev[:, :], scalar=float(NE - 1 - ahead), in1=f0[:, :], op0=ALU.is_le, op1=ALU.mult))
            for f, ahead, size in ((SLOT, 0, NSLOT), (LOAD_RAW, LOAD_AHEAD, NRAW), (SPLIT_RAW, SPLIT_AHEAD, NRAW), (SPLIT_SLOT, SPLIT_AHEAD, NSLOT)):
                step(v.tensor_scalar(i0[:, :], ev[:, :], float(ahead), None, ALU.add))
                step(v.tensor_scalar(meta[:, f, :], i0[:, :], size - 1, None, ALU.bitwise_and))
            step(v.tensor_scalar(i0[:, :], sc[:, :], UNROLL - 1.0, None, ALU.add))
            step(v.tensor_scalar(i1[:, :], i0[:, :], 3, 4, ALU.logical_shift_right, ALU.logical_shift_left))
            step(v.tensor_scalar(meta[:, RLOADS, :], i1[:, :], 16.0, None, ALU.add))

        @block.scalar
        def _(act):
            ln_root(act, rstd, stats, root, 0)
            with act.Fori(0, NB) as b:
                act.wait_ge(z_in, b + 1)
                act.activation(z[:, :, :], z[:, :, :], ACT.Silu).then_inc(z_done, 1)
                act.wait_ge(ln_var, b + 1)
                act.activation(rstd2[:, :], rstd2[:, :], ACT.Sqrt).then_inc(ln_rooted, 1)
                for t in range(LT):
                    act.wait_ge(h_ps, b * 4 + t + 1)
                    act.activation(hT[:, t, :], bank[4 + t][:, :], ACT.Copy).then_inc(h_sb, 1)
                act.wait_ge(r_in, b + 1)
                act.activation(ex[:, :, :], lg[:, :, :], ACT.Exp).then_inc(r_exp, 1)

        @block.tensor
        def _(pe):
            pe.wait_ge(ld_c, 16 * len(consts))
            with pe.Fori(0, NB // 2) as pair:
                for h in range(2):
                    b = pair * 2 + h
                    pe.wait_ge(g_done, b + 1)
                    for t in range(LT):
                        for k in range(KC):
                            mm = pe.transpose(bank[t][:, k * P:(k + 1) * P], yg[:, k, t * P:(t + 1) * P], ident[:, :])
                        mm.then_inc(yT_ps, 1)
                    for t in range(LT):
                        pe.wait_ge(h_in, b * 4 + t + 1)
                        for k in range(KC):
                            mm = pe.transpose(bank[4 + t][:, k * P:(k + 1) * P], row[h][:, t, k * P:(k + 1) * P], ident[:, :])
                        mm.then_inc(h_ps, 1)
                    for t in range(LT):
                        pe.wait_ge(h_sb, b * 4 + t + 1)
                        for k in range(KC):
                            mm = pe.matmul(bank[0][:, t * NE:(t + 1) * NE], hT[:, t, k * P:(k + 1) * P], gk[:, k, :], start=k == 0, stop=k == KC - 1)
                    mm.then_inc(lg_ps, 1)
                    pe.wait_ge(chosen_done, b + 1)
                    for t in range(LT):
                        for q in range(t):
                            pe.matmul(bank[1][:, t * NE:(t + 1) * NE], ones[:, :], chosen[:, q, :], start=q == 0, stop=False)
                        pe.matmul(bank[1][:, t * NE:(t + 1) * NE], before[:, :], chosen[:, t, :], start=t == 0, stop=True)
                    for t in range(LT):
                        mm = pe.matmul(bank[2][:, 0:NE], ones[:, :], chosen[:, t, :], start=t == 0, stop=t == LT - 1)
                    mm.then_inc(rank_ps, 1)
                    pe.wait_ge(fill_done, b + 1)
            pe.transpose(bank[3][0:NE, 0:P], fill[:, :], ident[:, :]).then_inc(fT_ps, 1)
            pe.wait_ge(need_done, 1)
            pe.matmul(bank[4][0:NE, 0:1], incl[:, :], need[:, :], start=True, stop=True).then_inc(ends_ps, 1)
            pe.wait_ge(past_done, 1)
            pe.matmul(bank[5][0:1, 0:NMETA], ones[0:NE, 0:1], past[:, :], start=True, stop=True)
            pe.matmul(bank[6][0:1, 0:NMETA], need[:, :], past[:, :], start=True, stop=True).then_inc(meta_ps, 1)


def block_d(nc, a, ident, bank, meta, rows_d):
    with ExitStack() as s:
        sb, sem = mem(nc, s, "D")
        GUW, MH = 2 * M, M // 2
        raw_gu, raw_d = sb("raw_gu", [P, NRAW, KC * GUW]), sb("raw_d", [MH, NRAW, 2 * D])
        gu_hi, gu_lo = (sb(f"gu_{h}", [P, NSLOT, KC * GUW], F32R) for h in ("hi", "lo"))
        d_hi, d_lo = (sb(f"d_{h}", [MH, NSLOT, 2 * D], F32R) for h in ("hi", "lo"))
        rows = [sb(f"rows{i}", [P, ROW]) for i in range(UNROLL)]
        xT_hi, xT_lo = ([sb(f"xT_{h}{i}", [P, KC * P], F32R) for i in range(2)] for h in ("hi", "lo"))
        sil, inner = [sb(f"sil{i}", [P, M]) for i in range(2)], [sb(f"inner{i}", [P, M]) for i in range(2)]
        iT_hi, iT_lo = ([sb(f"iT_{h}{i}", [MH, 2 * P], F32R) for i in range(2)] for h in ("hi", "lo"))
        ysb = [sb(f"y{i}", [P, D]) for i in range(UNROLL)]
        first_counts = sb("first_counts", [1, 4])
        pT, piT, pgu, py = bank[0], bank[1], [bank[2], bank[3]], [bank[4], bank[5]]
        ld_rows, ld_w = [sem(f"ld_rows{i}") for i in range(UNROLL)], sem("ld_w")
        added = [sem(f"added{i}") for i in range(4)]
        passed = sem("passed")
        w_hi, w_split = sem("w_hi"), sem("w_split")
        xT_ps, xT_first, xT_sb, gu_ps, sil_done, inner_done, iT_ps, iT_first, iT_sb, y_ps, y_sb = (
            sem(n) for n in ("xT_ps", "xT_first", "xT_sb", "gu_ps", "sil_done", "inner_done", "iT_ps", "iT_first", "iT_sb", "y_ps", "y_sb"))
        block = s.enter_context(nc.Block())

        def field(eng, f, tile, hi):
            return eng.value_load(meta[0:1, f, ds(tile, 1)], min_val=0, max_val=hi)

        def slot(t, i):
            return t[:, ds(i, 1), :].rearrange("p o n -> p (o n)")

        @block.sync
        def _(sp):
            def load_w(e, i):
                sp.dma_start(slot(raw_gu, i), a["wgu"][ds(e, 1)].rearrange("o p n -> p (o n)")).then_inc(ld_w, 16)
                sp.dma_start(slot(raw_d, i), a["wd"][ds(e, 1)].rearrange("o p n -> p (o n)")).then_inc(ld_w, 16)

            load_w(0, 0)
            for i in range(UNROLL):
                first = field(sp, BASE, i, NE * REGION)
                sp.dma_start(rows[i][:, :], rows_d[ds(first, P), :]).then_inc(ld_rows[i], 16)
            sp.wait_ge(ld_w, 32)
            load_w(1, 1)
            sp.wait_ge(ld_w, 64)
            sp.wait_ge(w_split, 1)
            load_w(2, 0)
            with sp.Fori(0, NTILE // UNROLL) as q:
                with sp.If(field(sp, GO, q * UNROLL, 1) > 0):
                    for i in range(UNROLL):
                        t = q * UNROLL + i
                        with sp.If(field(sp, LOADS, t, 1) > 0):
                            e, buf = field(sp, EXPERT, t, NE - 1 - LOAD_AHEAD), field(sp, LOAD_RAW, t, NRAW - 1)
                            sp.wait_ge(ld_w, (e + LOAD_AHEAD) * 32)
                            sp.sem_inc(passed)
                            sp.wait_ge(w_split, e + (LOAD_AHEAD - NRAW + 1))
                            sp.sem_inc(passed)
                            load_w(e + LOAD_AHEAD, buf)
                        first = field(sp, BASE, t + UNROLL, NE * REGION)
                        sp.wait_ge(added[i % 4], 32 * q + 16 * (i // 4 + 2))
                        sp.sem_inc(passed)
                        sp.dma_start(rows[i][:, :], rows_d[ds(first, P), :]).then_inc(ld_rows[i], 16)
            count = field(sp, RLOADS, NMETA - 1, 16 * (NTILE // UNROLL + 1))
            for i in range(UNROLL):
                sp.wait_ge(ld_rows[i], count)
                sp.sem_inc(passed)
            sp.wait_ge(ld_w, 32 * NE)

        @block.tensor
        def _(pe):
            def turn_rows(i):
                for k in range(KC):
                    mm = pe.transpose(pT[:, k * P:(k + 1) * P], rows[i][:, k * P:(k + 1) * P], ident[:, :])
                mm.then_inc(xT_ps, 1)

            def split_products(ps, hi, lo, whi, wlo, n, last):
                pe.matmul(ps, hi, whi, start=n == 0, stop=False)
                pe.matmul(ps, hi, wlo, start=False, stop=False)
                return pe.matmul(ps, lo, whi, start=False, stop=last)

            def gate_up(buf, i):
                for k in range(KC):
                    x, w = slice(k * P, (k + 1) * P), slice(k * GUW, (k + 1) * GUW)
                    whi, wlo = (t[:, ds(buf, 1), w].rearrange("p o n -> p (o n)") for t in (gu_hi, gu_lo))
                    mm = split_products(pgu[i % 2][:, 0:GUW], xT_hi[i % 2][:, x], xT_lo[i % 2][:, x], whi, wlo, k, k == KC - 1)
                mm.then_inc(gu_ps, 1)

            pe.wait_ge(ld_rows[0], 16)
            turn_rows(0)
            buf = field(pe, SLOT, 0, NSLOT - 1)
            pe.wait_ge(w_split, 1)
            pe.wait_ge(xT_sb, 1)
            gate_up(buf, 0)
            pe.wait_ge(ld_rows[1], 16)
            turn_rows(1)
            with pe.Fori(0, NTILE // UNROLL) as q:
                with pe.If(field(pe, GO, q * UNROLL, 1) > 0):
                    for i in range(UNROLL):
                        t = q * UNROLL + i
                        buf, next_buf = field(pe, SLOT, t, NSLOT - 1), field(pe, SLOT, t + 1, NSLOT - 1)
                        next_expert = field(pe, EXPERT, t + 1, NE - 1)
                        pe.wait_ge(inner_done, t + 1)
                        for c in range(2):
                            mm = pe.transpose(piT[0:MH, c * P:(c + 1) * P], inner[i % 2][:, c * MH:(c + 1) * MH], ident[:, :])
                        mm.then_inc(iT_ps, 1)
                        pe.wait_ge(xT_sb, t + 2)
                        pe.wait_ge(w_split, next_expert + 1)
                        gate_up(next_buf, i + 1)
                        j = (i + 2) % UNROLL
                        pe.wait_ge(ld_rows[j], q * 16 + (16 if i + 2 < UNROLL else 32))
                        turn_rows(j)
                        pe.wait_ge(iT_sb, t + 1)
                        for c in range(2):
                            x, w = slice(c * P, (c + 1) * P), slice(c * D, (c + 1) * D)
                            whi, wlo = (m[:, ds(buf, 1), w].rearrange("p o n -> p (o n)") for m in (d_hi, d_lo))
                            mm = split_products(py[i % 2][:, :], iT_hi[i % 2][:, x], iT_lo[i % 2][:, x], whi, wlo, c, c == 1)
                        mm.then_inc(y_ps, 1)

        @block.scalar
        def _(act):
            def turn(n, i):
                act.wait_ge(xT_ps, n + 1)
                act.activation(xT_hi[i % 2][:, :], pT[:, :], ACT.Copy).then_inc(xT_first, 1)

            def silu(n, i):
                act.wait_ge(gu_ps, n + 1)
                act.activation(sil[i % 2][:, :], pgu[i % 2][:, 0:M], ACT.Silu).then_inc(sil_done, 1)

            def split_hi(raw, buf):
                act.activation(slot(gu_hi, buf), slot(raw_gu, raw), ACT.Copy)
                act.activation(slot(d_hi, buf), slot(raw_d, raw), ACT.Copy).then_inc(w_hi, 1)

            for e in range(SPLIT_AHEAD):
                act.wait_ge(ld_w, 32 * e + 32)
                split_hi(e, e)
                if e == 0:
                    turn(0, 0)
            silu(0, 0)
            turn(1, 1)
            with act.Fori(0, NTILE // UNROLL) as q:
                with act.If(field(act, GO, q * UNROLL, 1) > 0):
                    for i in range(UNROLL):
                        t = q * UNROLL + i
                        silu(t + 1, i + 1)
                        turn(t + 2, i + 2)
                        with act.If(field(act, SPLITS, t, 1) > 0):
                            e = field(act, EXPERT, t, NE - 1 - SPLIT_AHEAD)
                            raw, buf = field(act, SPLIT_RAW, t, NRAW - 1), field(act, SPLIT_SLOT, t, NSLOT - 1)
                            act.wait_ge(ld_w, (e + SPLIT_AHEAD + 1) * 32)
                            act.sem_inc(passed)
                            split_hi(raw, buf)

        @block.vector
        def _(v):
            def weigh(tile, i):
                col = field(v, EXPERT, tile, NE - 1)
                v.wait_ge(sil_done, tile + 1)
                v.scalar_tensor_tensor(out=inner[i % 2][:, :], in0=sil[i % 2][:, :], scalar=rows[i % UNROLL][:, ds(col + D, 1)],
                                       in1=pgu[i % 2][:, M:2 * M], op0=ALU.mult, op1=ALU.mult).then_inc(inner_done, 1)

            def turn_lo(tile, i):
                v.wait_ge(xT_first, tile + 1)
                v.tensor_tensor(xT_lo[i % 2][:, :], pT[:, :], xT_hi[i % 2][:, :], ALU.subtract).then_inc(xT_sb, 1)

            turn_lo(0, 0)
            weigh(0, 0)
            turn_lo(1, 1)
            with v.Fori(0, NTILE // UNROLL) as q:
                with v.If(field(v, GO, q * UNROLL, 1) > 0):
                    for i in range(UNROLL):
                        t = q * UNROLL + i
                        v.wait_ge(iT_ps, t + 1)
                        v.tensor_copy(iT_hi[i % 2][:, :], piT[0:MH, 0:2 * P]).then_inc(iT_first, 1)
                        v.wait_ge(iT_first, t + 1)
                        v.tensor_tensor(iT_lo[i % 2][:, :], piT[0:MH, 0:2 * P], iT_hi[i % 2][:, :], ALU.subtract).then_inc(iT_sb, 1)
                        weigh(t + 1, i + 1)
                        turn_lo(t + 2, i + 2)
                        v.wait_ge(y_ps, t + 1)
                        v.tensor_copy(ysb[i][:, :], py[i % 2][:, :]).then_inc(y_sb, 1)

        @block.gpsimd
        def _(g):
            def split_lo(raw, buf):
                g.tensor_tensor(slot(gu_lo, buf), slot(raw_gu, raw), slot(gu_hi, buf), ALU.subtract)
                g.tensor_tensor(slot(d_lo, buf), slot(raw_d, raw), slot(d_hi, buf), ALU.subtract).then_inc(w_split, 1)

            for e in range(SPLIT_AHEAD):
                g.wait_ge(w_hi, e + 1)
                split_lo(e, e)
            for j in range(4):
                g.dma_start(first_counts[0:1, j:j + 1], a["tau0"][0:1, j:j + 1]).then_inc(added[j], 16)
            with g.Fori(0, NTILE // UNROLL) as q:
                with g.If(field(g, GO, q * UNROLL, 1) > 0):
                    for i in range(UNROLL):
                        t = q * UNROLL + i
                        done = 32 * q + 16 * (i // 4 + 1)
                        with g.If(field(g, FIRST, t, 1) > 0):
                            for j in range(4):
                                g.wait_ge(added[j], done + (16 if j < i % 4 else 0))
                            g.sem_inc(passed)
                        g.wait_ge(added[i % 4], done)
                        g.wait_ge(y_sb, t + 1)
                        g.sem_inc(passed)
                        g.indirect_dma_start(a["out"], bass.IndirectOffsetOnAxis(ap=rows[i][:, ROW - 1:ROW].bitcast(U32), axis=0),
                                             ysb[i][:, :], None, compute_op=ALU.add).then_inc(added[i % 4], 16)
                        with g.If(field(g, SPLITS, t, 1) > 0):
                            e = field(g, EXPERT, t, NE - 1 - SPLIT_AHEAD)
                            raw, buf = field(g, SPLIT_RAW, t, NRAW - 1), field(g, SPLIT_SLOT, t, NSLOT - 1)
                            g.wait_ge(w_hi, e + (SPLIT_AHEAD + 1))
                            g.sem_inc(passed)
                            split_lo(raw, buf)


def kernel(**inputs):
    import concourse.bacc as bacc
    from concourse.bass_utils import run_bass_kernel_spmd as run

    x = {k: np.ascontiguousarray(v) for k, v in inputs.items()}
    table, taps, powers, masks = spline_constants()

    def chunked(w):
        return w.reshape(-1, P, w.shape[-1]).transpose(1, 0, 2)

    def windows(cp):
        return np.where(taps >= 0, cp[np.maximum(taps, 0)], np.float32(0)).reshape(KC * 2 * 4, IPAD)

    gu = np.concatenate([x["L1_ffn_gate_proj"], x["L1_ffn_up_proj"]], 2)
    gu = gu.reshape(NE, KC, P, 2 * M).transpose(0, 2, 1, 3).reshape(NE, P, KC * 2 * M)
    down = x["L1_ffn_down_proj"].reshape(NE, 2, M // 2, D).transpose(0, 2, 1, 3).reshape(NE, M // 2, 2 * D)
    tiles = np.arange(NMETA, dtype=np.float32)
    region = np.arange(NE, dtype=np.float32) * REGION + 1
    arrays = {
        "x": x["x"],
        "ctxT": x["ctx_1024"].transpose(0, 2, 1).reshape(NB, 2, P, L).transpose(0, 2, 1, 3),
        "wqT": chunked(x["L0_xattn_Wq"].T), "wkT": chunked(x["L0_xattn_Wk"].T),
        "bq": x["L0_xattn_bq"].reshape(P, 1), "bk": x["L0_xattn_bk"].reshape(P, 1),
        "inwT": chunked(x["L1_xattn_in_proj_w"].T),
        "convw": x["L1_xattn_conv_w"].reshape(KC, P, TAPS).transpose(1, 0, 2),
        "convb": x["L1_xattn_conv_b"].reshape(KC, P).T,
        "xpT": chunked(x["L1_xattn_x_proj_w"].T), "dpT": x["L1_xattn_dt_proj_w"].T,
        "dpb": x["L1_xattn_dt_proj_b"].reshape(KC, P).T, "Dp": x["L1_xattn_D"].reshape(KC, P).T,
        "alog": chunked(x["L1_xattn_A_log"]),
        "taps_gate": windows(x["L0_ffn_gate_cp"]), "taps_up": windows(x["L0_ffn_up_cp"]),
        "taps_down": windows(x["L0_ffn_down_cp"]),
        "gk": chunked(x["L1_ffn_gate_kernel"]),
        "wgu": gu, "wd": down,
        "tok": np.arange(NB * L, dtype=np.int32).reshape(NT, P).T,
        "before": np.triu(np.ones((P, P), np.float32), 1), "ones": np.ones((P, P), np.float32),
        "fill": np.tile(region, (P, 1)), "neg_base": -region[:, None], "incl": np.triu(np.ones((NE, NE), np.float32)),
        "pad": np.zeros((P, ROW - 1), np.float32), "pad_tok": NB * L + np.arange(P, dtype=np.int32)[:, None],
        "tau": np.tile(tiles, (NE, 1)), "tau0": tiles[None],
        "ident": np.eye(P, dtype=np.float32), "table": table, "powers": powers.reshape(P, KC, 2, P), "masks": masks.view(np.int32),
    }
    nc = bacc.Bacc("TRN2", target_bir_lowering=False, num_devices=1)
    a, sent = {}, {}
    for name, v in arrays.items():
        sent[f"in_{name}"] = np.ascontiguousarray(v)
        a[name] = nc.dram_tensor(f"in_{name}", v.shape, mybir.dt.from_np(v.dtype), kind="ExternalInput").ap()
    a["out"] = nc.dram_tensor("out_x", (NB * L + P, D), F32, kind="ExternalOutput").ap()
    build(nc, a)
    return run(nc, [sent], core_ids=[0]).results[0]["out_x"][:NB * L].reshape(NB, L, D)
```
